# Optimizing a Trainium2 kernel written in Bass

```python
import numpy as np
import jax
import jax.numpy as jnp

def _softmax(x, axis=-1):
    return jax.nn.softmax(x, axis=axis)

def _gelu(x):
    return jax.nn.gelu(x, approximate=True)

def _silu(x):
    return jax.nn.silu(x)

def _sigmoid(x):
    return jax.nn.sigmoid(x)

def _layernorm(x, axis=-1, eps=1e-05):
    m = jnp.mean(x, axis=axis, keepdims=True)
    v = jnp.var(x, axis=axis, keepdims=True)
    return (x - m) / jnp.sqrt(v + eps)

def _scatter_add(tgt, idx, src, axis=0):
    return tgt.at[idx].add(src)

def _segment_sum(src, seg, n):
    return jax.ops.segment_sum(src, seg, n)
kernel_name = 'mk_adaln_attn_ffn_d1_seqx_r4_c42ec9'

def setup_inputs(seed: int=0):
    np.random.seed(seed)
    _w = jnp.asarray

    def _rec_inputs():
        import jax
        import jax.numpy as jnp
        _rk = jax.random.key(seed)
        x = -7.109e-05 + 0.9999 * jax.random.normal(jax.random.fold_in(_rk, 1), (128, 64, 256), jnp.float32)
        _lenS = 64 - jax.random.randint(jax.random.fold_in(_rk, 7), (128,), 0, max(1, 64 // 4) + 1, jnp.int32)
        _lenS2 = 64 - jax.random.randint(jax.random.fold_in(_rk, 8), (128,), 0, max(1, 64 // 4) + 1, jnp.int32)
        cond_512 = 0.0061147 + 1.02565 * jax.random.normal(jax.random.fold_in(_rk, 11), (128, 128), jnp.float32)
        return (x, cond_512)
    x, cond_512 = _rec_inputs()

    def _L0_cond_setup():
        import jax, jax.numpy as jnp
        import numpy as np
        W_DIM = 128
        CLAMP = 256.0
        key = jax.random.key(seed)
        ks = jax.random.split(key, 6)
        B, L, C = (8, 2048, 256)
        return {'x': jax.random.normal(ks[0], (B, L, C), dtype=jnp.float32), 'w': jax.random.normal(ks[1], (B, W_DIM), dtype=jnp.float32), 'weight': jax.random.normal(ks[2], (C, C), dtype=jnp.float32), 'bias': jax.random.normal(ks[3], (C,), dtype=jnp.float32), 'affine_w': jax.random.normal(ks[4], (C, W_DIM), dtype=jnp.float32), 'affine_b': jnp.ones((C,), dtype=jnp.float32)}
    _L0_cond_all = _L0_cond_setup()
    _L0_cond_in = {k: v for k, v in _L0_cond_all.items() if k in ('weight', 'bias', 'affine_w', 'affine_b')}
    del _L0_cond_all

    def _L0_attn_setup():
        import jax, jax.numpy as jnp
        import numpy as np
        import math
        B, N, DIM, H, DH, NNULL = (2, 512, 256, 16, 64, 2)
        SCALE = 8.0
        LN_EPS = 1e-05

        def _alibi_slopes(heads):
            start = 2.0 ** (-2.0 ** (-(math.log2(heads) - 3)))
            return np.array([start * start ** i for i in range(heads)], dtype=np.float32)

        def _l2norm(t):
            n = jnp.sqrt(jnp.sum(t * t, axis=-1, keepdims=True))
            return t / jnp.maximum(n, 1e-12)
        key = jax.random.key(seed)
        ks = jax.random.split(key, 6)
        inner = H * DH
        return {'x': jax.random.normal(ks[0], (B, N, DIM), dtype=jnp.float32), 'norm_g': jnp.ones((DIM,), jnp.float32), 'norm_b': jnp.zeros((DIM,), jnp.float32), 'Wq': jax.random.normal(ks[1], (DIM, inner), jnp.float32) * 0.02, 'Wkv': jax.random.normal(ks[2], (DIM, 2 * inner), jnp.float32) * 0.02, 'q_scale': jnp.ones((DH,), jnp.float32), 'k_scale': jnp.ones((DH,), jnp.float32), 'null_kv': jax.random.normal(ks[3], (H, 2 * NNULL, DH), jnp.float32), 'Wout': jax.random.normal(ks[4], (inner, DIM), jnp.float32) * 0.02}
    _L0_attn_all = _L0_attn_setup()
    _L0_attn_in = {k: v for k, v in _L0_attn_all.items() if k in ('norm_g', 'norm_b', 'Wq', 'Wkv', 'q_scale', 'k_scale', 'null_kv', 'Wout')}
    del _L0_attn_all

    def _L0_cond2_setup():
        import jax, jax.numpy as jnp
        import numpy as np
        import math
        HEAD_NUM = 16
        EPS = 1e-08

        def modulated_linear(x, s, aff_w, aff_b, w, b):
            style = s @ aff_w.T + aff_b
            w_mod = w[None, :, :] * style[:, None, :]
            demod = jax.lax.rsqrt(jnp.sum(w_mod * w_mod, axis=2) + EPS)
            w_mod = w_mod * demod[:, :, None]
            return jnp.einsum('bni,boi->bno', x, w_mod) + b
        key = jax.random.key(seed)
        ks = jax.random.split(key, 6)
        B, N, F, S = (8, 256, 256, 128)
        return {'x': jax.random.normal(ks[0], (B, N, F), dtype=jnp.float32), 's': jax.random.normal(ks[1], (B, S), dtype=jnp.float32), 'k_aff_w': jax.random.normal(ks[2], (F, S), dtype=jnp.float32) * 0.02, 'k_aff_b': jnp.ones((F,), dtype=jnp.float32), 'k_w': jax.random.normal(ks[3], (F, F), dtype=jnp.float32) * 0.02, 'k_b': jnp.zeros((F,), dtype=jnp.float32), 'o_aff_w': jax.random.normal(ks[4], (F, S), dtype=jnp.float32) * 0.02, 'o_aff_b': jnp.ones((F,), dtype=jnp.float32), 'o_w': jax.random.normal(ks[5], (F, F), dtype=jnp.float32) * 0.02, 'o_b': jnp.zeros((F,), dtype=jnp.float32)}
    _L0_cond2_all = _L0_cond2_setup()
    _L0_cond2_in = {k: v for k, v in _L0_cond2_all.items() if k in ('k_aff_w', 'k_aff_b', 'k_w', 'k_b', 'o_aff_w', 'o_aff_b', 'o_w', 'o_b')}
    del _L0_cond2_all

    def _L0_ffn_setup():
        import jax, jax.numpy as jnp
        import numpy as np
        D_MODEL = 256
        NUM_TILES = 64
        TPC = 8
        NUM_CLUSTERS = NUM_TILES // TPC
        GRID = 16
        COMP_H = 64
        NUM_KNOTS = 8
        EPS_LN = 1e-05

        def _calibrate(scores, knots, temperature):
            K = knots.shape[0]
            normalized = jax.nn.sigmoid(scores / (temperature[0] + 1e-06))
            idx_float = normalized * (K - 1)
            idx_low = jnp.clip(idx_float.astype(jnp.int32), 0, K - 2)
            idx_high = idx_low + 1
            t = idx_float - idx_low.astype(scores.dtype)
            val_low = knots[idx_low]
            val_high = knots[idx_high]
            return val_low + t * (val_high - val_low)

        def _forward(x, signatures_raw, knot_values, temperature, compress_w1, compress_b1, compress_w2, compress_b2, spline_w1, spline_b1, spline_w2, spline_b2, directions, norm_gamma, norm_beta, output_scale):
            B, T, D = x.shape
            xf = x.reshape(-1, D)
            q = jnp.where(signatures_raw > 0.3, 1.0, jnp.where(signatures_raw < -0.3, -1.0, 0.0)).astype(signatures_raw.dtype)
            sigs = signatures_raw + jax.lax.stop_gradient(q - signatures_raw)
            cluster_sigs = jnp.sign(sigs.reshape(NUM_CLUSTERS, TPC, D).mean(axis=1))
            cluster_scores = xf @ cluster_sigs.T
            cluster_gates = _calibrate(cluster_scores, knot_values, temperature)
            cluster_idx = jnp.argmax(cluster_gates, axis=-1)
            tile_scores = xf @ sigs.T
            tile_gates = _calibrate(tile_scores, knot_values, temperature)
            gates_by_cluster = tile_gates.reshape(-1, NUM_CLUSTERS, TPC)
            sel_gates = jnp.take_along_axis(gates_by_cluster, cluster_idx[:, None, None], axis=1)[:, 0, :]
            local_idx = jnp.argmax(sel_gates, axis=-1)
            tile_idx = cluster_idx * TPC + local_idx
            h = jax.nn.gelu(xf @ compress_w1 + compress_b1, approximate=False)
            comp = jnp.tanh(h @ compress_w2 + compress_b2)
            w1 = spline_w1[tile_idx]
            b1 = spline_b1[tile_idx]
            hh = jax.nn.relu(jnp.einsum('ni,nig->ng', comp, w1) + b1)
            w2 = spline_w2[tile_idx]
            b2 = spline_b2[tile_idx]
            mag = jnp.einsum('ng,ngo->no', hh, w2) + b2
            ffn_out = mag * directions[tile_idx] * output_scale[0]
            y = xf + ffn_out
            mu = y.mean(axis=-1, keepdims=True)
            var = ((y - mu) ** 2).mean(axis=-1, keepdims=True)
            y = (y - mu) / jnp.sqrt(var + EPS_LN) * norm_gamma + norm_beta
            return y.reshape(B, T, D)
        key = jax.random.key(seed)
        ks = jax.random.split(key, 12)
        B, T = (4, 1024)
        x = jax.random.normal(ks[0], (B, T, D_MODEL), dtype=jnp.float32)
        signatures_raw = jax.random.normal(ks[1], (NUM_TILES, D_MODEL), dtype=jnp.float32) * 0.5
        knot_values = jax.nn.sigmoid(jnp.linspace(-3.0, 3.0, NUM_KNOTS).astype(jnp.float32))
        temperature = jnp.ones((1,), dtype=jnp.float32)
        compress_w1 = jax.random.normal(ks[2], (D_MODEL, COMP_H), dtype=jnp.float32) * (1.0 / np.sqrt(D_MODEL))
        compress_b1 = jnp.zeros((COMP_H,), dtype=jnp.float32)
        compress_w2 = jax.random.normal(ks[3], (COMP_H, 2), dtype=jnp.float32) * (1.0 / np.sqrt(COMP_H))
        compress_b2 = jnp.zeros((2,), dtype=jnp.float32)
        spline_w1 = jax.random.normal(ks[4], (NUM_TILES, 2, GRID), dtype=jnp.float32) * (1.0 / np.sqrt(2.0))
        spline_b1 = jnp.zeros((NUM_TILES, GRID), dtype=jnp.float32)
        spline_w2 = jax.random.normal(ks[5], (NUM_TILES, GRID, 1), dtype=jnp.float32) * (1.0 / np.sqrt(GRID))
        spline_b2 = jnp.zeros((NUM_TILES, 1), dtype=jnp.float32)
        directions = jax.random.normal(ks[6], (NUM_TILES, D_MODEL), dtype=jnp.float32) * 0.02
        norm_gamma = jnp.ones((D_MODEL,), dtype=jnp.float32)
        norm_beta = jnp.zeros((D_MODEL,), dtype=jnp.float32)
        output_scale = jnp.ones((1,), dtype=jnp.float32) * 0.1
        return dict(x=x, signatures_raw=signatures_raw, knot_values=knot_values, temperature=temperature, compress_w1=compress_w1, compress_b1=compress_b1, compress_w2=compress_w2, compress_b2=compress_b2, spline_w1=spline_w1, spline_b1=spline_b1, spline_w2=spline_w2, spline_b2=spline_b2, directions=directions, norm_gamma=norm_gamma, norm_beta=norm_beta, output_scale=output_scale)
    _L0_ffn_all = _L0_ffn_setup()
    _L0_ffn_in = {k: v for k, v in _L0_ffn_all.items() if k in ('signatures_raw', 'knot_values', 'temperature', 'compress_w1', 'compress_b1', 'compress_w2', 'compress_b2', 'spline_w1', 'spline_b1', 'spline_w2', 'spline_b2', 'directions', 'norm_gamma', 'norm_beta', 'output_scale')}
    del _L0_ffn_all
    return {'x': x, 'cond_512': cond_512, 'L0_cond_weight': _L0_cond_in['weight'], 'L0_cond_bias': _L0_cond_in['bias'], 'L0_cond_affine_w': _L0_cond_in['affine_w'], 'L0_cond_affine_b': _L0_cond_in['affine_b'], 'L0_attn_norm_g': _L0_attn_in['norm_g'], 'L0_attn_norm_b': _L0_attn_in['norm_b'], 'L0_attn_Wq': _L0_attn_in['Wq'], 'L0_attn_Wkv': _L0_attn_in['Wkv'], 'L0_attn_q_scale': _L0_attn_in['q_scale'], 'L0_attn_k_scale': _L0_attn_in['k_scale'], 'L0_attn_null_kv': _L0_attn_in['null_kv'], 'L0_attn_Wout': _L0_attn_in['Wout'], 'L0_cond2_k_aff_w': _L0_cond2_in['k_aff_w'], 'L0_cond2_k_aff_b': _L0_cond2_in['k_aff_b'], 'L0_cond2_k_w': _L0_cond2_in['k_w'], 'L0_cond2_k_b': _L0_cond2_in['k_b'], 'L0_cond2_o_aff_w': _L0_cond2_in['o_aff_w'], 'L0_cond2_o_aff_b': _L0_cond2_in['o_aff_b'], 'L0_cond2_o_w': _L0_cond2_in['o_w'], 'L0_cond2_o_b': _L0_cond2_in['o_b'], 'L0_ffn_signatures_raw': _L0_ffn_in['signatures_raw'], 'L0_ffn_knot_values': _L0_ffn_in['knot_values'], 'L0_ffn_temperature': _L0_ffn_in['temperature'], 'L0_ffn_compress_w1': _L0_ffn_in['compress_w1'], 'L0_ffn_compress_b1': _L0_ffn_in['compress_b1'], 'L0_ffn_compress_w2': _L0_ffn_in['compress_w2'], 'L0_ffn_compress_b2': _L0_ffn_in['compress_b2'], 'L0_ffn_spline_w1': _L0_ffn_in['spline_w1'], 'L0_ffn_spline_b1': _L0_ffn_in['spline_b1'], 'L0_ffn_spline_w2': _L0_ffn_in['spline_w2'], 'L0_ffn_spline_b2': _L0_ffn_in['spline_b2'], 'L0_ffn_directions': _L0_ffn_in['directions'], 'L0_ffn_norm_gamma': _L0_ffn_in['norm_gamma'], 'L0_ffn_norm_beta': _L0_ffn_in['norm_beta'], 'L0_ffn_output_scale': _L0_ffn_in['output_scale']}

def reference(x, cond_512, L0_cond_weight, L0_cond_bias, L0_cond_affine_w, L0_cond_affine_b, L0_attn_norm_g, L0_attn_norm_b, L0_attn_Wq, L0_attn_Wkv, L0_attn_q_scale, L0_attn_k_scale, L0_attn_null_kv, L0_attn_Wout, L0_cond2_k_aff_w, L0_cond2_k_aff_b, L0_cond2_k_w, L0_cond2_k_b, L0_cond2_o_aff_w, L0_cond2_o_aff_b, L0_cond2_o_w, L0_cond2_o_b, L0_ffn_signatures_raw, L0_ffn_knot_values, L0_ffn_temperature, L0_ffn_compress_w1, L0_ffn_compress_b1, L0_ffn_compress_w2, L0_ffn_compress_b2, L0_ffn_spline_w1, L0_ffn_spline_b1, L0_ffn_spline_w2, L0_ffn_spline_b2, L0_ffn_directions, L0_ffn_norm_gamma, L0_ffn_norm_beta, L0_ffn_output_scale):
    import jax
    import jax.numpy as jnp

    def _L0_cond_ref(x, w, weight, bias, affine_w, affine_b):
        import jax, jax.numpy as jnp
        import numpy as np
        W_DIM = 128
        CLAMP = 256.0
        B, L, C = x.shape
        gain = 1.0 / np.sqrt(W_DIM).astype(np.float32)
        styles = w @ (affine_w * gain).T + affine_b
        ws = weight[None, :, :] * styles[:, None, :]
        dcoefs = jax.lax.rsqrt(jnp.sum(ws * ws, axis=2) + 1e-08)
        xm = x * styles[:, None, :]
        y = jnp.einsum('blc,oc->blo', xm, weight)
        y = y * dcoefs[:, None, :]
        y = jnp.clip(y + bias, -CLAMP, CLAMP)
        return y

    def _L0_attn_ref(x, norm_g, norm_b, Wq, Wkv, q_scale, k_scale, null_kv, Wout):
        import jax, jax.numpy as jnp
        import numpy as np
        import math
        B, N, DIM, H, DH, NNULL = (2, 512, 256, 16, 64, 2)
        SCALE = 8.0
        LN_EPS = 1e-05

        def _alibi_slopes(heads):
            start = 2.0 ** (-2.0 ** (-(math.log2(heads) - 3)))
            return np.array([start * start ** i for i in range(heads)], dtype=np.float32)

        def _l2norm(t):
            n = jnp.sqrt(jnp.sum(t * t, axis=-1, keepdims=True))
            return t / jnp.maximum(n, 1e-12)
        b, n, dim = x.shape
        h, dh, nn = (H, DH, NNULL)
        j = n + nn
        mu = jnp.mean(x, axis=-1, keepdims=True)
        var = jnp.mean((x - mu) ** 2, axis=-1, keepdims=True)
        xn = (x - mu) * jax.lax.rsqrt(var + LN_EPS) * norm_g + norm_b
        q = (xn @ Wq).reshape(b, n, h, dh).transpose(0, 2, 1, 3)
        kv = x @ Wkv
        k, v = jnp.split(kv, 2, axis=-1)
        k = k.reshape(b, n, h, dh).transpose(0, 2, 1, 3)
        v = v.reshape(b, n, h, dh).transpose(0, 2, 1, 3)
        null = null_kv.reshape(h, nn, 2, dh)
        nk = jnp.broadcast_to(null[:, :, 0, :][None], (b, h, nn, dh))
        nv = jnp.broadcast_to(null[:, :, 1, :][None], (b, h, nn, dh))
        k = jnp.concatenate([nk, k], axis=2)
        v = jnp.concatenate([nv, v], axis=2)
        q = _l2norm(q) * q_scale
        k = _l2norm(k) * k_scale
        sim = jnp.einsum('bhid,bhjd->bhij', q, k) * SCALE
        irow = jnp.arange(j - n, j)
        jcol = jnp.arange(j)
        bias = -jnp.abs(jcol[None, :] - irow[:, None]).astype(sim.dtype)
        slopes = jnp.asarray(_alibi_slopes(h))[:, None, None]
        sim = sim + slopes * bias
        causal = jnp.triu(jnp.ones((n, j), dtype=bool), k=j - n + 1)
        neg = jnp.finfo(sim.dtype).max
        sim = jnp.where(causal[None, None], -neg, sim)
        attn = jax.nn.softmax(sim, axis=-1)
        out = jnp.einsum('bhij,bhjd->bhid', attn, v)
        out = out.transpose(0, 2, 1, 3).reshape(b, n, h * dh)
        return out @ Wout

    def _L0_cond2_ref(x, s, k_aff_w, k_aff_b, k_w, k_b, o_aff_w, o_aff_b, o_w, o_b):
        import jax, jax.numpy as jnp
        import numpy as np
        import math
        HEAD_NUM = 16
        EPS = 1e-08

        def modulated_linear(x, s, aff_w, aff_b, w, b):
            style = s @ aff_w.T + aff_b
            w_mod = w[None, :, :] * style[:, None, :]
            demod = jax.lax.rsqrt(jnp.sum(w_mod * w_mod, axis=2) + EPS)
            w_mod = w_mod * demod[:, :, None]
            return jnp.einsum('bni,boi->bno', x, w_mod) + b
        B, N, F = x.shape
        H = HEAD_NUM
        D = F // H
        kx = modulated_linear(x, s, k_aff_w, k_aff_b, k_w, k_b)
        kx = kx.reshape(B, N, H, D)
        q = k = v = kx
        scores = jnp.einsum('bnhd,bnjd->bnhj', q, k) / math.sqrt(D)
        A = jax.nn.softmax(scores, axis=-1)
        out = jnp.einsum('bnhj,bnjd->bnhd', A, v).reshape(B, N, F)
        out = modulated_linear(out, s, o_aff_w, o_aff_b, o_w, o_b)
        return out

    def _L0_ffn_ref(x, signatures_raw, knot_values, temperature, compress_w1, compress_b1, compress_w2, compress_b2, spline_w1, spline_b1, spline_w2, spline_b2, directions, norm_gamma, norm_beta, output_scale):
        import jax, jax.numpy as jnp
        import numpy as np
        D_MODEL = 256
        NUM_TILES = 64
        TPC = 8
        NUM_CLUSTERS = NUM_TILES // TPC
        GRID = 16
        COMP_H = 64
        NUM_KNOTS = 8
        EPS_LN = 1e-05

        def _calibrate(scores, knots, temperature):
            K = knots.shape[0]
            normalized = jax.nn.sigmoid(scores / (temperature[0] + 1e-06))
            idx_float = normalized * (K - 1)
            idx_low = jnp.clip(idx_float.astype(jnp.int32), 0, K - 2)
            idx_high = idx_low + 1
            t = idx_float - idx_low.astype(scores.dtype)
            val_low = knots[idx_low]
            val_high = knots[idx_high]
            return val_low + t * (val_high - val_low)

        def _forward(x, signatures_raw, knot_values, temperature, compress_w1, compress_b1, compress_w2, compress_b2, spline_w1, spline_b1, spline_w2, spline_b2, directions, norm_gamma, norm_beta, output_scale):
            B, T, D = x.shape
            xf = x.reshape(-1, D)
            q = jnp.where(signatures_raw > 0.3, 1.0, jnp.where(signatures_raw < -0.3, -1.0, 0.0)).astype(signatures_raw.dtype)
            sigs = signatures_raw + jax.lax.stop_gradient(q - signatures_raw)
            cluster_sigs = jnp.sign(sigs.reshape(NUM_CLUSTERS, TPC, D).mean(axis=1))
            cluster_scores = xf @ cluster_sigs.T
            cluster_gates = _calibrate(cluster_scores, knot_values, temperature)
            cluster_idx = jnp.argmax(cluster_gates, axis=-1)
            tile_scores = xf @ sigs.T
            tile_gates = _calibrate(tile_scores, knot_values, temperature)
            gates_by_cluster = tile_gates.reshape(-1, NUM_CLUSTERS, TPC)
            sel_gates = jnp.take_along_axis(gates_by_cluster, cluster_idx[:, None, None], axis=1)[:, 0, :]
            local_idx = jnp.argmax(sel_gates, axis=-1)
            tile_idx = cluster_idx * TPC + local_idx
            h = jax.nn.gelu(xf @ compress_w1 + compress_b1, approximate=False)
            comp = jnp.tanh(h @ compress_w2 + compress_b2)
            w1 = spline_w1[tile_idx]
            b1 = spline_b1[tile_idx]
            hh = jax.nn.relu(jnp.einsum('ni,nig->ng', comp, w1) + b1)
            w2 = spline_w2[tile_idx]
            b2 = spline_b2[tile_idx]
            mag = jnp.einsum('ng,ngo->no', hh, w2) + b2
            ffn_out = mag * directions[tile_idx] * output_scale[0]
            y = xf + ffn_out
            mu = y.mean(axis=-1, keepdims=True)
            var = ((y - mu) ** 2).mean(axis=-1, keepdims=True)
            y = (y - mu) / jnp.sqrt(var + EPS_LN) * norm_gamma + norm_beta
            return y.reshape(B, T, D)
        return _forward(x, signatures_raw, knot_values, temperature, compress_w1, compress_b1, compress_w2, compress_b2, spline_w1, spline_b1, spline_w2, spline_b2, directions, norm_gamma, norm_beta, output_scale)
    x = x + _L0_attn_ref(_L0_cond_ref(x, cond_512, L0_cond_weight, L0_cond_bias, L0_cond_affine_w, L0_cond_affine_b), L0_attn_norm_g, L0_attn_norm_b, L0_attn_Wq, L0_attn_Wkv, L0_attn_q_scale, L0_attn_k_scale, L0_attn_null_kv, L0_attn_Wout)
    x = x + _L0_ffn_ref(_L0_cond2_ref(x, cond_512, L0_cond2_k_aff_w, L0_cond2_k_aff_b, L0_cond2_k_w, L0_cond2_k_b, L0_cond2_o_aff_w, L0_cond2_o_aff_b, L0_cond2_o_w, L0_cond2_o_b), L0_ffn_signatures_raw, L0_ffn_knot_values, L0_ffn_temperature, L0_ffn_compress_w1, L0_ffn_compress_b1, L0_ffn_compress_w2, L0_ffn_compress_b2, L0_ffn_spline_w1, L0_ffn_spline_b1, L0_ffn_spline_w2, L0_ffn_spline_b2, L0_ffn_directions, L0_ffn_norm_gamma, L0_ffn_norm_beta, L0_ffn_output_scale)
    return x

_drawn_inputs = setup_inputs


def setup_inputs(seed=0):
    import zlib

    import numpy as np

    out = dict(_drawn_inputs(seed))
    spreads = {'L0_cond_affine_b': (1.0, 0.6),
     'L0_attn_norm_g': (1.0, 0.6),
     'L0_attn_norm_b': (0.0, 0.728),
     'L0_attn_q_scale': (1.0, 0.6),
     'L0_attn_k_scale': (1.0, 0.6),
     'L0_cond2_k_aff_b': (1.0, 0.2),
     'L0_cond2_k_b': (0.0, 0.1),
     'L0_cond2_o_aff_b': (1.0, 0.2),
     'L0_cond2_o_b': (0.0, 0.1),
     'L0_ffn_compress_b1': (0.0, 0.8),
     'L0_ffn_compress_b2': (0.0, 0.8),
     'L0_ffn_spline_b1': (0.0, 0.8),
     'L0_ffn_spline_b2': (0.0, 0.8),
     'L0_ffn_norm_gamma': (1.0, 0.2),
     'L0_ffn_norm_beta': (0.0, 0.1)}
    factors = {'L0_ffn_signatures_raw': 8.0,
     'L0_ffn_knot_values': 8.0,
     'L0_ffn_compress_w1': 8.0,
     'L0_ffn_compress_w2': 8.0,
     'L0_ffn_spline_w1': 8.0,
     'L0_ffn_spline_w2': 8.0,
     'L0_ffn_directions': 8.0}
    for name, (base, spread) in spreads.items():
        noise = np.random.default_rng([zlib.crc32(name.encode()), seed]).standard_normal(out[name].shape)
        drawn = base * np.exp(spread * noise) if base else spread * noise
        out[name] = jnp.asarray(drawn.astype(out[name].dtype))
    for name, factor in factors.items():
        out[name] = (out[name] * factor).astype(out[name].dtype)
    return out
```

```python
import concourse.bass as bass
from concourse import mybir
from contextlib import ExitStack


def adaln_attention_ffn(nc: bass.Bass, A: dict, out: bass.AP):
    f32, bf16 = mybir.dt.float32, mybir.dt.bfloat16
    ALU, ACT, AX = mybir.AluOpType, mybir.ActivationFunctionType, mybir.AxisListType.X

    NB, L, C = A["x"].shape
    P = 128
    BT = P // L
    T = NB * L // P
    CK = C // P
    H, DH = 16, 64
    HP = H // 2
    NN = 2
    J = L + NN
    PJ = 2 * J
    V1 = DH + 1
    INNER = H * DH
    DM = C // H
    TG = P // H
    G = P // TG
    QG = 4
    DP = 32
    NT, NC = 64, 8
    TPC = NT // NC
    KN = 8
    GRID = 16
    CH = 64
    NS = NC + NT
    GATH = 2 * GRID + GRID + GRID + 1 + C
    CLAMP = 256.0
    LN_EPS = 1e-5

    ctx = ExitStack()
    with ctx:
        def sb(name, shape, dt=f32):
            return ctx.enter_context(nc.sbuf_tensor(name, shape, dt))

        sems = {}

        def S(name):
            if name not in sems:
                sems[name] = ctx.enter_context(nc.semaphore(name))
            return sems[name]

        def wait(eng, name, t, by=1):
            eng.wait_ge(S(name), (t + 1) * by)

        def wait_before(eng, name, t, back=1, by=1):
            if isinstance(t, int) and t < back:
                return
            eng.wait_ge(S(name), (t + 1 - back) * by)

        def wait_dma(eng, name, t, p):
            eng.wait_ge(S(name + "_even" * (not p) + "_odd" * p), (t - p) * 8 + 16)

        def wait_dma_before(eng, name, t, p):
            if isinstance(t, int) and t < 2:
                return
            eng.wait_ge(S(name + "_even" * (not p) + "_odd" * p), (t - p) * 8)

        def D(name, p):
            return S(name + "_even" * (not p) + "_odd" * p)

        ident = sb("ident", [P, P])
        identb = sb("identb", [P, P], bf16)
        offmask = sb("offmask", [P, QG, P], bf16)
        alibi = sb("alibi", [P, HP, PJ])
        wc = sb("wc", [P, CK, C])
        wk2 = sb("wk2", [P, CK, C])
        wo2 = sb("wo2", [P, CK, C])
        wq = sb("wq", [P, CK, INNER])
        wk = sb("wk", [P, CK, INNER])
        wv = sb("wv", [P, CK, INNER])
        wout = sb("wout", [P, HP, C])
        wsc = sb("wsc", [P, CK, NS + CH])
        sty = sb("sty", [P, 3, CK, NB])
        dem = sb("dem", [P, 3, CK, NB])
        cols = sb("cols", [P, 8, CK])
        CB, NG, NBI, KB, OB, AB0, AB1, AB2 = range(8)
        qks = sb("qks", [P, 2])
        nullw = sb("nullw", [H * NN, C])

        xin = sb("xin", [P, 2, C])
        xm = sb("xm", [P, CK, BT, L])
        yT = sb("yT", [P, CK, BT, L])
        xn = sb("xn", [P, C])
        xnT = sb("xnT", [P, CK, P])
        sq = sb("sq", [P, INNER])
        kn = sb("kn", [P, INNER])
        qn = sb("qn", [P, INNER])
        qT = sb("qT", [P, HP, P])
        kbd = sb("kbd", [P, BT, HP, PJ])
        vbd = sb("vbd", [P, BT, HP, 2, V1])
        pr = sb("pr", [P, HP, PJ])
        pT = sb("pT", [P, HP, P])
        on = sb("on", [P, INNER])
        yTs = sb("yTs", [P, CK, BT, L])
        pnr = sb("pnr", [P, H, NN])
        mxn = sb("mxn", [P, H])
        mxm = sb("mxm", [P, H])
        oT = sb("oT", [P, HP, P])
        pn = sb("pn", [P, H, NN])
        pnT = sb("pnT", [H * NN, P])
        st6 = sb("st6", [P, 6])
        mv = sb("mv", [P, 2])
        ve = sb("ve", [P, 1])
        rs = sb("rs", [P, 1])
        nrm = sb("nrm", [P, 2, H])
        nrg = sb("nrg", [P, 2, H])
        rn = sb("rn", [P, 2, H])
        mhalf = sb("mhalf", [P, H])
        eps = sb("eps", [P, 1])
        pad = sb("pad", [P, 1])
        mx = sb("mx", [P, H])
        den = sb("den", [P, H])
        den2 = sb("den2", [P, H])
        rden = sb("rden", [P, H])
        x1 = sb("x1", [P, 2, C])
        xm2 = sb("xm2", [P, CK, BT, L])
        kxd_ = sb("kxd_", [P, CK, BT, L])
        kxT = sb("kxT", [P, CK, P])
        kxn = sb("kxn", [P, C])
        v2 = sb("v2", [P, 2, G, DP])
        kT = sb("kT", [P, QG, P])
        E = sb("E", [P, QG, QG, P])
        ET = sb("ET", [P, QG, QG, P])
        mx2 = sb("mx2", [P, QG, QG])
        av = sb("av", [P, QG, P])
        rd2 = sb("rd2", [P, G])
        o2 = sb("o2", [P, G, DM])
        on2 = sb("on2", [P, C])
        om = sb("om", [P, CK, BT, L])
        zd = sb("zd", [P, CK, BT, L])
        zT = sb("zT", [P, CK, P])
        zn = sb("zn", [P, C])
        SC = sb("SC", [P, T, NS])
        HPR = sb("HPR", [P, T, CH])

        pa = ctx.enter_context(nc.psum_tensor("pa", [P, 4, 512], f32))
        pc = ctx.enter_context(nc.psum_tensor("pc", [P, 2, 512], f32))
        pb = ctx.enter_context(nc.psum_tensor("pb", [P, 512], f32))
        pd = ctx.enter_context(nc.psum_tensor("pd", [P, 512], f32))

        x1d = nc.dram_tensor("x1d", [T, P, C], f32)
        kxdr = nc.dram_tensor("kxdr", [T, P, C], f32)
        odr = nc.dram_tensor("odr", [T, P, C], f32)
        xfd = nc.dram_tensor("xfd", [T, P, C], f32)
        x_t = A["x"].rearrange("(t b) l c -> t (b l) c", b=BT)
        out_t = out.rearrange("(t b) l c -> t (b l) c", b=BT)

        def mixed(dram, t):
            return dram[bass.ds(t, 1), :, :].rearrange(
                "o (g k) (h d) -> (o k h) g d", k=TG, h=H)

        def plain(dram, t):
            return dram[bass.ds(t, 1), :, :].rearrange("o p c -> (o p) c")

        def bc(ap, axis, n):
            u = ap.unsqueeze(axis)
            shape = list(u.shape)
            shape[axis] = n
            return u.broadcast_to(shape)

        def two(bank, lo):
            return bank[:, lo:lo + C].rearrange("p (k q) -> p k q", k=CK)

        rawT = E[:, :, :, :].rearrange("p a b c -> p (a b c)")
        awT = rawT[:, 0:3 * C].rearrange("p (m c) -> p m c", m=3)
        condT = rawT[:, 3 * C:3 * C + NB]
        w2 = ET[:, :, :, :].rearrange("p a b c -> p (a b c)")[:, 0:3 * CK * C].rearrange(
            "p (m k c) -> p m k c", m=3, k=CK)
        s2 = rawT[:, 1024:1024 + 3 * CK * NB].rearrange("p (m k n) -> p m k n", m=3, k=CK)
        sig = kn[:, 0:CK * NT].rearrange("p (k n) -> p k n", k=CK)
        sg1 = kn[:, 256:256 + CK * NT].rearrange("p (k n) -> p k n", k=CK)
        sg2 = kn[:, 512:512 + CK * NT].rearrange("p (k n) -> p k n", k=CK)
        acc = kn[:, 768:768 + CK * NC].rearrange("p (k n) -> p k n", k=CK)
        acp = kn[:, 800:800 + CK * NC].rearrange("p (k n) -> p k n", k=CK)
        acn = kn[:, 832:832 + CK * NC].rearrange("p (k n) -> p k n", k=CK)
        NR = HP * NN
        nk = qn[0:NR, 0:P].rearrange("r (a d) -> r a d", a=2)
        nv = qn[0:NR, P:2 * P].rearrange("r (a d) -> r a d", a=2)
        nks = qn[0:NR, 2 * P:3 * P].rearrange("r (a d) -> r a d", a=2)
        nkh = qn[0:NR, 3 * P:4 * P].rearrange("r (a d) -> r a d", a=2)
        nvbd = sq[:, 0:HP * H * NN].rearrange("p (r n) -> p r n", r=HP)
        dsq = on[:, 0:3 * CK * NB].rearrange("p (m k n) -> p m k n", m=3, k=CK)
        drt = pT[:, :, :].rearrange("p a b -> p (a b)")[:, 0:3 * CK * NB].rearrange(
            "p (m k n) -> p m k n", m=3, k=CK)
        dnw = oT[:, :, :].rearrange("p a b -> p (a b)")[:, 0:3 * CK * NB].rearrange(
            "p (m k n) -> p m k n", m=3, k=CK)
        linear = ["L0_cond_weight", "L0_cond2_k_w", "L0_cond2_o_w"]
        affine = ["L0_cond_affine_w", "L0_cond2_k_aff_w", "L0_cond2_o_aff_w"]
        LOADS = 30

        def load_all(sp):
            n = [0]

            def ld(dst, src):
                sp.dma_start(dst, src).then_inc(S("weights"), 16)
                n[0] += 1

            ld(condT, A["condT"])
            for m, name in enumerate(affine):
                ld(awT[:, m, :], A[name + "T"])
            for dst, name in zip((wc, wk2, wo2), linear):
                ld(dst[:, :, :], A[name + "T"].rearrange("(k p) n -> p k n", p=P))
            for n_, name in ((CB, "L0_cond_bias"), (NG, "L0_attn_norm_g"), (NBI, "L0_attn_norm_b"),
                             (KB, "L0_cond2_k_b"), (OB, "L0_cond2_o_b"), (AB0, "L0_cond_affine_b"),
                             (AB1, "L0_cond2_k_aff_b"), (AB2, "L0_cond2_o_aff_b")):
                ld(cols[:, n_, :], A[name + "_c"])
            ld(qks[:, :], A["qk_scale"])
            ld(sig, A["sigT"].rearrange("(k p) n -> p k n", p=P))
            ld(nk, A["null_k"])
            ld(nv, A["null_v"])
            ld(alibi[:, :, :], A["alibi"])
            ld(wq[:, :, :], A["L0_attn_Wq"].rearrange("(k p) n -> p k n", p=P))
            ld(wk[:, :, :], A["Wk"].rearrange("(k p) n -> p k n", p=P))
            ld(wv[:, :, :], A["Wv"].rearrange("(k p) n -> p k n", p=P))
            ld(wout[:, :, :], A["L0_attn_Wout"].rearrange("(r p) n -> p r n", p=P))
            ld(wsc[:, :, NS:NS + CH], A["L0_ffn_compress_w1"].rearrange("(k p) n -> p k n", p=P))
            ld(ident[:, :], A["ident"])
            ld(coef[:, :], A["coef"])
            ld(gb[:, :, :], A["gb"])
            ld(gath[:, :], A["gath"])
            ld(offmask[:, :, :], A["offmask"])
            assert n[0] == LOADS, n[0]

        coef = sb("coef", [P, 2 * CH + CH + 2 + KN + NC + 2])
        gb = sb("gb", [P, 2, C])
        gath = sb("gath", [NT, GATH])
        CO = {}
        at = 0
        for name, n in (("w2", 2 * CH), ("b1", CH), ("b2", 2), ("knots", KN), ("iota", NC), ("temp", 1),
                        ("scale", 1)):
            CO[name] = coef[:, at:at + n]
            at += n
        ninv = sb("ninv", [P, 2])
        kdif = sb("kdif", [P, KN])
        clo = sb("clo", [P, T, NC])
        loc = sb("loc", [P, T, NC])
        comp = sb("comp", [P, T, 2])
        best = sb("best", [P, 2, T])
        oh = sb("oh", [P, 2, P])
        ohT = sb("ohT", [NT, 2, P])
        gs = sb("gs", [P, 2, GATH])
        cc = sb("cc", [P, 2, 2])
        hid = sb("hid", [P, 2, 2, GRID])
        junk = sb("junk", [P, 2, GRID])
        mag = sb("mag", [P, 2, 2])
        yy = sb("yy", [P, 2, C])
        ys6 = sb("ys6", [P, 2, 6])
        ymv = sb("ymv", [P, 2, 2])
        yve = sb("yve", [P, 2, 2])
        yn = sb("yn", [P, 2, C])
        res = sb("res", [P, 2, C])

        def tiles8(buf, part):
            return buf[:, part * 512:(part + 1) * 512].rearrange("p (t c) -> p t c", c=NC)

        score, knot_at, frac = tiles8(sq, 0), tiles8(sq, 1), tiles8(qn, 0)
        low, rise, pick = tiles8(qn, 1), tiles8(on, 0), tiles8(on, 1)
        local = tiles8(kn, 0)
        TH = T // 2
        prod = [z[:, :, :, :].rearrange("p a b c -> p (a b c)") for z in (E, ET)]

        def final_loads(sp):
            def back(t, p):
                wait_before(sp, "res_done", t, 2)
                wait_before(sp, "y_sum", t, 2)
                sp.dma_start(xin[:, p, :], plain(x1d, t)).then_inc(D("x1_back", p), 16)
                sp.dma_start(x1[:, p, :], plain(xfd, t)).then_inc(D("xf_back", p), 16)

            def out_(t, p):
                wait(sp, "res_done", t)
                sp.dma_start(plain(out_t, t), res[:, p, :]).then_inc(D("out", p), 16)

            back(0, 0)
            back(1, 1)
            out_(0, 0)
            with sp.Fori(0, (T - 2) // 2) as n:
                t = n * 2 + 2
                back(t, 0)
                out_(t - 1, 1)
                back(t + 1, 1)
                out_(t, 0)
            out_(T - 1, 1)
            for p in range(2):
                sp.wait_ge(D("out", p), T * 8)
            for name in ("kx_out", "o2_out"):
                sp.wait_ge(S(name), T * 16)

        def final_loop(eng, step):
            step(0, 0)
            step(1, 1)
            with eng.Fori(0, (T - 2) // 2) as n:
                t = n * 2 + 2
                step(t, 0)
                step(t + 1, 1)

        def final_pe(pe):
            def step(t, p):
                wait(pe, "oh_done", t)
                wait_before(pe, "ohT_done", t, 1)
                nc.tensor.transpose(pa[:, p, 0:P], oh[:, p, :], ident[:, :]).then_inc(S("ohT_mm"), 1)
                wait(pe, "ohT_done", t)
                wait_before(pe, "gs_done", t, 2)
                nc.tensor.matmul(pa[:, 2 + p, 0:GATH], ohT[:, p, :], gath[:, :], start=True, stop=True)\
                    .then_inc(S("gathered"), 1)

            final_loop(pe, step)

        def final_act(act):
            fn = nc.scalar.activation
            act.wait_ge(S("temp_done"), 1)
            act.wait_ge(S("scores_done"), T)
            fn(score, SC[:, :, 0:NC], ACT.Exp, scale=ninv[:, 1:2]).then_inc(S("cluster_exp"), 1)
            act.wait_ge(S("local_score"), 1)
            fn(score, local, ACT.Exp, scale=ninv[:, 1:2]).then_inc(S("local_exp"), 1)
            act.wait_ge(S("pre_bias"), 1)
            fn(HPR[:, :, :], HPR[:, :, :], ACT.Gelu).then_inc(S("gelu_done"), 1)
            act.wait_ge(S("comp_pre"), 1)
            fn(comp[:, :, :], comp[:, :, :], ACT.Tanh).then_inc(S("comp_done"), 1)

            def step(t, p):
                wait(act, "ohT_mm", t)
                wait_before(act, "gathered", t, 2)
                fn(ohT[:, p, :], pa[0:NT, p, 0:P], ACT.Copy).then_inc(S("ohT_done"), 1)
                wait(act, "gathered", t)
                wait_before(act, "y_sum", t, 2)
                fn(gs[:, p, :], pa[:, 2 + p, 0:GATH], ACT.Copy).then_inc(S("gs_done"), 1)

            final_loop(act, step)

        def final_dve(dve, link):
            v = nc.vector
            link(v.tensor_scalar(ninv[:, 0:1], CO["temp"], 1e-6, -1.0, ALU.add, ALU.mult))
            v.reciprocal(ninv[:, 1:2], ninv[:, 0:1]).then_inc(S("temp_done"), 1)
            link(v.tensor_tensor(kdif[:, 0:KN - 1], CO["knots"][:, 1:KN], CO["knots"][:, 0:KN - 1],
                                 ALU.subtract))

            def calibrate():
                link(v.tensor_scalar(score, score, 1.0, None, ALU.add))
                link(v.reciprocal(score, score))
                link(v.tensor_scalar(score, score, float(KN - 1), None, ALU.mult))
                link(v.tensor_scalar(knot_at, score, 1.0, None, ALU.is_ge))
                for k in range(2, KN - 1):
                    link(v.scalar_tensor_tensor(out=knot_at, in0=score, scalar=float(k), in1=knot_at,
                                                op0=ALU.is_ge, op1=ALU.add))
                link(v.tensor_tensor(frac, score, knot_at, ALU.subtract))
                link(v.tensor_scalar(low, knot_at, 0.0, CO["knots"][:, 0:1], ALU.is_equal, ALU.mult))
                link(v.tensor_scalar(rise, knot_at, 0.0, kdif[:, 0:1], ALU.is_equal, ALU.mult))
                for k in range(1, KN - 1):
                    for dst, val in ((low, CO["knots"]), (rise, kdif)):
                        link(v.tensor_scalar(pick, knot_at, float(k), val[:, k:k + 1], ALU.is_equal, ALU.mult))
                        link(v.tensor_tensor(dst, dst, pick, ALU.add))
                link(v.tensor_tensor(frac, frac, rise, ALU.mult))
                link(v.tensor_tensor(score, low, frac, ALU.add))

            def first_best(dst):
                link(v.tensor_reduce(best[:, 0, :], score, AX, ALU.max))
                link(v.tensor_tensor(pick, score, bc(best[:, 0, :], 2, NC), ALU.is_equal))
                link(v.tensor_tensor(pick, pick, bc(CO["iota"], 1, T), ALU.mult))
                link(v.tensor_reduce(best[:, 1, :], pick, AX, ALU.min))
                link(v.tensor_tensor(dst, bc(CO["iota"], 1, T), bc(best[:, 1, :], 2, NC), ALU.is_equal))

            dve.wait_ge(S("cluster_exp"), 1)
            calibrate()
            first_best(clo[:, :, :])
            for n in range(2):
                t = slice(n * TH, (n + 1) * TH)
                link(v.tensor_tensor(prod[n].rearrange("p (t c k) -> p t c k", c=NC, k=TPC),
                                     SC[:, t, NC:NS].rearrange("p t (c k) -> p t c k", k=TPC),
                                     bc(clo[:, t, :], 3, TPC), ALU.mult))
                link(v.tensor_reduce(local[:, t, :], prod[n].rearrange("p (t c k) -> p t k c", c=NC, k=TPC),
                                     AX, ALU.add))
            v.tensor_tensor(HPR[:, :, :], HPR[:, :, :], bc(CO["b1"], 1, T), ALU.add).then_inc(S("pre_bias"), 1)
            v.tensor_copy(local, local).then_inc(S("local_score"), 1)
            dve.wait_ge(S("local_exp"), 1)
            calibrate()
            first_best(loc[:, :, :])
            dve.wait_ge(S("gelu_done"), 1)
            for n in range(2):
                t = slice(n * TH, (n + 1) * TH)
                for o in range(2):
                    w = bc(CO["w2"][:, o * CH:(o + 1) * CH], 1, TH)
                    buf = prod[o].rearrange("p (t n) -> p t n", n=CH)
                    link(v.tensor_tensor(buf, HPR[:, t, :], w, ALU.mult))
                    link(v.tensor_reduce(comp[:, t, o], buf, AX, ALU.add))
            v.tensor_tensor(comp[:, :, :], comp[:, :, :], bc(CO["b2"], 1, T), ALU.add)\
                .then_inc(S("comp_pre"), 1)
            dve.wait_ge(S("comp_done"), 1)

            def first(t, p):
                wait_before(dve, "ohT_mm", t, 2)
                one = lambda z: z[:, bass.ds(t, 1), :].rearrange("p o n -> p (o n)")
                v.tensor_tensor(oh[:, p, 0:NT].rearrange("p (c k) -> p c k", k=TPC), bc(one(clo), 2, TPC),
                                bc(one(loc), 1, NC), ALU.mult).then_inc(S("oh_done"), 1)
                v.tensor_copy(cc[:, p, :], one(comp)).then_inc(S("cc_done"), 1)
                wait(dve, "cc_done", t)
                wait(dve, "gs_done", t)
                G_ = gs[:, p, :]
                v.scalar_tensor_tensor(out=hid[:, p, 0, :], in0=G_[:, 0:GRID], scalar=cc[:, p, 0:1],
                                       in1=G_[:, 2 * GRID:3 * GRID], op0=ALU.mult, op1=ALU.add)\
                    .then_inc(S("hid_0"), 1)
                wait(dve, "hid_0", t)
                v.scalar_tensor_tensor(out=hid[:, p, 1, :], in0=G_[:, GRID:2 * GRID], scalar=cc[:, p, 1:2],
                                       in1=hid[:, p, 0, :], op0=ALU.mult, op1=ALU.add)\
                    .then_inc(S("hid_1"), 1)
                wait(dve, "hid_1", t)
                v.scalar_tensor_tensor(out=junk[:, p, :], in0=hid[:, p, 1, :], scalar=0.0,
                                       in1=G_[:, 3 * GRID:4 * GRID], op0=ALU.max, op1=ALU.mult,
                                       accum_out=mag[:, p, 0:1]).then_inc(S("mag_sum"), 1)
                wait(dve, "mag_sum", t)
                v.tensor_scalar(mag[:, p, 1:2], mag[:, p, 0:1], G_[:, 4 * GRID:4 * GRID + 1], CO["scale"],
                                ALU.add, ALU.mult).then_inc(S("mag_done"), 1)
                wait(dve, "mag_done", t)
                wait_dma(dve, "xf_back", t, p)
                v.scalar_tensor_tensor(out=yy[:, p, :], in0=G_[:, 4 * GRID + 1:GATH], scalar=mag[:, p, 1:2],
                                       in1=x1[:, p, :], op0=ALU.mult, op1=ALU.add).then_inc(S("y_sum"), 1)
                wait(dve, "y_sum", t)
                v.bn_stats(ys6[:, p, :], yy[:, p, :]).then_inc(S("y_stats"), 1)
                wait(dve, "y_stats", t)
                v.memset(pad[:, :], 0.0)
                v.bn_aggr(ymv[:, p, :], ys6[:, p, :]).then_inc(S("y_moments"), 1)

            def second(t, p):
                wait(dve, "y_rsqrt", t)
                wait_before(dve, "res_done", t, 2)
                v.tensor_scalar(yn[:, p, :], yy[:, p, :], ymv[:, p, 0:1], yve[:, p, 1:2],
                                ALU.subtract, ALU.mult).then_inc(S("yn_done"), 1)

            first(0, 0)
            first(1, 1)
            second(0, 0)
            with dve.Fori(0, (T - 2) // 2) as n:
                t = n * 2 + 2
                first(t, 0)
                second(t - 1, 1)
                first(t + 1, 1)
                second(t, 0)
            second(T - 1, 1)

        def final_pool(pool):
            g = nc.gpsimd

            def rsqrt(t, p):
                wait(pool, "y_moments", t)
                g.tensor_tensor(yve[:, p, 0:1], ymv[:, p, 1:2], eps[:, :], ALU.add).then_inc(S("yve_0"), 1)
                wait(pool, "yve_0", t)
                g.tensor_tensor(yve[:, p, 1:2], yve[:, p, 0:1], mhalf[:, 0:1], ALU.pow)\
                    .then_inc(S("y_rsqrt"), 1)

            def scale(t, p):
                wait_dma(pool, "x1_back", t, p)
                wait_dma_before(pool, "out", t, p)
                g.tensor_tensor(xin[:, p, :], xin[:, p, :], gb[:, 1, :], ALU.add).then_inc(S("x1_beta"), 1)
                wait(pool, "yn_done", t)
                g.tensor_tensor(yn[:, p, :], yn[:, p, :], gb[:, 0, :], ALU.mult).then_inc(S("yn_gamma"), 1)
                wait(pool, "yn_gamma", t)
                wait(pool, "x1_beta", t)
                g.tensor_tensor(res[:, p, :], yn[:, p, :], xin[:, p, :], ALU.add).then_inc(S("res_done"), 1)

            rsqrt(0, 0)
            rsqrt(1, 1)
            scale(0, 0)
            with pool.Fori(0, (T - 2) // 2) as n:
                t = n * 2 + 2
                rsqrt(t, 0)
                scale(t - 1, 1)
                rsqrt(t + 1, 1)
                scale(t, 0)
            scale(T - 1, 1)

        def pipeline(eng, step):
            step(0, 0, True, False, False, False, True)
            step(1, 1, True, True, False, False, True)
            step(2, 0, True, True, True, False, True)
            step(3, 1, True, True, True, True, True)
            with eng.Fori(0, (T - 6) // 2) as n:
                i = n * 2 + 4
                step(i, 0, True, True, True, True, True)
                step(i + 1, 1, True, True, True, True, True)
            step(T - 2, 0, True, True, True, True, True)
            step(T - 1, 1, True, True, True, True, False)
            step(T, 0, False, True, True, True, False)
            step(T + 1, 1, False, False, True, True, False)
            step(T + 2, 0, False, False, False, True, False)

        block = ctx.enter_context(nc.Block())

        @block.sync
        def _(sp):
            load_all(sp)

            def x_load(t, p):
                wait_before(sp, "x1_done", t, 2)
                sp.dma_start(xin[:, p, :], plain(x_t, t)).then_inc(D("x_in", p), 16)

            def mix_in(t, p):
                wait_before(sp, "av_mm", t, 2)
                wait(sp, "kxn_done", t)
                sp.dma_start(plain(kxdr, t), kxn[:, :]).then_inc(S("kx_out"), 16)
                wait(sp, "kx_out", t, 16)
                sp.dma_start(v2[:, p, :, 0:DM], mixed(kxdr, t)).then_inc(D("v2_in", p), 16)

            def mix_out(t):
                wait_before(sp, "omT", t, 1)
                wait(sp, "o2_done", t)
                sp.dma_start(mixed(odr, t), o2[:, :, :]).then_inc(S("o2_out"), 16)
                wait(sp, "o2_out", t, 16)
                sp.dma_start(on2[:, :], plain(odr, t)).then_inc(S("on2_in"), 16)

            def xf_out(t):
                wait(sp, "zn_done", t)
                sp.dma_start(plain(xfd, t), zn[:, :]).then_inc(S("xf_out"), 16)

            def x1_out(t, p):
                wait(sp, "x1_done", t)
                sp.dma_start(plain(x1d, t), x1[:, p, :]).then_inc(D("x1_out", p), 16)

            def step(i, p, a, b, c, d, more):
                if more:
                    x_load(i + 1, 1 - p)
                if b:
                    mix_in(i - 1, 1 - p)
                if c:
                    mix_out(i - 2)
                if d:
                    xf_out(i - 3)
                if a:
                    x1_out(i, p)

            x_load(0, 0)
            pipeline(sp, step)

            for p in range(2):
                sp.wait_ge(D("x1_out", p), T * 8)
            sp.wait_ge(S("xf_out"), T * 16)
            final_loads(sp)

        @block.tensor
        def _(pe):
            mm = nc.tensor.matmul
            pe.wait_ge(S("weights"), 16 * LOADS)
            for m in range(3):
                for k in range(CK):
                    last = mm(pa[:, m, k * NB:(k + 1) * NB], awT[:, m, k * P:(k + 1) * P], condT,
                              start=True, stop=True)
            last.then_inc(S("style_mm"), 1)
            pe.wait_ge(S("squares"), 4)
            for m in range(3):
                for o in range(CK):
                    for k in range(CK):
                        last = mm(pa[:, m, C + o * NB:C + (o + 1) * NB],
                                  w2[:, m, k, o * P:(o + 1) * P], s2[:, m, k, :],
                                  start=(k == 0), stop=(k == CK - 1))
            last.then_inc(S("demod_mm"), 1)
            pe.wait_ge(S("nullk_unit"), 1)
            nc.tensor.transpose(pb[:, 0:NR], qn[0:NR, 3 * P:4 * P], ident[0:NR, 0:NR])
            nc.tensor.transpose(pb[:, NR:2 * NR], qn[0:NR, P:2 * P], ident[0:NR, 0:NR])\
                .then_inc(S("null_T"), 1)
            pe.wait_ge(S("nvbd_done"), 2 * HP)
            for r in range(HP):
                last = mm(pb[0:H * NN, C:2 * C], nvbd[:, r, :], wout[:, r, :],
                          start=(r == 0), stop=(r == HP - 1))
            last.then_inc(S("nullw_mm"), 1)
            pe.wait_ge(S("setup_act"), 1)
            pe.wait_ge(S("setup_dve"), 1)
            pe.wait_ge(S("setup_pool"), 1)

            def linear_T(dst, w, src):
                for o in range(CK):
                    for k in range(CK):
                        last = mm(dst[:, o, :], w[:, k, o * P:(o + 1) * P],
                                  src[:, k, :, :].rearrange("p b l -> p (b l)"),
                                  start=(k == 0), stop=(k == CK - 1))
                return last

            def to_T(dst, src):
                for k in range(CK):
                    last = nc.tensor.transpose(dst[:, k, :], src[:, k * P:(k + 1) * P], ident[:, :])
                return last

            def from_T(dst, src):
                for k in range(CK):
                    last = nc.tensor.transpose(dst[:, k, :], src[:, k, :], ident[:, :])
                return last

            def project(b0, lhs, w):
                for n in range(2):
                    for k in range(CK):
                        last = mm(pa[:, b0 + n, :], lhs[:, k, :], w[:, k, n * 512:(n + 1) * 512],
                                  start=(k == 0), stop=(k == CK - 1))
                return last

            yTf = yT[:, :, :, :].rearrange("p k b l -> p k (b l)")

            def step(i, p, a, b, c, d, more):
                tb, tc, td = i - 1, i - 2, i - 3
                if a:
                    wait_dma(pe, "x_in", i, p)
                    to_T(two(pa[:, 0, :], 0), xin[:, p, :]).then_inc(S("xT"), 1)
                if c:
                    wait_dma(pe, "v2_in", tc, p)
                    wait_before(pe, "av_done", tc)
                    for q in range(QG):
                        last = nc.tensor.transpose(
                            pc[:, 0, q * P:(q + 1) * P],
                            v2[:, p, q * QG:(q + 1) * QG, :].rearrange("p g d -> p (g d)"), ident[:, :])
                    last.then_inc(S("mix_kT"), 1)
                if a:
                    wait(pe, "xm_done", i)
                    linear_T(two(pa[:, 1, :], 0), wc, xm).then_inc(S("yT_mm"), 1)

                def gram(half):
                    for r in range(2):
                        g4 = 2 * half + r
                        mm(pc[:, r, :], identb[:, :], offmask[:, :, :].rearrange("p a b -> p (a b)"),
                           start=True, stop=False, skip_group_check=True)
                        for q in range(QG):
                            z = kT[g4 * DP:g4 * DP + DM, q, :]
                            last = mm(pc[:, r, q * P:(q + 1) * P], z, z, start=False, stop=(q == QG - 1),
                                      skip_group_check=True)
                    return last

                if c:
                    wait(pe, "kT_done", tc)
                    gram(0).then_inc(S("gram0"), 1)
                if a:
                    wait(pe, "yT_done", i)
                    from_T(two(pa[:, 0, :], 0), yTf).then_inc(S("y_nat"), 1)
                    project(2, yTf, wk).then_inc(S("k_mm"), 1)
                if b:
                    wait(pe, "x1_done", tb)
                    wait_before(pe, "kxn_done", tb)
                    to_T(two(pb, 0), x1[:, 1 - p, :]).then_inc(S("x1T"), 1)
                if a:
                    wait(pe, "xn_done", i)
                    to_T(two(pa[:, 1, :], 0), xn).then_inc(S("xnT_mm"), 1)
                if c:
                    wait(pe, "e0_done", tc)
                    gram(1).then_inc(S("gram1"), 1)
                if a:
                    wait(pe, "xnT_done", i)
                    project(0, xnT, wq).then_inc(S("q_mm"), 1)
                if b:
                    wait(pe, "xm2_done", tb)
                    linear_T(two(pb, C), wk2, xm2).then_inc(S("kxT_mm"), 1)

                def e_T(half):
                    for r in range(2):
                        for q in range(QG):
                            last = nc.tensor.transpose(pc[:, r, q * P:(q + 1) * P],
                                                       E[:, 2 * half + r, q, :], ident[:, :])
                    return last

                if c:
                    wait(pe, "e1_done", tc)
                    wait(pe, "exp0", tc)
                    e_T(0).then_inc(S("eT0"), 1)
                if a:
                    wait(pe, "kn_done", i)
                    for r in range(HP):
                        last = nc.tensor.transpose(pa[:, 2 + r // 4, (r % 4) * P:(r % 4 + 1) * P],
                                                   kn[:, r * P:(r + 1) * P], ident[:, :])
                    last.then_inc(S("kT_mm"), 1)
                    wait(pe, "kbd_done", i)
                    wv4 = wv[:, :, :].rearrange("p k (r e d) -> p k r e d", r=HP, e=2)
                    for e in range(2):
                        for k in range(CK):
                            lhs = (yTs if e else yT)[:, k, :, :].rearrange("p b l -> p (b l)")
                            last = mm(pa[:, 2 + e, :], lhs, wv4[:, k, :, e, :],
                                      start=(k == 0), stop=(k == CK - 1))
                    last.then_inc(S("v_mm"), 1)
                if c:
                    wait(pe, "et0_done", tc)
                    wait(pe, "exp1", tc)
                    e_T(1).then_inc(S("eT1"), 1)
                if a:
                    wait(pe, "qn_done", i)
                    for r in range(HP):
                        last = nc.tensor.transpose(pa[:, r // 4, (r % 4) * P:(r % 4 + 1) * P],
                                                   qn[:, r * P:(r + 1) * P], ident[:, :])
                    last.then_inc(S("qT_mm"), 1)
                if b:
                    wait(pe, "kxT_done", tb)
                    from_T(two(pb, 0), kxT).then_inc(S("kxn_mm"), 1)
                if c:
                    wait(pe, "et1_done", tc)
                    for q in range(QG):
                        for g4 in range(QG):
                            last = mm(pc[g4 * DP:(g4 + 1) * DP, 0, q * P:(q + 1) * P],
                                      v2[:, p, q * QG + g4, :], ET[:, g4, q, :], start=True, stop=True,
                                      skip_group_check=True)
                    last.then_inc(S("av_mm"), 1)
                if a:
                    wait(pe, "qT_done", i)
                    wait(pe, "vbd_done", i)
                    for s in range(BT):
                        for r in range(HP):
                            last = mm(pa[s * L:(s + 1) * L, r // 3, (r % 3) * 2 * J:(r % 3 + 1) * 2 * J],
                                      qT[:, r, s * L:(s + 1) * L],
                                      kbd[:, s, r, :],
                                      start=True, stop=True, skip_group_check=True)
                    last.then_inc(S("sim_mm"), 1)
                if d:
                    wait(pe, "on2_in", td, 16)
                    wait_before(pe, "scores_done", td)
                    wait_before(pe, "zn_done", td)
                    to_T(two(pd, 0), on2).then_inc(S("omT"), 1)
                if c:
                    wait(pe, "av_done", tc)
                    for q in range(QG):
                        last = nc.tensor.transpose(pc[:, 1, q * P:(q + 1) * P], av[:, q, :], ident[:, :])
                    last.then_inc(S("av_nat"), 1)
                if a:
                    wait(pe, "probs", i)
                    for r in range(HP):
                        last = nc.tensor.transpose(pa[:, r // 4, (r % 4) * P:(r % 4 + 1) * P],
                                                   pr[:, r, 0:P], ident[:, :])
                    last.then_inc(S("pT_mm"), 1)
                if d:
                    wait(pe, "om_done", td)
                    linear_T(two(pd, C), wo2, om).then_inc(S("zT_mm"), 1)
                if a:
                    wait(pe, "pT_done", i)
                    for s in range(BT):
                        for r in range(HP):
                            last = mm(pa[s * L:(s + 1) * L, 1 + r // 3, (r % 3) * 2 * V1:(r % 3 + 1) * 2 * V1],
                                      pT[:, r, s * L:(s + 1) * L],
                                      vbd[:, s, r, :, :].rearrange("p e v -> p (e v)"),
                                      start=True, stop=True, skip_group_check=True)
                    last.then_inc(S("pv_mm"), 1)
                if d:
                    wait(pe, "zT_done", td)
                    from_T(two(pd, 0), zT).then_inc(S("zn_mm"), 1)
                    for k in range(CK):
                        last = mm(pd[:, C:C + NS + CH], zT[:, k, :], wsc[:, k, :],
                                  start=(k == 0), stop=(k == CK - 1), skip_group_check=True)
                    last.then_inc(S("score_mm"), 1)
                if a:
                    wait(pe, "on_done", i)
                    for r in range(HP):
                        nc.tensor.transpose(pa[:, r // 4, (r % 4) * P:(r % 4 + 1) * P],
                                            on[:, r * P:(r + 1) * P], ident[:, :])
                    wait(pe, "pn_done", i)
                    nc.tensor.transpose(pa[0:H * NN, 2, 0:P], pn[:, :, :].rearrange("p h n -> p (h n)"),
                                        ident[:, :]).then_inc(S("oT_mm"), 1)
                    wait(pe, "oT_done", i)
                    for r in range(HP):
                        mm(pa[:, 3, 0:C], oT[:, r, :], wout[:, r, :], start=(r == 0), stop=False)
                    mm(pa[:, 3, 0:C], pnT[:, :], nullw[:, :], start=False, stop=True)\
                        .then_inc(S("out_mm"), 1)

            pipeline(pe, step)
            final_pe(pe)

        @block.scalar
        def _(act):
            fn = nc.scalar.activation
            act.wait_ge(S("weights"), 16 * LOADS)
            act.wait_ge(S("style_mm"), 1)
            for m, col in enumerate((AB0, AB1, AB2)):
                for k in range(CK):
                    last = fn(sty[:, m, k, :], pa[:, m, k * NB:(k + 1) * NB], ACT.Identity,
                              bias=cols[:, col, k:k + 1], scale=(float(P) ** -0.5 if m == 0 else 1.0))
            last.then_inc(S("styles"), 1)
            act.wait_ge(S("styles"), 1)
            fn(s2, sty[:, :, :, :], ACT.Square).then_inc(S("squares"), 1)
            for m, w in enumerate((wc, wk2, wo2)):
                fn(w2[:, m, :, :], w[:, :, :], ACT.Square).then_inc(S("squares"), 1)
            act.wait_ge(S("demod_in"), 1)
            fn(drt, dsq, ACT.Sqrt).then_inc(S("demod_sqrt"), 1)
            act.wait_ge(S("nullw_mm"), 1)
            fn(nullw[:, :], pb[0:H * NN, C:2 * C], ACT.Copy).then_inc(S("setup_act"), 1)

            def step(i, p, a, b, c, d, more):
                tb, tc, td = i - 1, i - 2, i - 3
                if c:
                    wait(act, "mix_kT", tc)
                    fn(kT[:, :, :].rearrange("p a b -> p (a b)"), pc[:, 0, :], ACT.Copy)\
                        .then_inc(S("kT_done"), 1)
                    wait(act, "e0_done", tc)
                    fn(E[:, 0:2, :, :], E[:, 0:2, :, :], ACT.Exp, scale=DM ** -0.5).then_inc(S("exp0"), 1)
                if a:
                    wait(act, "k_mm", i)
                    wait_before(act, "q_norm", i)
                    fn(sq[:, :].rearrange("p (b n) -> p b n", b=2), pa[:, 2:4, :], ACT.Square)\
                        .then_inc(S("k_sq"), 1)
                    wait(act, "xnT_mm", i)
                    for k in range(CK):
                        last = fn(xnT[:, k, :], pa[:, 1, k * P:(k + 1) * P], ACT.Identity,
                                  bias=cols[:, NBI, k:k + 1], scale=cols[:, NG, k:k + 1])
                    last.then_inc(S("xnT_done"), 1)
                if c:
                    wait(act, "e1_done", tc)
                    fn(E[:, 2:4, :, :], E[:, 2:4, :, :], ACT.Exp, scale=DM ** -0.5).then_inc(S("exp1"), 1)
                if a:
                    wait(act, "q_mm", i)
                    wait(act, "k_norm", i)
                    fn(sq[:, :].rearrange("p (b n) -> p b n", b=2), pa[:, 0:2, :], ACT.Square)\
                        .then_inc(S("q_sq"), 1)
                if c:
                    wait(act, "eT0", tc)
                    fn(ET[:, 0:2, :, :].rearrange("p a b c -> p a (b c)"), pc[:, :, :], ACT.Copy)\
                        .then_inc(S("et0_done"), 1)
                if a:
                    wait(act, "kT_mm", i)
                    for e in range(2):
                        rows = slice(e * DH, (e + 1) * DH)
                        for s in range(BT):
                            slot = e ^ s
                            last = fn(kbd[rows, s, :, slot * L:(slot + 1) * L],
                                      pa[rows, 2:4, :].rearrange("p b (r s l) -> p (b r) s l", s=BT, l=L)[:, :, s, :],
                                      ACT.Identity, bias=0.0, scale=qks[rows, 1:2])
                    last.then_inc(S("kbd_done"), 1)
                    wait(act, "v_mm", i)
                    pv = pa[:, 2:4, :].rearrange("p e (r d) -> p e r d", d=DH)
                    for s in range(BT):
                        for e in range(2):
                            half = s ^ e
                            rows = slice(half * L, (half + 1) * L)
                            last = fn(vbd[rows, s, :, e, 0:DH], pv[rows, e, :, :], ACT.Copy)
                    last.then_inc(S("vbd_done"), 1)
                    wait(act, "qT_mm", i)
                    fn(qT[:, :, :].rearrange("p (b r) t -> p b (r t)", b=2), pa[:, 0:2, :], ACT.Identity,
                       bias=0.0, scale=qks[:, 0:1]).then_inc(S("qT_done"), 1)
                if b:
                    wait(act, "kxn_mm", tb)
                    wait_before(act, "kx_out", tb, 1, 16)
                    fn(kxn[:, :], pb[:, 0:C], ACT.Copy).then_inc(S("kxn_done"), 1)
                if a:
                    wait(act, "pr_sub", i)
                    fn(pr[:, :, :], pr[:, :, :], ACT.Exp).then_inc(S("probs"), 1)
                    wait(act, "pT_mm", i)
                    fn(pT[:, :, :].rearrange("p (b r) t -> p b (r t)", b=2), pa[:, 0:2, :], ACT.Copy)\
                        .then_inc(S("pT_done"), 1)
                if d:
                    wait(act, "zn_mm", td)
                    wait(act, "score_mm", td)
                    wait_before(act, "xf_out", td, 1, 16)
                    fn(zn[:, :], pd[:, 0:C], ACT.Copy).then_inc(S("zn_done"), 1)
                if a:
                    wait(act, "oT_mm", i)
                    fn(oT[:, :, :].rearrange("p (b r) t -> p b (r t)", b=2), pa[:, 0:2, :], ACT.Copy)
                    fn(pnT[:, :], pa[0:H * NN, 2, 0:P], ACT.Copy).then_inc(S("oT_done"), 1)

            pipeline(act, step)
            final_act(act)

        @block.vector
        def _(dve):
            v = nc.vector
            chain = [0]

            def link(ins):
                chain[0] += 1
                ins.then_inc(S("vector_chain"), 1)
                dve.wait_ge(S("vector_chain"), chain[0])

            for s in range(BT):
                v.memset(kbd[:, s, :, :], 0.0)
            v.memset(vbd[:, :, :, :, :], 0.0)
            v.memset(nvbd, 0.0)
            v.memset(oh[:, :, :], 0.0)
            v.memset(mhalf[:, :], -0.5)
            v.memset(eps[:, :], LN_EPS)
            v.memset(v2[:, :, :, :], 0.0).then_inc(S("zeros"), 1)
            dve.wait_ge(S("zeros"), 1)
            v.memset(v2[:, :, :, DM:DM + 1], 1.0)
            for s in range(BT):
                for e in range(2):
                    rows = slice((s ^ e) * L, (s ^ e) * L + L)
                    last = v.memset(vbd[rows, s, :, e, DH:V1], 1.0)
            last.then_inc(S("ones"), 1)
            dve.wait_ge(S("weights"), 16 * LOADS)
            v.tensor_copy(identb[:, :], ident[:, :])
            v.tensor_scalar(sg1, sig, 0.3, None, ALU.is_gt)
            link(v.tensor_scalar(sg2, sig, -0.3, None, ALU.is_lt))
            link(v.tensor_tensor(sg1, sg1, sg2, ALU.subtract))
            link(v.tensor_tensor(sg2, sg1, sig, ALU.subtract))
            link(v.tensor_tensor(wsc[:, :, NC:NS], sig, sg2, ALU.add))
            members = wsc[:, :, NC:NS].rearrange("p k (c t) -> p k c t", t=TPC)
            link(v.tensor_tensor(acc, members[:, :, :, 0], members[:, :, :, 1], ALU.add))
            for t in range(2, TPC):
                link(v.tensor_tensor(acc, acc, members[:, :, :, t], ALU.add))
            v.tensor_scalar(acp, acc, 0.0, None, ALU.is_gt)
            link(v.tensor_scalar(acn, acc, 0.0, None, ALU.is_lt))
            v.tensor_tensor(wsc[:, :, 0:NC], acp, acn, ALU.subtract)
            link(v.tensor_tensor(nks, nk, nk, ALU.mult))
            v.tensor_reduce(nrm[0:NR, 0, 0:2], nks, AX, ALU.add).then_inc(S("nullk_n2"), 1)
            dve.wait_ge(S("nullk_r"), 1)
            v.tensor_tensor(nkh, nk, bc(rn[0:NR, 0, 0:2], 2, DH), ALU.mult).then_inc(S("nullk_unit"), 1)
            dve.wait_ge(S("demod_mm"), 1)
            v.tensor_scalar(dsq, pa[:, 0:3, C:2 * C].rearrange("p m (k n) -> p m k n", k=CK),
                            1e-8, None, ALU.add).then_inc(S("demod_in"), 1)
            dve.wait_ge(S("demod_sqrt"), 1)
            link(v.reciprocal(dem[:, :, :, :], drt))
            link(v.tensor_tensor(dnw, dem[:, :, :, :], dem[:, :, :, :], ALU.mult))
            link(v.tensor_tensor(dnw, dnw, dsq, ALU.mult))
            link(v.tensor_scalar(dnw, dnw, -0.5, 1.5, ALU.mult, ALU.add))
            v.tensor_tensor(dem[:, :, :, :], dem[:, :, :, :], dnw, ALU.mult)
            dve.wait_ge(S("null_T"), 1)
            for e in range(2):
                rows = slice(e * DH, (e + 1) * DH)
                for s in range(BT):
                    v.tensor_scalar(kbd[rows, s, :, P + (e ^ s) * NN:P + (e ^ s) * NN + NN],
                                    pb[rows, 0:NR].rearrange("p (r n) -> p r n", n=NN),
                                    qks[rows, 1:2], None, ALU.mult)
                for r in range(HP):
                    at = (2 * r + e) * NN
                    v.tensor_copy(nvbd[rows, r, at:at + NN], pb[rows, NR + r * NN:NR + (r + 1) * NN])\
                        .then_inc(S("nvbd_done"), 1)
            v.tensor_scalar(qks[:, 0:1], qks[:, 0:1], 8.0, None, ALU.mult).then_inc(S("setup_dve"), 1)
            dve.wait_ge(S("setup_dve"), 1)

            def modulate(dst, src, table, t):
                return v.tensor_tensor(
                    dst[:, :, :, :], src.rearrange("p k (b l) -> p k b l", b=BT),
                    bc(table[:, :, bass.ds(t * BT, BT)], 3, L), ALU.mult)

            def step(i, p, a, b, c, d, more):
                tb, tc, td = i - 1, i - 2, i - 3
                if a:
                    wait(dve, "xT", i)
                    modulate(xm, two(pa[:, 0, :], 0), sty[:, 0, :, :], i).then_inc(S("xm_done"), 1)
                    wait(dve, "yT_mm", i)
                    modulate(yT, two(pa[:, 1, :], 0), dem[:, 0, :, :], i).then_inc(S("y_dem"), 1)
                    wait(dve, "y_dem", i)
                    for k in range(CK):
                        last = v.tensor_scalar(yT[:, k, :, :], yT[:, k, :, :], cols[:, CB, k:k + 1], CLAMP,
                                               ALU.add, ALU.min)
                    last.then_inc(S("y_min"), 1)
                    wait(dve, "y_min", i)
                    v.tensor_scalar(yTs[:, :, ::-1, :], yT[:, :, :, :], -CLAMP, None, ALU.max)\
                        .then_inc(S("yTs_done"), 1)
                    wait(dve, "yTs_done", i)
                    v.tensor_scalar(yT[:, :, :, :], yT[:, :, :, :], -CLAMP, None, ALU.max)\
                        .then_inc(S("yT_done"), 1)

                def soften(half, done):
                    src = pc[:, :, :].rearrange("p r (q n) -> p r q n", n=P)
                    v.tensor_reduce(mx2[:, 2 * half:2 * half + 2, :], src, AX, ALU.max)\
                        .then_inc(S(f"mix_max{half}"), 1)
                    wait(dve, f"mix_max{half}", tc)
                    v.tensor_tensor(E[:, 2 * half:2 * half + 2, :, :], src,
                                    bc(mx2[:, 2 * half:2 * half + 2, :], 3, P), ALU.subtract)\
                        .then_inc(S(done), 1)

                if c:
                    wait(dve, "gram0", tc)
                    soften(0, "e0_done")
                if a:
                    wait(dve, "y_nat", i)
                    v.bn_stats(st6[:, :], pa[:, 0, 0:C]).then_inc(S("y_st6"), 1)
                    wait(dve, "y_st6", i)
                    v.memset(pad[:, :], 0.0)
                    v.bn_aggr(mv[:, :], st6[:, :]).then_inc(S("y_mv"), 1)
                    wait(dve, "k_sq", i)
                    wait(dve, "y_rstd", i)
                    v.tensor_scalar(xn[:, :], pa[:, 0, 0:C], mv[:, 0:1], rs[:, 0:1],
                                    ALU.subtract, ALU.mult).then_inc(S("xn_done"), 1)
                    v.tensor_reduce(nrm[:, 1, :], sq[:, :].rearrange("p (h d) -> p h d", d=DH), AX, ALU.add)\
                        .then_inc(S("k_norm"), 1)
                    wait(dve, "k_norm", i)
                    v.tensor_scalar(nrg[:, 1, :], nrm[:, 1, :], 1e-24, None, ALU.max)\
                        .then_inc(S("k_guard"), 1)
                if b:
                    wait(dve, "x1T", tb)
                    modulate(xm2, two(pb, 0), sty[:, 1, :, :], tb).then_inc(S("xm2_done"), 1)
                if c:
                    wait(dve, "gram1", tc)
                    soften(1, "e1_done")
                if a:
                    wait(dve, "q_sq", i)
                    v.tensor_reduce(nrm[:, 0, :], sq[:, :].rearrange("p (h d) -> p h d", d=DH), AX, ALU.add)\
                        .then_inc(S("q_norm"), 1)
                    wait(dve, "q_norm", i)
                    v.tensor_scalar(nrg[:, 0, :], nrm[:, 0, :], 1e-24, None, ALU.max)\
                        .then_inc(S("q_guard"), 1)
                    wait(dve, "k_rsqrt", i)
                    v.tensor_tensor(kn[:, :].rearrange("p (b h d) -> p b h d", b=2, d=DH),
                                    pa[:, 2:4, :].rearrange("p b (h d) -> p b h d", d=DH),
                                    bc(rn[:, 1, :].rearrange("p (b h) -> p b h", b=2), 3, DH), ALU.mult)\
                        .then_inc(S("kn_done"), 1)
                if b:
                    wait(dve, "kxT_mm", tb)
                    modulate(kxd_, two(pb, C), dem[:, 1, :, :], tb).then_inc(S("kx_dem"), 1)
                    wait(dve, "kx_dem", tb)
                    v.tensor_tensor(kxT[:, :, :], kxd_[:, :, :, :].rearrange("p k b l -> p k (b l)"),
                                    bc(cols[:, KB, :], 2, P), ALU.add).then_inc(S("kxT_done"), 1)
                if a:
                    wait(dve, "q_rsqrt", i)
                    v.tensor_tensor(qn[:, :].rearrange("p (b h d) -> p b h d", b=2, d=DH),
                                    pa[:, 0:2, :].rearrange("p b (h d) -> p b h d", d=DH),
                                    bc(rn[:, 0, :].rearrange("p (b h) -> p b h", b=2), 3, DH), ALU.mult)\
                        .then_inc(S("qn_done"), 1)
                if c:
                    wait(dve, "eT1", tc)
                    v.tensor_copy(ET[:, 2:4, :, :].rearrange("p a b c -> p a (b c)"), pc[:, :, :])\
                        .then_inc(S("et1_done"), 1)
                    wait(dve, "av_mm", tc)
                    v.tensor_copy(av[:, :, :].rearrange("p a b -> p (a b)"), pc[:, 0, :])\
                        .then_inc(S("av_done"), 1)
                if a:
                    wait(dve, "sim_mm", i)
                    v.tensor_tensor(pr[:, 0:6, :].rearrange("p (b r) j -> p b (r j)", b=2),
                                    pa[:, 0:2, 0:3 * PJ],
                                    alibi[:, 0:6, :].rearrange("p (b r) j -> p b (r j)", b=2), ALU.add)
                    v.tensor_tensor(pr[:, 6:8, :].rearrange("p r j -> p (r j)"), pa[:, 2, 0:2 * PJ],
                                    alibi[:, 6:8, :].rearrange("p r j -> p (r j)"), ALU.add)\
                        .then_inc(S("pr_add"), 1)
                    wait(dve, "pr_add", i)
                    keys = pr[:, :, 0:P].rearrange("p r (e j) -> p r e j", e=2)
                    nulls = pr[:, :, P:PJ].rearrange("p r (e n) -> p r e n", e=2)
                    by_pair = lambda z: z[:, :].rearrange("p (r e) -> p r e", e=2)
                    v.tensor_reduce(by_pair(mxm), keys, AX, ALU.max)
                    v.tensor_reduce(by_pair(mxn), nulls, AX, ALU.max).then_inc(S("pr_maxes"), 1)
                    wait(dve, "pr_maxes", i)
                    v.tensor_tensor(mx[:, :], mxm[:, :], mxn[:, :], ALU.max).then_inc(S("pr_max"), 1)
                    wait(dve, "pr_max", i)
                    v.tensor_tensor(keys, keys, bc(by_pair(mx), 3, L), ALU.subtract)
                    v.tensor_tensor(nulls, nulls, bc(by_pair(mx), 3, NN), ALU.subtract)\
                        .then_inc(S("pr_sub"), 1)
                if d:
                    wait(dve, "omT", td)
                    modulate(om, two(pd, 0), sty[:, 2, :, :], td).then_inc(S("om_done"), 1)
                if c:
                    wait(dve, "av_nat", tc)
                    wait_before(dve, "o2_out", tc, 1, 16)
                    src = pc[:, 1, :].rearrange("p (g d) -> p g d", d=DP)
                    v.reciprocal(rd2[:, :], src[:, :, DM:DM + 1].rearrange("p g o -> p (g o)"))\
                        .then_inc(S("mix_rden"), 1)
                    wait(dve, "mix_rden", tc)
                    v.tensor_tensor(o2[:, :, :], src[:, :, 0:DM], bc(rd2[:, :], 2, DM), ALU.mult)\
                        .then_inc(S("o2_done"), 1)
                if d:
                    wait(dve, "zT_mm", td)
                    modulate(zd, two(pd, C), dem[:, 2, :, :], td).then_inc(S("z_dem"), 1)
                    wait(dve, "z_dem", td)
                    v.tensor_tensor(zT[:, :, :], zd[:, :, :, :].rearrange("p k b l -> p k (b l)"),
                                    bc(cols[:, OB, :], 2, P), ALU.add).then_inc(S("zT_done"), 1)
                if a:
                    wait(dve, "probs", i)
                    for s in range(BT):
                        rows = slice(s * L, (s + 1) * L)
                        src = pr[rows, :, P:PJ].rearrange("p r (e n) -> p r e n", e=2)
                        last = v.tensor_copy(pnr[rows, :, :].rearrange("p (r e) n -> p r e n", e=2),
                                             src[:, :, ::-1, :] if s else src)
                    last.then_inc(S("null_order"), 1)
                    wait(dve, "null_order", i)
                    v.tensor_reduce(den[:, :], pnr[:, :, :], AX, ALU.add).then_inc(S("null_sum"), 1)
                    wait(dve, "pv_mm", i)
                    wait(dve, "null_sum", i)
                    head = pa[:, 1:3, 0:6 * V1].rearrange("p b (h v) -> p b h v", v=V1)
                    tail = pa[:, 3, 0:4 * V1].rearrange("p (h v) -> p h v", v=V1)
                    v.tensor_tensor(den2[:, 0:12].rearrange("p (b h) -> p b h", b=2), head[:, :, :, DH],
                                    den[:, 0:12].rearrange("p (b h) -> p b h", b=2), ALU.add)
                    v.tensor_tensor(den2[:, 12:16], tail[:, :, DH], den[:, 12:16], ALU.add)\
                        .then_inc(S("den_done"), 1)
                    wait(dve, "den_done", i)
                    v.reciprocal(rden[:, :], den2[:, :]).then_inc(S("rden_done"), 1)
                    wait(dve, "rden_done", i)
                    v.tensor_tensor(on[:, 0:12 * DH].rearrange("p (b h d) -> p b h d", b=2, d=DH),
                                    head[:, :, :, 0:DH],
                                    bc(rden[:, 0:12].rearrange("p (b h) -> p b h", b=2), 3, DH), ALU.mult)
                    v.tensor_tensor(on[:, 12 * DH:].rearrange("p (h d) -> p h d", d=DH), tail[:, :, 0:DH],
                                    bc(rden[:, 12:16], 2, DH), ALU.mult).then_inc(S("on_done"), 1)
                    v.tensor_tensor(pn[:, :, :], pnr[:, :, :], bc(rden[:, :], 2, NN), ALU.mult)\
                        .then_inc(S("pn_done"), 1)
                if d:
                    wait(dve, "zn_done", td)
                    v.tensor_copy(SC[:, bass.ds(td, 1), :].rearrange("p o n -> p (o n)"), pd[:, C:C + NS])
                    v.tensor_copy(HPR[:, bass.ds(td, 1), :].rearrange("p o n -> p (o n)"),
                                  pd[:, C + NS:C + NS + CH]).then_inc(S("scores_done"), 1)
                if a:
                    wait(dve, "out_mm", i)
                    wait_dma_before(dve, "x1_out", i, p)
                    v.tensor_tensor(x1[:, p, :], pa[:, 3, 0:C], xin[:, p, :], ALU.add)\
                        .then_inc(S("x1_done"), 1)

            pipeline(dve, step)
            final_dve(dve, link)

        @block.gpsimd
        def _(pool):
            g = nc.gpsimd
            pool.wait_ge(S("zeros"), 1)
            pool.wait_ge(S("ones"), 1)
            pool.wait_ge(S("nullk_n2"), 1)
            g.tensor_scalar(nrg[0:NR, 0, 0:2], nrm[0:NR, 0, 0:2], 1e-24, None, ALU.max).then_inc(S("nullk_g"), 1)
            pool.wait_ge(S("nullk_g"), 1)
            g.tensor_tensor(rn[0:NR, 0, 0:2], nrg[0:NR, 0, 0:2], mhalf[0:NR, 0:2], ALU.pow)\
                .then_inc(S("nullk_r"), 1)
            pool.wait_ge(S("nullk_unit"), 1)
            g.memset(ve[:, :], 0.0).then_inc(S("setup_pool"), 1)
            pool.wait_ge(S("setup_pool"), 1)

            def step(i, p, a, b, c, d, more):
                if a:
                    wait(pool, "y_mv", i)
                    g.tensor_tensor(ve[:, :], mv[:, 1:2], eps[:, :], ALU.add).then_inc(S("y_var"), 1)
                    wait(pool, "y_var", i)
                    g.tensor_tensor(rs[:, :], ve[:, :], mhalf[:, 0:1], ALU.pow).then_inc(S("y_rstd"), 1)
                    for n, name in ((1, "k"), (0, "q")):
                        wait(pool, name + "_guard", i)
                        g.tensor_tensor(rn[:, n, :], nrg[:, n, :], mhalf[:, :], ALU.pow)\
                            .then_inc(S(name + "_rsqrt"), 1)

            pipeline(pool, step)
            final_pool(pool)


_OUT = ((128, 64, 256), "float32")


def kernel(**inputs):
    import numpy as np
    import concourse.bacc as bacc
    from concourse import mybir as mb
    from concourse.bass_utils import run_bass_kernel_spmd as run

    a = {k: np.asarray(v) for k, v in inputs.items()}
    ar = {"x": a["x"], "condT": a["cond_512"].T}
    for n in ("L0_cond_affine_w", "L0_cond2_k_aff_w", "L0_cond2_o_aff_w", "L0_cond_weight", "L0_cond2_k_w",
              "L0_cond2_o_w"):
        ar[n + "T"] = a[n].T
    for n in ("L0_cond_bias", "L0_attn_norm_g", "L0_attn_norm_b", "L0_cond2_k_b", "L0_cond2_o_b",
              "L0_cond_affine_b", "L0_cond2_k_aff_b", "L0_cond2_o_aff_b"):
        ar[n + "_c"] = a[n].reshape(2, 128).T
    ar["qk_scale"] = np.stack([np.tile(a["L0_attn_q_scale"], 2), np.tile(a["L0_attn_k_scale"], 2)], axis=1)
    ar["sigT"] = a["L0_ffn_signatures_raw"].T
    null = a["L0_attn_null_kv"].reshape(8, 2, 2, 2, 64).transpose(3, 0, 2, 1, 4)
    ar["null_k"], ar["null_v"] = null[0].reshape(16, 2, 64), null[1].reshape(16, 2, 64)
    ar["L0_attn_Wq"] = a["L0_attn_Wq"]
    ar["Wk"], ar["Wv"] = a["L0_attn_Wkv"][:, :1024], a["L0_attn_Wkv"][:, 1024:]
    ar["L0_attn_Wout"] = a["L0_attn_Wout"]
    ar["L0_ffn_compress_w1"] = a["L0_ffn_compress_w1"]
    ar["ident"] = np.eye(128, dtype=np.float32)
    start = 2.0 ** (-2.0 ** (-(np.log2(16) - 3)))
    slopes = np.array([start * start ** i for i in range(16)], dtype=np.float32)
    row = np.arange(64)
    pos = np.concatenate([np.arange(64) + 2, np.arange(2)])
    dist = -np.abs(pos[None, :] - (row[:, None] + 2)).astype(np.float32)
    table = slopes[None, :, None] * dist[:, None, :]
    seen = pos[None, :] <= row[:, None] + 2
    table = np.where(seen[:, None, :], table, np.float32(-3.0e38)).astype(np.float32)
    table = table.reshape(64, 8, 2, 66)
    ar["alibi"] = np.concatenate([np.concatenate([z[:, :, :, :64].reshape(64, 8, 128), z[:, :, :, 64:].reshape(64, 8, 4)],
                                                 axis=2) for z in (table, table[:, :, ::-1])])
    import ml_dtypes
    own = np.arange(128)[:, None] // 16 == np.arange(128)[None, :] // 16
    ar["offmask"] = np.repeat(np.where(own, 0.0, -1e30).astype(ml_dtypes.bfloat16)[:, None, :], 4, axis=1)
    row_of = np.concatenate([a["L0_ffn_compress_w2"].T.reshape(-1), a["L0_ffn_compress_b1"],
                             a["L0_ffn_compress_b2"], a["L0_ffn_knot_values"],
                             np.arange(8, dtype=np.float32) - 8, a["L0_ffn_temperature"],
                             a["L0_ffn_output_scale"]])
    ar["coef"] = np.repeat(row_of[None, :], 128, axis=0)
    ar["gb"] = np.repeat(np.stack([a["L0_ffn_norm_gamma"], a["L0_ffn_norm_beta"]])[None], 128, axis=0)
    ar["gath"] = np.concatenate([a["L0_ffn_spline_w1"].reshape(64, 32), a["L0_ffn_spline_b1"],
                                 a["L0_ffn_spline_w2"].reshape(64, 16), a["L0_ffn_spline_b2"],
                                 a["L0_ffn_directions"]], axis=1)

    nc = bacc.Bacc("TRN2", target_bir_lowering=False, num_devices=1)
    arrays, aps = {}, {}
    for name, v in ar.items():
        v = np.ascontiguousarray(v)
        arrays[f"in_{name}"] = v
        aps[name] = nc.dram_tensor(f"in_{name}", v.shape, mb.dt.from_np(v.dtype), kind="ExternalInput").ap()
    out = nc.dram_tensor("out_0", _OUT[0], mb.dt.from_np(np.dtype(_OUT[1])), kind="ExternalOutput").ap()
    adaln_attention_ffn(nc, aps, out)
    r = run(nc, [arrays], core_ids=[0])
    return r.results[0]["out_0"]
```

```python
import concourse.bass as bass
from concourse import mybir
from contextlib import ExitStack


def adaln_attention_ffn(nc: bass.Bass, A: dict, out: bass.AP):
    f32, bf16 = mybir.dt.float32, mybir.dt.bfloat16
    ALU, ACT, AX = mybir.AluOpType, mybir.ActivationFunctionType, mybir.AxisListType.X

    NB, L, C = A["x"].shape
    P = 128
    BT = P // L
    T = NB * L // P
    CK = C // P
    H, DH = 16, 64
    HP = H // 2
    NN = 2
    J = L + NN
    PJ = 2 * J
    V1 = DH + 1
    INNER = H * DH
    DM = C // H
    TG = P // H
    G = P // TG
    QG = 4
    DP = 32
    NT, NC = 64, 8
    TPC = NT // NC
    KN = 8
    GRID = 16
    CH = 64
    NS = NC + NT
    GATH = 2 * GRID + GRID + GRID + 1 + C
    CLAMP = 256.0
    LN_EPS = 1e-5

    ctx = ExitStack()
    with ctx:
        def sb(name, shape, dt=f32):
            return ctx.enter_context(nc.sbuf_tensor(name, shape, dt))

        sems = {}

        def S(name):
            if name not in sems:
                sems[name] = ctx.enter_context(nc.semaphore(name))
            return sems[name]

        def wait(eng, name, t, by=1):
            eng.wait_ge(S(name), (t + 1) * by)

        def wait_part(eng, name, t, k, of):
            eng.wait_ge(S(name), t * of + k)

        def wait_before(eng, name, t, back=1, by=1):
            if isinstance(t, int) and t < back:
                return
            eng.wait_ge(S(name), (t + 1 - back) * by)

        def wait_dma(eng, name, t, p):
            eng.wait_ge(S(name + "_even" * (not p) + "_odd" * p), (t - p) * 8 + 16)

        def wait_dma_before(eng, name, t, p):
            if isinstance(t, int) and t < 2:
                return
            eng.wait_ge(S(name + "_even" * (not p) + "_odd" * p), (t - p) * 8)

        def D(name, p):
            return S(name + "_even" * (not p) + "_odd" * p)

        ident = sb("ident", [P, P])
        identb = sb("identb", [P, P], bf16)
        offmask = sb("offmask", [P, QG, P], bf16)
        alibi = sb("alibi", [P, HP, PJ])
        wc = sb("wc", [P, CK, C])
        wk2 = sb("wk2", [P, CK, C])
        wo2 = sb("wo2", [P, CK, C])
        wq = sb("wq", [P, CK, INNER])
        wk = sb("wk", [P, CK, INNER])
        wv = sb("wv", [P, CK, INNER])
        wout = sb("wout", [P, HP, C])
        wsc = sb("wsc", [P, CK, NS + CH])
        sty = sb("sty", [P, 3, CK, NB])
        dem = sb("dem", [P, 3, CK, NB])
        cols = sb("cols", [P, 8, CK])
        CB, NG, NBI, KB, OB, AB0, AB1, AB2 = range(8)
        qks = sb("qks", [P, 2])
        nullw = sb("nullw", [H * NN, C])

        xin = sb("xin", [P, 2, C])
        xm = sb("xm", [P, CK, BT, L])
        yT = sb("yT", [P, CK, BT, L])
        xn = sb("xn", [P, C])
        xnT = sb("xnT", [P, CK, P])
        sq = sb("sq", [P, INNER])
        kn = sb("kn", [P, INNER])
        qn = sb("qn", [P, INNER])
        qT = sb("qT", [P, HP, P])
        kbd = sb("kbd", [P, BT, HP, PJ])
        vbd = sb("vbd", [P, 2, BT, HP, 2, V1])
        pr = sb("pr", [P, HP, PJ])
        pT = sb("pT", [P, HP, P])
        on = sb("on", [P, INNER])
        yTs = sb("yTs", [P, CK, BT, L])
        pnr = sb("pnr", [P, H, NN])
        mxn = sb("mxn", [P, H])
        mxm = sb("mxm", [P, H])
        oT = sb("oT", [P, HP, P])
        pn = sb("pn", [P, H, NN])
        pnT = sb("pnT", [H * NN, P])
        st6 = sb("st6", [P, 6])
        mv = sb("mv", [P, 2])
        ve = sb("ve", [P, 1])
        rs = sb("rs", [P, 1])
        nrm = sb("nrm", [P, 2, H])
        nrg = sb("nrg", [P, 2, H])
        rn = sb("rn", [P, 2, H])
        mhalf = sb("mhalf", [P, H])
        eps = sb("eps", [P, 1])
        pad = sb("pad", [P, 1])
        mx = sb("mx", [P, H])
        den = sb("den", [P, H])
        den2 = sb("den2", [P, H])
        rden = sb("rden", [P, H])
        x1 = sb("x1", [P, 2, C])
        xm2 = sb("xm2", [P, CK, BT, L])
        kxd_ = sb("kxd_", [P, CK, BT, L])
        kxT = sb("kxT", [P, CK, P])
        kxn = sb("kxn", [P, C])
        v2 = sb("v2", [P, 2, G, DP])
        kT = sb("kT", [P, QG, P])
        E = sb("E", [P, QG, QG, P])
        ET = sb("ET", [P, QG, QG, P])
        mx2 = sb("mx2", [P, QG, QG])
        av = sb("av", [P, QG, P])
        rd2 = sb("rd2", [P, G])
        o2 = sb("o2", [P, G, DM])
        on2 = sb("on2", [P, C])
        om = sb("om", [P, CK, BT, L])
        zd = sb("zd", [P, CK, BT, L])
        zT = sb("zT", [P, CK, P])
        zn = sb("zn", [P, C])
        SC = sb("SC", [P, T, NS])
        HPR = sb("HPR", [P, T, CH])

        pa = ctx.enter_context(nc.psum_tensor("pa", [P, 3, 512], f32))
        ps = ctx.enter_context(nc.psum_tensor("ps", [P, 3, 512], f32))
        pc = ctx.enter_context(nc.psum_tensor("pc", [P, 512], f32))
        pb = ctx.enter_context(nc.psum_tensor("pb", [P, 512], f32))

        x1d = nc.dram_tensor("x1d", [T, P, C], f32)
        kxdr = nc.dram_tensor("kxdr", [T, P, C], f32)
        odr = nc.dram_tensor("odr", [T, P, C], f32)
        xfd = nc.dram_tensor("xfd", [T, P, C], f32)
        x_t = A["x"].rearrange("(t b) l c -> t (b l) c", b=BT)
        out_t = out.rearrange("(t b) l c -> t (b l) c", b=BT)

        def mixed(dram, t):
            return dram[bass.ds(t, 1), :, :].rearrange(
                "o (g k) (h d) -> (o k h) g d", k=TG, h=H)

        def plain(dram, t):
            return dram[bass.ds(t, 1), :, :].rearrange("o p c -> (o p) c")

        def bc(ap, axis, n):
            u = ap.unsqueeze(axis)
            shape = list(u.shape)
            shape[axis] = n
            return u.broadcast_to(shape)

        def two(bank, lo):
            return bank[:, lo:lo + C].rearrange("p (k q) -> p k q", k=CK)

        rawT = E[:, :, :, :].rearrange("p a b c -> p (a b c)")
        awT = rawT[:, 0:3 * C].rearrange("p (m c) -> p m c", m=3)
        condT = rawT[:, 3 * C:3 * C + NB]
        w2 = ET[:, :, :, :].rearrange("p a b c -> p (a b c)")[:, 0:3 * CK * C].rearrange(
            "p (m k c) -> p m k c", m=3, k=CK)
        s2 = rawT[:, 1024:1024 + 3 * CK * NB].rearrange("p (m k n) -> p m k n", m=3, k=CK)
        sig = kn[:, 0:CK * NT].rearrange("p (k n) -> p k n", k=CK)
        sg1 = kn[:, 256:256 + CK * NT].rearrange("p (k n) -> p k n", k=CK)
        sg2 = kn[:, 512:512 + CK * NT].rearrange("p (k n) -> p k n", k=CK)
        acc = kn[:, 768:768 + CK * NC].rearrange("p (k n) -> p k n", k=CK)
        acp = kn[:, 800:800 + CK * NC].rearrange("p (k n) -> p k n", k=CK)
        acn = kn[:, 832:832 + CK * NC].rearrange("p (k n) -> p k n", k=CK)
        NR = HP * NN
        nk = qn[0:NR, 0:P].rearrange("r (a d) -> r a d", a=2)
        nv = qn[0:NR, P:2 * P].rearrange("r (a d) -> r a d", a=2)
        nks = qn[0:NR, 2 * P:3 * P].rearrange("r (a d) -> r a d", a=2)
        nkh = qn[0:NR, 3 * P:4 * P].rearrange("r (a d) -> r a d", a=2)
        nvbd = sq[:, 0:HP * H * NN].rearrange("p (r n) -> p r n", r=HP)
        dsq = on[:, 0:3 * CK * NB].rearrange("p (m k n) -> p m k n", m=3, k=CK)
        drt = pT[:, :, :].rearrange("p a b -> p (a b)")[:, 0:3 * CK * NB].rearrange(
            "p (m k n) -> p m k n", m=3, k=CK)
        dnw = oT[:, :, :].rearrange("p a b -> p (a b)")[:, 0:3 * CK * NB].rearrange(
            "p (m k n) -> p m k n", m=3, k=CK)
        linear = ["L0_cond_weight", "L0_cond2_k_w", "L0_cond2_o_w"]
        affine = ["L0_cond_affine_w", "L0_cond2_k_aff_w", "L0_cond2_o_aff_w"]
        LOADS = 30

        def load_all(sp):
            n = [0]

            def ld(dst, src):
                sp.dma_start(dst, src).then_inc(S("weights"), 16)
                n[0] += 1

            ld(condT, A["condT"])
            for m, name in enumerate(affine):
                ld(awT[:, m, :], A[name + "T"])
            for dst, name in zip((wc, wk2, wo2), linear):
                ld(dst[:, :, :], A[name + "T"].rearrange("(k p) n -> p k n", p=P))
            for n_, name in ((CB, "L0_cond_bias"), (NG, "L0_attn_norm_g"), (NBI, "L0_attn_norm_b"),
                             (KB, "L0_cond2_k_b"), (OB, "L0_cond2_o_b"), (AB0, "L0_cond_affine_b"),
                             (AB1, "L0_cond2_k_aff_b"), (AB2, "L0_cond2_o_aff_b")):
                ld(cols[:, n_, :], A[name + "_c"])
            ld(qks[:, :], A["qk_scale"])
            ld(sig, A["sigT"].rearrange("(k p) n -> p k n", p=P))
            ld(nk, A["null_k"])
            ld(nv, A["null_v"])
            ld(alibi[:, :, :], A["alibi"])
            ld(wq[:, :, :], A["L0_attn_Wq"].rearrange("(k p) n -> p k n", p=P))
            ld(wk[:, :, :], A["Wk"].rearrange("(k p) n -> p k n", p=P))
            ld(wv[:, :, :], A["Wv"].rearrange("(k p) n -> p k n", p=P))
            ld(wout[:, :, :], A["L0_attn_Wout"].rearrange("(r p) n -> p r n", p=P))
            ld(wsc[:, :, NS:NS + CH], A["L0_ffn_compress_w1"].rearrange("(k p) n -> p k n", p=P))
            ld(ident[:, :], A["ident"])
            ld(coef[:, :], A["coef"])
            ld(gb[:, :, :], A["gb"])
            ld(gath[:, :], A["gath"])
            ld(offmask[:, :, :], A["offmask"])
            assert n[0] == LOADS, n[0]

        coef = sb("coef", [P, 2 * CH + CH + 2 + KN + NC + 2])
        gb = sb("gb", [P, 2, C])
        gath = sb("gath", [NT, GATH])
        CO = {}
        at = 0
        for name, n in (("w2", 2 * CH), ("b1", CH), ("b2", 2), ("knots", KN), ("iota", NC), ("temp", 1),
                        ("scale", 1)):
            CO[name] = coef[:, at:at + n]
            at += n
        ninv = sb("ninv", [P, 2])
        kdif = sb("kdif", [P, KN])
        clo = sb("clo", [P, T, NC])
        loc = sb("loc", [P, T, NC])
        comp = sb("comp", [P, T, 2])
        best = sb("best", [P, 2, T])
        oh = sb("oh", [P, 2, P])
        ohT = sb("ohT", [NT, 2, P])
        gs = sb("gs", [P, 2, GATH])
        cc = sb("cc", [P, 2, 2])
        hid = sb("hid", [P, 2, 2, GRID])
        junk = sb("junk", [P, 2, GRID])
        mag = sb("mag", [P, 2, 2])
        yy = sb("yy", [P, 2, C])
        ys6 = sb("ys6", [P, 2, 6])
        ymv = sb("ymv", [P, 2, 2])
        yve = sb("yve", [P, 2, 2])
        yn = sb("yn", [P, 2, C])
        res = sb("res", [P, 2, C])

        def tiles8(buf, part):
            return buf[:, part * 512:(part + 1) * 512].rearrange("p (t c) -> p t c", c=NC)

        score, knot_at, frac = tiles8(sq, 0), tiles8(sq, 1), tiles8(qn, 0)
        low, rise, pick = tiles8(qn, 1), tiles8(on, 0), tiles8(on, 1)
        local = tiles8(kn, 0)
        TH = T // 2
        prod = [z[:, :, :, :].rearrange("p a b c -> p (a b c)") for z in (E, ET)]

        def final_loads(sp):
            def back(t, p):
                wait_before(sp, "res_done", t, 2)
                wait_before(sp, "y_sum", t, 2)
                sp.dma_start(xin[:, p, :], plain(x1d, t)).then_inc(D("x1_back", p), 16)
                sp.dma_start(x1[:, p, :], plain(xfd, t)).then_inc(D("xf_back", p), 16)

            def out_(t, p):
                wait(sp, "res_done", t)
                sp.dma_start(plain(out_t, t), res[:, p, :]).then_inc(D("out", p), 16)

            back(0, 0)
            back(1, 1)
            out_(0, 0)
            with sp.Fori(0, (T - 2) // 2) as n:
                t = n * 2 + 2
                back(t, 0)
                out_(t - 1, 1)
                back(t + 1, 1)
                out_(t, 0)
            out_(T - 1, 1)
            for p in range(2):
                sp.wait_ge(D("out", p), T * 8)
            for name in ("kx_out", "o2_out"):
                sp.wait_ge(S(name), T * 16)

        def final_loop(eng, step):
            step(0, 0)
            step(1, 1)
            with eng.Fori(0, (T - 2) // 2) as n:
                t = n * 2 + 2
                step(t, 0)
                step(t + 1, 1)

        def final_pe(pe):
            def step(t, p):
                wait(pe, "oh_done", t)
                wait_before(pe, "ohT_done", t, 1)
                nc.tensor.transpose(pa[:, p, 0:P], oh[:, p, :], ident[:, :]).then_inc(S("ohT_mm"), 1)
                wait(pe, "ohT_done", t)
                wait_before(pe, "gs_done", t, 2)
                nc.tensor.matmul(ps[:, p, 0:GATH], ohT[:, p, :], gath[:, :], start=True, stop=True)\
                    .then_inc(S("gathered"), 1)

            final_loop(pe, step)

        def final_act(act):
            fn = nc.scalar.activation
            act.wait_ge(S("temp_done"), 1)
            act.wait_ge(S("scores_done"), T)
            fn(score, SC[:, :, 0:NC], ACT.Exp, scale=ninv[:, 1:2]).then_inc(S("cluster_exp"), 1)
            act.wait_ge(S("local_score"), 1)
            fn(score, local, ACT.Exp, scale=ninv[:, 1:2]).then_inc(S("local_exp"), 1)
            act.wait_ge(S("pre_bias"), 1)
            fn(HPR[:, :, :], HPR[:, :, :], ACT.Gelu).then_inc(S("gelu_done"), 1)
            act.wait_ge(S("comp_pre"), 1)
            fn(comp[:, :, :], comp[:, :, :], ACT.Tanh).then_inc(S("comp_done"), 1)

            def step(t, p):
                wait(act, "ohT_mm", t)
                wait_before(act, "gathered", t, 2)
                fn(ohT[:, p, :], pa[0:NT, p, 0:P], ACT.Copy).then_inc(S("ohT_done"), 1)
                wait(act, "gathered", t)
                wait_before(act, "y_sum", t, 2)
                fn(gs[:, p, :], ps[:, p, 0:GATH], ACT.Copy).then_inc(S("gs_done"), 1)

            final_loop(act, step)

        def final_dve(dve, link):
            v = nc.vector
            link(v.tensor_scalar(ninv[:, 0:1], CO["temp"], 1e-6, -1.0, ALU.add, ALU.mult))
            v.reciprocal(ninv[:, 1:2], ninv[:, 0:1]).then_inc(S("temp_done"), 1)
            link(v.tensor_tensor(kdif[:, 0:KN - 1], CO["knots"][:, 1:KN], CO["knots"][:, 0:KN - 1],
                                 ALU.subtract))

            def calibrate():
                link(v.tensor_scalar(score, score, 1.0, None, ALU.add))
                link(v.reciprocal(score, score))
                link(v.tensor_scalar(score, score, float(KN - 1), None, ALU.mult))
                link(v.tensor_scalar(knot_at, score, 1.0, None, ALU.is_ge))
                for k in range(2, KN - 1):
                    link(v.scalar_tensor_tensor(out=knot_at, in0=score, scalar=float(k), in1=knot_at,
                                                op0=ALU.is_ge, op1=ALU.add))
                link(v.tensor_tensor(frac, score, knot_at, ALU.subtract))
                link(v.tensor_scalar(low, knot_at, 0.0, CO["knots"][:, 0:1], ALU.is_equal, ALU.mult))
                link(v.tensor_scalar(rise, knot_at, 0.0, kdif[:, 0:1], ALU.is_equal, ALU.mult))
                for k in range(1, KN - 1):
                    for dst, val in ((low, CO["knots"]), (rise, kdif)):
                        link(v.tensor_scalar(pick, knot_at, float(k), val[:, k:k + 1], ALU.is_equal, ALU.mult))
                        link(v.tensor_tensor(dst, dst, pick, ALU.add))
                link(v.tensor_tensor(frac, frac, rise, ALU.mult))
                link(v.tensor_tensor(score, low, frac, ALU.add))

            def first_best(dst):
                link(v.tensor_reduce(best[:, 0, :], score, AX, ALU.max))
                link(v.tensor_tensor(pick, score, bc(best[:, 0, :], 2, NC), ALU.is_equal))
                link(v.tensor_tensor(pick, pick, bc(CO["iota"], 1, T), ALU.mult))
                link(v.tensor_reduce(best[:, 1, :], pick, AX, ALU.min))
                link(v.tensor_tensor(dst, bc(CO["iota"], 1, T), bc(best[:, 1, :], 2, NC), ALU.is_equal))

            dve.wait_ge(S("cluster_exp"), 1)
            calibrate()
            first_best(clo[:, :, :])
            for n in range(2):
                t = slice(n * TH, (n + 1) * TH)
                link(v.tensor_tensor(prod[n].rearrange("p (t c k) -> p t c k", c=NC, k=TPC),
                                     SC[:, t, NC:NS].rearrange("p t (c k) -> p t c k", k=TPC),
                                     bc(clo[:, t, :], 3, TPC), ALU.mult))
                link(v.tensor_reduce(local[:, t, :], prod[n].rearrange("p (t c k) -> p t k c", c=NC, k=TPC),
                                     AX, ALU.add))
            v.tensor_tensor(HPR[:, :, :], HPR[:, :, :], bc(CO["b1"], 1, T), ALU.add).then_inc(S("pre_bias"), 1)
            v.tensor_copy(local, local).then_inc(S("local_score"), 1)
            dve.wait_ge(S("local_exp"), 1)
            calibrate()
            first_best(loc[:, :, :])
            dve.wait_ge(S("gelu_done"), 1)
            for n in range(2):
                t = slice(n * TH, (n + 1) * TH)
                for o in range(2):
                    w = bc(CO["w2"][:, o * CH:(o + 1) * CH], 1, TH)
                    buf = prod[o].rearrange("p (t n) -> p t n", n=CH)
                    link(v.tensor_tensor(buf, HPR[:, t, :], w, ALU.mult))
                    link(v.tensor_reduce(comp[:, t, o], buf, AX, ALU.add))
            v.tensor_tensor(comp[:, :, :], comp[:, :, :], bc(CO["b2"], 1, T), ALU.add)\
                .then_inc(S("comp_pre"), 1)
            dve.wait_ge(S("comp_done"), 1)

            def first(t, p):
                wait_before(dve, "ohT_mm", t, 2)
                one = lambda z: z[:, bass.ds(t, 1), :].rearrange("p o n -> p (o n)")
                v.tensor_tensor(oh[:, p, 0:NT].rearrange("p (c k) -> p c k", k=TPC), bc(one(clo), 2, TPC),
                                bc(one(loc), 1, NC), ALU.mult).then_inc(S("oh_done"), 1)
                v.tensor_copy(cc[:, p, :], one(comp)).then_inc(S("cc_done"), 1)
                wait(dve, "cc_done", t)
                wait(dve, "gs_done", t)
                G_ = gs[:, p, :]
                v.scalar_tensor_tensor(out=hid[:, p, 0, :], in0=G_[:, 0:GRID], scalar=cc[:, p, 0:1],
                                       in1=G_[:, 2 * GRID:3 * GRID], op0=ALU.mult, op1=ALU.add)\
                    .then_inc(S("hid_0"), 1)
                wait(dve, "hid_0", t)
                v.scalar_tensor_tensor(out=hid[:, p, 1, :], in0=G_[:, GRID:2 * GRID], scalar=cc[:, p, 1:2],
                                       in1=hid[:, p, 0, :], op0=ALU.mult, op1=ALU.add)\
                    .then_inc(S("hid_1"), 1)
                wait(dve, "hid_1", t)
                v.scalar_tensor_tensor(out=junk[:, p, :], in0=hid[:, p, 1, :], scalar=0.0,
                                       in1=G_[:, 3 * GRID:4 * GRID], op0=ALU.max, op1=ALU.mult,
                                       accum_out=mag[:, p, 0:1]).then_inc(S("mag_sum"), 1)
                wait(dve, "mag_sum", t)
                v.tensor_scalar(mag[:, p, 1:2], mag[:, p, 0:1], G_[:, 4 * GRID:4 * GRID + 1], CO["scale"],
                                ALU.add, ALU.mult).then_inc(S("mag_done"), 1)
                wait(dve, "mag_done", t)
                wait_dma(dve, "xf_back", t, p)
                v.scalar_tensor_tensor(out=yy[:, p, :], in0=G_[:, 4 * GRID + 1:GATH], scalar=mag[:, p, 1:2],
                                       in1=x1[:, p, :], op0=ALU.mult, op1=ALU.add).then_inc(S("y_sum"), 1)
                wait(dve, "y_sum", t)
                v.bn_stats(ys6[:, p, :], yy[:, p, :]).then_inc(S("y_stats"), 1)
                wait(dve, "y_stats", t)
                v.memset(pad[:, :], 0.0)
                v.bn_aggr(ymv[:, p, :], ys6[:, p, :]).then_inc(S("y_moments"), 1)

            def second(t, p):
                wait(dve, "y_rsqrt", t)
                wait_before(dve, "res_done", t, 2)
                v.tensor_scalar(yn[:, p, :], yy[:, p, :], ymv[:, p, 0:1], yve[:, p, 1:2],
                                ALU.subtract, ALU.mult).then_inc(S("yn_done"), 1)

            first(0, 0)
            first(1, 1)
            second(0, 0)
            with dve.Fori(0, (T - 2) // 2) as n:
                t = n * 2 + 2
                first(t, 0)
                second(t - 1, 1)
                first(t + 1, 1)
                second(t, 0)
            second(T - 1, 1)

        def final_pool(pool):
            g = nc.gpsimd

            def rsqrt(t, p):
                wait(pool, "y_moments", t)
                g.tensor_tensor(yve[:, p, 0:1], ymv[:, p, 1:2], eps[:, :], ALU.add).then_inc(S("yve_0"), 1)
                wait(pool, "yve_0", t)
                g.tensor_tensor(yve[:, p, 1:2], yve[:, p, 0:1], mhalf[:, 0:1], ALU.pow)\
                    .then_inc(S("y_rsqrt"), 1)

            def scale(t, p):
                wait_dma(pool, "x1_back", t, p)
                wait_dma_before(pool, "out", t, p)
                g.tensor_tensor(xin[:, p, :], xin[:, p, :], gb[:, 1, :], ALU.add).then_inc(S("x1_beta"), 1)
                wait(pool, "yn_done", t)
                g.tensor_tensor(yn[:, p, :], yn[:, p, :], gb[:, 0, :], ALU.mult).then_inc(S("yn_gamma"), 1)
                wait(pool, "yn_gamma", t)
                wait(pool, "x1_beta", t)
                g.tensor_tensor(res[:, p, :], yn[:, p, :], xin[:, p, :], ALU.add).then_inc(S("res_done"), 1)

            rsqrt(0, 0)
            rsqrt(1, 1)
            scale(0, 0)
            with pool.Fori(0, (T - 2) // 2) as n:
                t = n * 2 + 2
                rsqrt(t, 0)
                scale(t - 1, 1)
                rsqrt(t + 1, 1)
                scale(t, 0)
            scale(T - 1, 1)

        def pipeline(eng, step):
            first, last = 6, T - 2
            for i in range(first):
                step(i, i % 2)
            with eng.Fori(0, (last - first) // 2) as n:
                step(n * 2 + first, 0)
                step(n * 2 + first + 1, 1)
            for i in range(last, T + 5):
                step(i, i % 2)

        def live(i, behind):
            return not isinstance(i, int) or 0 <= i - behind < T

        block = ctx.enter_context(nc.Block())

        @block.sync
        def _(sp):
            load_all(sp)

            def x_load(t, p):
                wait_before(sp, "x_copied", t, 2)
                sp.dma_start(xin[:, p, :], plain(x_t, t)).then_inc(D("x_in", p), 16)

            def step(i, p):
                if live(i, 4):
                    t = i - 4
                    wait(sp, "o2_done", t)
                    sp.dma_start(mixed(odr, t), o2[:, :, :]).then_inc(S("o2_out"), 16)
                if live(i, -1):
                    x_load(i + 1, 1 - p)
                if live(i, 2):
                    t = i - 2
                    wait(sp, "kxn_done", t)
                    sp.dma_start(plain(kxdr, t), kxn[:, :]).then_inc(S("kx_out"), 16)
                    wait(sp, "kx_out", t, 16)
                    sp.dma_start(v2[:, p, :, 0:DM], mixed(kxdr, t)).then_inc(D("v2_in", p), 16)
                if live(i, 5):
                    t = i - 5
                    wait(sp, "zn_done", t)
                    sp.dma_start(plain(xfd, t), zn[:, :]).then_inc(S("xf_out"), 16)
                if live(i, 4):
                    t = i - 4
                    wait(sp, "o2_out", t, 16)
                    sp.dma_start(on2[:, :], plain(odr, t)).then_inc(S("on2_in"), 16)
                if live(i, 1):
                    t = i - 1
                    wait(sp, "x1_done", t)
                    sp.dma_start(plain(x1d, t), x1[:, 1 - p, :]).then_inc(D("x1_out", 1 - p), 16)

            x_load(0, 0)
            pipeline(sp, step)

            for p in range(2):
                sp.wait_ge(D("x1_out", p), T * 8)
            sp.wait_ge(S("xf_out"), T * 16)
            final_loads(sp)

        @block.tensor
        def _(pe):
            mm = nc.tensor.matmul
            pe.wait_ge(S("weights"), 16 * LOADS)
            for m in range(3):
                for k in range(CK):
                    last = mm(pa[:, m, k * NB:(k + 1) * NB], awT[:, m, k * P:(k + 1) * P], condT,
                              start=True, stop=True)
            last.then_inc(S("style_mm"), 1)
            pe.wait_ge(S("squares"), 4)
            for m in range(3):
                for o in range(CK):
                    for k in range(CK):
                        last = mm(pa[:, m, C + o * NB:C + (o + 1) * NB],
                                  w2[:, m, k, o * P:(o + 1) * P], s2[:, m, k, :],
                                  start=(k == 0), stop=(k == CK - 1))
            last.then_inc(S("demod_mm"), 1)
            pe.wait_ge(S("nullk_unit"), 1)
            nc.tensor.transpose(pb[:, 0:NR], qn[0:NR, 3 * P:4 * P], ident[0:NR, 0:NR])
            nc.tensor.transpose(pb[:, NR:2 * NR], qn[0:NR, P:2 * P], ident[0:NR, 0:NR])\
                .then_inc(S("null_T"), 1)
            pe.wait_ge(S("nvbd_done"), 2 * HP)
            for r in range(HP):
                last = mm(pb[0:H * NN, C:2 * C], nvbd[:, r, :], wout[:, r, :],
                          start=(r == 0), stop=(r == HP - 1))
            last.then_inc(S("nullw_mm"), 1)
            pe.wait_ge(S("setup_act"), 1)
            pe.wait_ge(S("setup_dve"), 1)
            pe.wait_ge(S("setup_pool"), 1)

            def linear_T(dst, w, src):
                for o in range(CK):
                    for k in range(CK):
                        last = mm(dst[:, o, :], w[:, k, o * P:(o + 1) * P],
                                  src[:, k, :, :].rearrange("p b l -> p (b l)"),
                                  start=(k == 0), stop=(k == CK - 1))
                return last

            def to_T(dst, src):
                for k in range(CK):
                    last = nc.tensor.transpose(dst[:, k, :], src[:, k * P:(k + 1) * P], ident[:, :])
                return last

            def from_T(dst, src):
                for k in range(CK):
                    last = nc.tensor.transpose(dst[:, k, :], src[:, k, :], ident[:, :])
                return last

            def project(bank, lhs, rhs):
                for k in range(CK):
                    last = mm(bank, lhs(k), rhs(k), start=(k == 0), stop=(k == CK - 1))
                return last

            def four(bank, src, r0):
                for r in range(4):
                    last = nc.tensor.transpose(bank[:, r * P:(r + 1) * P],
                                               src[:, (r0 + r) * P:(r0 + r + 1) * P], ident[:, :])
                return last

            yTf = yT[:, :, :, :].rearrange("p k b l -> p k (b l)")
            yTsf = yTs[:, :, :, :].rearrange("p k b l -> p k (b l)")
            wv4 = wv[:, :, :].rearrange("p k (r e d) -> p k r e d", r=HP, e=2)
            offs = offmask[:, :, :].rearrange("p a b -> p (a b)")

            def step(i, p):
                ta, tb, tc, to, td = i - 1, i - 2, i - 3, i - 4, i - 5
                a, at_, b, c, o, d = (live(i, n) for n in range(6))

                def gram(g4):
                    if g4:
                        wait_part(pe, "e_done", tc, g4, QG)
                    mm(pc[:, :], identb[:, :], offs, start=True, stop=False, skip_group_check=True)
                    for q in range(QG):
                        z = kT[g4 * DP:g4 * DP + DM, q, :]
                        last = mm(pc[:, q * P:(q + 1) * P], z, z, start=False, stop=(q == QG - 1),
                                  skip_group_check=True)
                    last.then_inc(S("gram"), 1)

                def e_T(g4):
                    if g4:
                        wait_part(pe, "et_done", tc, g4, QG)
                    else:
                        wait_part(pe, "e_done", tc, QG, QG)
                    wait_part(pe, "exp_done", tc, g4 + 1, QG)
                    for q in range(QG):
                        last = nc.tensor.transpose(pc[:, q * P:(q + 1) * P], E[:, g4, q, :], ident[:, :])
                    last.then_inc(S("eT"), 1)

                def out_half(r0):
                    for r in range(r0, r0 + 4):
                        mm(ps[:, 2, 0:C], oT[:, r, :], wout[:, r, :], start=(r == 0), stop=False)

                if a:
                    wait_dma(pe, "x_in", i, p)
                    if not (isinstance(i, int) and i == 0):
                        wait_part(pe, "qT_done", i - 1, 1, 2)
                    to_T(two(pa[:, 0, :], 0), xin[:, p, :]).then_inc(S("xT"), 1)
                if o:
                    wait_part(pe, "et_done", to, QG, QG)
                    for q in range(QG):
                        for g4 in range(QG):
                            last = mm(pc[g4 * DP:(g4 + 1) * DP, q * P:(q + 1) * P],
                                      v2[:, p, q * QG + g4, :], ET[:, g4, q, :], start=True, stop=True,
                                      skip_group_check=True)
                    last.then_inc(S("av_mm"), 1)
                if at_:
                    wait(pe, "kbd_done", ta, 2)
                    wait(pe, "qT_done", ta, 2)
                    wait_before(pe, "x1_done", ta)
                    for s in range(BT):
                        for r in range(HP):
                            last = mm(ps[s * L:(s + 1) * L, r // 3, (r % 3) * PJ:(r % 3 + 1) * PJ],
                                      qT[:, r, s * L:(s + 1) * L], kbd[:, s, r, :],
                                      start=True, stop=True, skip_group_check=True)
                    last.then_inc(S("sim_mm"), 1)
                if o:
                    wait(pe, "av_done", to)
                    for q in range(QG):
                        last = nc.tensor.transpose(pc[:, q * P:(q + 1) * P], av[:, q, :], ident[:, :])
                    last.then_inc(S("av_nat"), 1)
                if a:
                    wait(pe, "xm_done", i)
                    wait_before(pe, "qT_done", i, 1, 2)
                    linear_T(two(pa[:, 1, :], 0), wc, xm).then_inc(S("yT_mm"), 1)
                if b:
                    wait_before(pe, "scores_done", tb, 4)
                    wait(pe, "x1_done", tb)
                    to_T(two(pb, 0), x1[:, p, :]).then_inc(S("x1T"), 1)
                if c:
                    wait_dma(pe, "v2_in", tc, 1 - p)
                    wait_before(pe, "o2_done", tc)
                    for q in range(QG):
                        last = nc.tensor.transpose(
                            pc[:, q * P:(q + 1) * P],
                            v2[:, 1 - p, q * QG:(q + 1) * QG, :].rearrange("p g d -> p (g d)"), ident[:, :])
                    last.then_inc(S("mix_kT"), 1)
                if a:
                    wait(pe, "yT_done", i)
                    from_T(two(pa[:, 1, :], 0), yTf).then_inc(S("y_nat"), 1)
                    project(pa[:, 2, :], lambda k: yTf[:, k, :], lambda k: wk[:, k, 0:512])\
                        .then_inc(S("k_mm"), 1)
                    project(pa[:, 0, :], lambda k: yTf[:, k, :], lambda k: wk[:, k, 512:])\
                        .then_inc(S("k_mm"), 1)
                if c:
                    wait(pe, "kT_done", tc)
                    gram(0)
                if b:
                    wait(pe, "xm2_done", tb)
                    linear_T(two(pb, C), wk2, xm2).then_inc(S("kxT_mm"), 1)
                if a:
                    wait_part(pe, "k_raw", i, 1, 2)
                    project(pa[:, 2, :], lambda k: yTf[:, k, :], lambda k: wv4[:, k, :, 0, :])\
                        .then_inc(S("v_mm"), 1)
                    wait_part(pe, "k_raw", i, 2, 2)
                    project(pa[:, 0, :], lambda k: yTsf[:, k, :], lambda k: wv4[:, k, :, 1, :])\
                        .then_inc(S("v_mm"), 1)
                if at_:
                    wait(pe, "probs", ta)
                    for r in range(HP):
                        last = nc.tensor.transpose(ps[:, r // 4, (r % 4) * P:(r % 4 + 1) * P],
                                                   pr[:, r, 0:P], ident[:, :])
                    last.then_inc(S("pT_mm"), 1)
                if c:
                    gram(1)
                if a:
                    wait(pe, "xn_done", i)
                    to_T(two(pa[:, 1, :], 0), xn).then_inc(S("xnT_mm"), 1)
                if b:
                    wait(pe, "kxT_done", tb)
                    from_T(two(pb, 0), kxT).then_inc(S("kxn_mm"), 1)
                if at_:
                    wait(pe, "pT_done", ta)
                    for s in range(BT):
                        for r in range(HP):
                            last = mm(ps[s * L:(s + 1) * L, r // 3, (r % 3) * 2 * V1:(r % 3 + 1) * 2 * V1],
                                      pT[:, r, s * L:(s + 1) * L],
                                      vbd[:, 1 - p, s, r, :, :].rearrange("p e v -> p (e v)"),
                                      start=True, stop=True, skip_group_check=True)
                    last.then_inc(S("pv_mm"), 1)
                if c:
                    gram(2)
                if a:
                    wait(pe, "xnT_done", i)
                    for h in range(2):
                        wait_part(pe, "vbd_done", i, h + 1, 2)
                        project(pa[:, 2 - 2 * h, :], lambda k: xnT[:, k, :],
                                lambda k: wq[:, k, h * 512:(h + 1) * 512]).then_inc(S("q_mm"), 1)
                if d:
                    wait(pe, "on2_in", td, 16)
                    if b:
                        wait(pe, "kxn_done", tb)
                    else:
                        wait_before(pe, "scores_done", td)
                    to_T(two(pb, 0), on2).then_inc(S("omT"), 1)
                if a:
                    wait(pe, "kn_done", i)
                    four(pa[:, 1, :], kn, 0).then_inc(S("kT_mm"), 1)
                if at_:
                    wait(pe, "on_done", ta)
                    four(ps[:, 0, :], on, 0)
                    four(ps[:, 1, :], on, 4)
                    wait(pe, "pn_done", ta)
                    nc.tensor.transpose(ps[0:H * NN, 2, C:C + P], pn[:, :, :].rearrange("p h n -> p (h n)"),
                                        ident[:, :]).then_inc(S("oT_mm"), 1)
                if c:
                    gram(3)
                if d:
                    wait(pe, "om_done", td)
                    linear_T(two(pb, C), wo2, om).then_inc(S("zT_mm"), 1)
                if a:
                    wait_part(pe, "q_raw", i, 1, 2)
                    four(pa[:, 2, :], kn, 4).then_inc(S("kT_mm"), 1)
                if at_:
                    wait(pe, "oT_done", ta)
                    out_half(0)
                if c:
                    e_T(0)
                if at_:
                    out_half(4)
                    mm(ps[:, 2, 0:C], pnT[:, :], nullw[:, :], start=False, stop=True)\
                        .then_inc(S("out_mm"), 1)
                if c:
                    e_T(1)
                if d:
                    wait(pe, "zT_done", td)
                    from_T(two(pb, 0), zT).then_inc(S("zn_mm"), 1)
                    for k in range(CK):
                        last = mm(pb[:, C:C + NS + CH], zT[:, k, :], wsc[:, k, :],
                                  start=(k == 0), stop=(k == CK - 1), skip_group_check=True)
                    last.then_inc(S("score_mm"), 1)
                if a:
                    wait(pe, "qn_done", i)
                    four(pa[:, 0, :], qn, 0).then_inc(S("qT_mm"), 1)
                if c:
                    e_T(2)
                if a:
                    wait_part(pe, "kbd_done", i, 1, 2)
                    four(pa[:, 1, :], qn, 4).then_inc(S("qT_mm"), 1)
                if c:
                    e_T(3)

            pipeline(pe, step)
            final_pe(pe)

        @block.scalar
        def _(act):
            fn = nc.scalar.activation
            act.wait_ge(S("weights"), 16 * LOADS)
            act.wait_ge(S("style_mm"), 1)
            for m, col in enumerate((AB0, AB1, AB2)):
                for k in range(CK):
                    last = fn(sty[:, m, k, :], pa[:, m, k * NB:(k + 1) * NB], ACT.Identity,
                              bias=cols[:, col, k:k + 1], scale=(float(P) ** -0.5 if m == 0 else 1.0))
            last.then_inc(S("styles"), 1)
            act.wait_ge(S("styles"), 1)
            fn(s2, sty[:, :, :, :], ACT.Square).then_inc(S("squares"), 1)
            for m, w in enumerate((wc, wk2, wo2)):
                fn(w2[:, m, :, :], w[:, :, :], ACT.Square).then_inc(S("squares"), 1)
            act.wait_ge(S("demod_in"), 1)
            fn(drt, dsq, ACT.Sqrt).then_inc(S("demod_sqrt"), 1)
            act.wait_ge(S("nullw_mm"), 1)
            fn(nullw[:, :], pb[0:H * NN, C:2 * C], ACT.Copy).then_inc(S("setup_act"), 1)

            def step(i, p):
                ta, tb, tc, td = i - 1, i - 2, i - 3, i - 5
                a, at_, b, c, o, d = (live(i, n) for n in range(6))

                def raw(name, h):
                    wait_part(act, name + "_mm", i, h + 1, 2)
                    cols_ = slice(h * 512, (h + 1) * 512)
                    fn(sq[:, cols_], pa[:, 2 - 2 * h, :], ACT.Square)
                    fn((kn if name == "k" else qn)[:, cols_], pa[:, 2 - 2 * h, :], ACT.Copy)\
                        .then_inc(S(name + "_raw"), 1)

                def exps(g4):
                    wait_part(act, "e_done", tc, g4 + 1, QG)
                    fn(E[:, g4, :, :], E[:, g4, :, :], ACT.Exp, scale=DM ** -0.5).then_inc(S("exp_done"), 1)

                def keys(h):
                    wait_part(act, "kT_mm", i, h + 1, 2)
                    bank = pa[:, 1 + h, :].rearrange("p (r s l) -> p r s l", s=BT, l=L)
                    for e in range(2):
                        rows = slice(e * DH, (e + 1) * DH)
                        for s in range(BT):
                            slot = e ^ s
                            last = fn(kbd[rows, s, 4 * h:4 * h + 4, slot * L:(slot + 1) * L],
                                      bank[rows, :, s, :], ACT.Identity, bias=0.0, scale=qks[rows, 1:2])
                    last.then_inc(S("kbd_done"), 1)

                def queries(h):
                    wait_part(act, "qT_mm", i, h + 1, 2)
                    fn(qT[:, 4 * h:4 * h + 4, :].rearrange("p r t -> p (r t)"), pa[:, h, :], ACT.Identity,
                       bias=0.0, scale=qks[:, 0:1]).then_inc(S("qT_done"), 1)

                def et(g4):
                    wait_part(act, "eT", tc, g4 + 1, QG)
                    fn(ET[:, g4, :, :].rearrange("p b c -> p (b c)"), pc[:, :], ACT.Copy)\
                        .then_inc(S("et_done"), 1)

                if a:
                    wait_before(act, "x1T", i, 2)
                    wait_dma_before(act, "x1_out", i, p)
                    wait(act, "xT", i)
                    fn(x1[:, p, :], xin[:, p, :], ACT.Copy).then_inc(S("x_copied"), 1)
                if c:
                    wait(act, "mix_kT", tc)
                    fn(kT[:, :, :].rearrange("p a b -> p (a b)"), pc[:, :], ACT.Copy)\
                        .then_inc(S("kT_done"), 1)
                if a:
                    wait_before(act, "q_norm", i)
                    raw("k", 0)
                    raw("k", 1)
                if at_:
                    wait(act, "pr_sub", ta)
                    fn(pr[:, :, :], pr[:, :, :], ACT.Exp).then_inc(S("probs"), 1)
                if c:
                    exps(0)
                if a:
                    for e in range(2):
                        wait_part(act, "v_mm", i, e + 1, 2)
                        for s in range(BT):
                            rows = slice((s ^ e) * L, (s ^ e) * L + L)
                            last = fn(vbd[rows, p, s, :, e, 0:DH],
                                      pa[rows, 2 - 2 * e, :].rearrange("p (r d) -> p r d", d=DH), ACT.Copy)
                        last.then_inc(S("vbd_done"), 1)
                if at_:
                    wait(act, "pT_mm", ta)
                    fn(pT[:, :, :].rearrange("p (b r) t -> p b (r t)", b=2), ps[:, 0:2, :], ACT.Copy)\
                        .then_inc(S("pT_done"), 1)
                if a:
                    wait(act, "xnT_mm", i)
                    for k in range(CK):
                        last = fn(xnT[:, k, :], pa[:, 1, k * P:(k + 1) * P], ACT.Identity,
                                  bias=cols[:, NBI, k:k + 1], scale=cols[:, NG, k:k + 1])
                    last.then_inc(S("xnT_done"), 1)
                if b:
                    wait(act, "kxn_mm", tb)
                    wait_before(act, "kx_out", tb, 1, 16)
                    fn(kxn[:, :], pb[:, 0:C], ACT.Copy).then_inc(S("kxn_done"), 1)
                if c:
                    exps(1)
                    exps(2)
                if a:
                    wait(act, "k_norm", i)
                    raw("q", 0)
                    raw("q", 1)
                if at_:
                    wait(act, "oT_mm", ta)
                    fn(oT[:, :, :].rearrange("p (b r) t -> p b (r t)", b=2), ps[:, 0:2, :], ACT.Copy)
                    fn(pnT[:, :], ps[0:H * NN, 2, C:C + P], ACT.Copy).then_inc(S("oT_done"), 1)
                if a:
                    keys(0)
                if c:
                    exps(3)
                if a:
                    keys(1)
                if c:
                    et(0)
                if d:
                    wait(act, "zn_mm", td)
                    wait(act, "score_mm", td)
                    wait_before(act, "xf_out", td, 1, 16)
                    fn(zn[:, :], pb[:, 0:C], ACT.Copy).then_inc(S("zn_done"), 1)
                if a:
                    queries(0)
                if c:
                    et(2)
                if a:
                    queries(1)

            pipeline(act, step)
            final_act(act)

        @block.vector
        def _(dve):
            v = nc.vector
            chain = [0]

            def link(ins):
                chain[0] += 1
                ins.then_inc(S("vector_chain"), 1)
                dve.wait_ge(S("vector_chain"), chain[0])

            for s in range(BT):
                v.memset(kbd[:, s, :, :], 0.0)
            for p in range(2):
                v.memset(vbd[:, p, :, :, :, :], 0.0)
            v.memset(nvbd, 0.0)
            v.memset(oh[:, :, :], 0.0)
            v.memset(mhalf[:, :], -0.5)
            v.memset(eps[:, :], LN_EPS)
            v.memset(v2[:, :, :, :], 0.0).then_inc(S("zeros"), 1)
            dve.wait_ge(S("zeros"), 1)
            v.memset(v2[:, :, :, DM:DM + 1], 1.0)
            for s in range(BT):
                for e in range(2):
                    rows = slice((s ^ e) * L, (s ^ e) * L + L)
                    for p in range(2):
                        last = v.memset(vbd[rows, p, s, :, e, DH:V1], 1.0)
            last.then_inc(S("ones"), 1)
            dve.wait_ge(S("weights"), 16 * LOADS)
            v.tensor_copy(identb[:, :], ident[:, :])
            v.tensor_scalar(sg1, sig, 0.3, None, ALU.is_gt)
            link(v.tensor_scalar(sg2, sig, -0.3, None, ALU.is_lt))
            link(v.tensor_tensor(sg1, sg1, sg2, ALU.subtract))
            link(v.tensor_tensor(sg2, sg1, sig, ALU.subtract))
            link(v.tensor_tensor(wsc[:, :, NC:NS], sig, sg2, ALU.add))
            members = wsc[:, :, NC:NS].rearrange("p k (c t) -> p k c t", t=TPC)
            link(v.tensor_tensor(acc, members[:, :, :, 0], members[:, :, :, 1], ALU.add))
            for t in range(2, TPC):
                link(v.tensor_tensor(acc, acc, members[:, :, :, t], ALU.add))
            v.tensor_scalar(acp, acc, 0.0, None, ALU.is_gt)
            link(v.tensor_scalar(acn, acc, 0.0, None, ALU.is_lt))
            v.tensor_tensor(wsc[:, :, 0:NC], acp, acn, ALU.subtract)
            link(v.tensor_tensor(nks, nk, nk, ALU.mult))
            v.tensor_reduce(nrm[0:NR, 0, 0:2], nks, AX, ALU.add).then_inc(S("nullk_n2"), 1)
            dve.wait_ge(S("nullk_r"), 1)
            v.tensor_tensor(nkh, nk, bc(rn[0:NR, 0, 0:2], 2, DH), ALU.mult).then_inc(S("nullk_unit"), 1)
            dve.wait_ge(S("demod_mm"), 1)
            v.tensor_scalar(dsq, pa[:, 0:3, C:2 * C].rearrange("p m (k n) -> p m k n", k=CK),
                            1e-8, None, ALU.add).then_inc(S("demod_in"), 1)
            dve.wait_ge(S("demod_sqrt"), 1)
            link(v.reciprocal(dem[:, :, :, :], drt))
            link(v.tensor_tensor(dnw, dem[:, :, :, :], dem[:, :, :, :], ALU.mult))
            link(v.tensor_tensor(dnw, dnw, dsq, ALU.mult))
            link(v.tensor_scalar(dnw, dnw, -0.5, 1.5, ALU.mult, ALU.add))
            v.tensor_tensor(dem[:, :, :, :], dem[:, :, :, :], dnw, ALU.mult)
            dve.wait_ge(S("null_T"), 1)
            for e in range(2):
                rows = slice(e * DH, (e + 1) * DH)
                for s in range(BT):
                    v.tensor_scalar(kbd[rows, s, :, P + (e ^ s) * NN:P + (e ^ s) * NN + NN],
                                    pb[rows, 0:NR].rearrange("p (r n) -> p r n", n=NN),
                                    qks[rows, 1:2], None, ALU.mult)
                for r in range(HP):
                    at = (2 * r + e) * NN
                    v.tensor_copy(nvbd[rows, r, at:at + NN], pb[rows, NR + r * NN:NR + (r + 1) * NN])\
                        .then_inc(S("nvbd_done"), 1)
            v.tensor_scalar(qks[:, 0:1], qks[:, 0:1], 8.0, None, ALU.mult).then_inc(S("setup_dve"), 1)
            dve.wait_ge(S("setup_dve"), 1)

            def modulate(dst, src, table, t):
                return v.tensor_tensor(
                    dst[:, :, :, :], src.rearrange("p k (b l) -> p k b l", b=BT),
                    bc(table[:, :, bass.ds(t * BT, BT)], 3, L), ALU.mult)

            by_pair = lambda z: z[:, :].rearrange("p (r e) -> p r e", e=2)

            def step(i, p):
                ta, tb, tc, to, td = i - 1, i - 2, i - 3, i - 4, i - 5
                a, at_, b, c, o, d = (live(i, n) for n in range(6))

                def soften(g4):
                    wait_part(dve, "gram", tc, g4 + 1, QG)
                    src = pc[:, :].rearrange("p (q n) -> p q n", n=P)
                    v.tensor_reduce(mx2[:, g4, :], src, AX, ALU.max).then_inc(S("mix_max"), 1)
                    wait_part(dve, "mix_max", tc, g4 + 1, QG)
                    v.tensor_tensor(E[:, g4, :, :], src, bc(mx2[:, g4, :], 2, P), ALU.subtract)\
                        .then_inc(S("e_done"), 1)

                def et(g4):
                    wait_part(dve, "eT", tc, g4 + 1, QG)
                    v.tensor_copy(ET[:, g4, :, :].rearrange("p b c -> p (b c)"), pc[:, :])\
                        .then_inc(S("et_done"), 1)

                def norms(name, n):
                    wait_part(dve, name + "_raw", i, 2, 2)
                    v.tensor_reduce(nrm[:, n, :], sq[:, :].rearrange("p (h d) -> p h d", d=DH), AX, ALU.add)\
                        .then_inc(S(name + "_norm"), 1)
                    wait(dve, name + "_norm", i)
                    v.tensor_scalar(nrg[:, n, :], nrm[:, n, :], 1e-24, None, ALU.max)\
                        .then_inc(S(name + "_guard"), 1)

                def unit(name, n, buf):
                    wait(dve, name + "_rsqrt", i)
                    z = buf[:, :].rearrange("p (h d) -> p h d", d=DH)
                    v.tensor_tensor(z, z, bc(rn[:, n, :], 2, DH), ALU.mult).then_inc(S(name + "n_done"), 1)

                if a:
                    wait(dve, "xT", i)
                    modulate(xm, two(pa[:, 0, :], 0), sty[:, 0, :, :], i).then_inc(S("xm_done"), 1)
                if o:
                    wait(dve, "av_mm", to)
                    v.tensor_copy(av[:, :, :].rearrange("p a b -> p (a b)"), pc[:, :])\
                        .then_inc(S("av_done"), 1)
                if at_:
                    wait(dve, "sim_mm", ta)
                    v.tensor_tensor(pr[:, 0:6, :].rearrange("p (b r) j -> p b (r j)", b=2),
                                    ps[:, 0:2, 0:3 * PJ],
                                    alibi[:, 0:6, :].rearrange("p (b r) j -> p b (r j)", b=2), ALU.add)
                    v.tensor_tensor(pr[:, 6:8, :].rearrange("p r j -> p (r j)"), ps[:, 2, 0:2 * PJ],
                                    alibi[:, 6:8, :].rearrange("p r j -> p (r j)"), ALU.add)\
                        .then_inc(S("pr_add"), 1)
                if o:
                    wait(dve, "av_nat", to)
                    wait_before(dve, "o2_out", to, 1, 16)
                    src = pc[:, :].rearrange("p (g d) -> p g d", d=DP)
                    v.reciprocal(rd2[:, :], src[:, :, DM:DM + 1].rearrange("p g o -> p (g o)"))\
                        .then_inc(S("mix_rden"), 1)
                    wait(dve, "mix_rden", to)
                    v.tensor_tensor(o2[:, :, :], src[:, :, 0:DM], bc(rd2[:, :], 2, DM), ALU.mult)\
                        .then_inc(S("o2_done"), 1)
                if a:
                    wait(dve, "yT_mm", i)
                    modulate(yT, two(pa[:, 1, :], 0), dem[:, 0, :, :], i).then_inc(S("y_dem"), 1)
                    wait(dve, "y_dem", i)
                    for k in range(CK):
                        last = v.tensor_scalar(yT[:, k, :, :], yT[:, k, :, :], cols[:, CB, k:k + 1], CLAMP,
                                               ALU.add, ALU.min)
                    last.then_inc(S("y_min"), 1)
                    wait(dve, "y_min", i)
                    v.tensor_scalar(yTs[:, :, ::-1, :], yT[:, :, :, :], -CLAMP, None, ALU.max)\
                        .then_inc(S("yTs_done"), 1)
                    wait(dve, "yTs_done", i)
                    v.tensor_scalar(yT[:, :, :, :], yT[:, :, :, :], -CLAMP, None, ALU.max)\
                        .then_inc(S("yT_done"), 1)
                if at_:
                    keys = pr[:, :, 0:P].rearrange("p r (e j) -> p r e j", e=2)
                    nulls = pr[:, :, P:PJ].rearrange("p r (e n) -> p r e n", e=2)
                    wait(dve, "pr_add", ta)
                    v.tensor_reduce(by_pair(mxm), keys, AX, ALU.max)
                    v.tensor_reduce(by_pair(mxn), nulls, AX, ALU.max).then_inc(S("pr_maxes"), 1)
                    wait(dve, "pr_maxes", ta)
                    v.tensor_tensor(mx[:, :], mxm[:, :], mxn[:, :], ALU.max).then_inc(S("pr_max"), 1)
                    wait(dve, "pr_max", ta)
                    v.tensor_tensor(keys, keys, bc(by_pair(mx), 3, L), ALU.subtract)
                    v.tensor_tensor(nulls, nulls, bc(by_pair(mx), 3, NN), ALU.subtract)\
                        .then_inc(S("pr_sub"), 1)
                if b:
                    wait(dve, "x1T", tb)
                    modulate(xm2, two(pb, 0), sty[:, 1, :, :], tb).then_inc(S("xm2_done"), 1)
                if a:
                    wait(dve, "y_nat", i)
                    v.bn_stats(st6[:, :], pa[:, 1, 0:C]).then_inc(S("y_st6"), 1)
                    wait(dve, "y_st6", i)
                    v.memset(pad[:, :], 0.0)
                    v.bn_aggr(mv[:, :], st6[:, :]).then_inc(S("y_mv"), 1)
                if c:
                    soften(0)
                if b:
                    wait(dve, "kxT_mm", tb)
                    modulate(kxd_, two(pb, C), dem[:, 1, :, :], tb).then_inc(S("kx_dem"), 1)
                if a:
                    wait(dve, "y_rstd", i)
                    v.tensor_scalar(xn[:, :], pa[:, 1, 0:C], mv[:, 0:1], rs[:, 0:1],
                                    ALU.subtract, ALU.mult).then_inc(S("xn_done"), 1)
                if b:
                    wait(dve, "kx_dem", tb)
                    v.tensor_tensor(kxT[:, :, :], kxd_[:, :, :, :].rearrange("p k b l -> p k (b l)"),
                                    bc(cols[:, KB, :], 2, P), ALU.add).then_inc(S("kxT_done"), 1)
                if a:
                    norms("k", 1)
                if at_:
                    wait(dve, "probs", ta)
                    for s in range(BT):
                        rows = slice(s * L, (s + 1) * L)
                        src = pr[rows, :, P:PJ].rearrange("p r (e n) -> p r e n", e=2)
                        last = v.tensor_copy(pnr[rows, :, :].rearrange("p (r e) n -> p r e n", e=2),
                                             src[:, :, ::-1, :] if s else src)
                    last.then_inc(S("null_order"), 1)
                    wait(dve, "null_order", ta)
                    v.tensor_reduce(den[:, :], pnr[:, :, :], AX, ALU.add).then_inc(S("null_sum"), 1)
                if c:
                    soften(1)
                if a:
                    unit("k", 1, kn)
                if at_:
                    wait(dve, "pv_mm", ta)
                    wait(dve, "null_sum", ta)
                    head = ps[:, 0:2, 0:6 * V1].rearrange("p b (h v) -> p b h v", v=V1)
                    tail = ps[:, 2, 0:4 * V1].rearrange("p (h v) -> p h v", v=V1)
                    v.tensor_tensor(den2[:, 0:12].rearrange("p (b h) -> p b h", b=2), head[:, :, :, DH],
                                    den[:, 0:12].rearrange("p (b h) -> p b h", b=2), ALU.add)
                    v.tensor_tensor(den2[:, 12:16], tail[:, :, DH], den[:, 12:16], ALU.add)\
                        .then_inc(S("den_done"), 1)
                    wait(dve, "den_done", ta)
                    v.reciprocal(rden[:, :], den2[:, :]).then_inc(S("rden_done"), 1)
                    wait(dve, "rden_done", ta)
                    v.tensor_tensor(on[:, 0:12 * DH].rearrange("p (b h d) -> p b h d", b=2, d=DH),
                                    head[:, :, :, 0:DH],
                                    bc(rden[:, 0:12].rearrange("p (b h) -> p b h", b=2), 3, DH), ALU.mult)
                    v.tensor_tensor(on[:, 12 * DH:].rearrange("p (h d) -> p h d", d=DH), tail[:, :, 0:DH],
                                    bc(rden[:, 12:16], 2, DH), ALU.mult).then_inc(S("on_done"), 1)
                    v.tensor_tensor(pn[:, :, :], pnr[:, :, :], bc(rden[:, :], 2, NN), ALU.mult)\
                        .then_inc(S("pn_done"), 1)
                if c:
                    soften(2)
                if d:
                    wait(dve, "omT", td)
                    modulate(om, two(pb, 0), sty[:, 2, :, :], td).then_inc(S("om_done"), 1)
                if a:
                    norms("q", 0)
                if c:
                    soften(3)
                if d:
                    wait(dve, "zT_mm", td)
                    modulate(zd, two(pb, C), dem[:, 2, :, :], td).then_inc(S("z_dem"), 1)
                    wait(dve, "z_dem", td)
                    v.tensor_tensor(zT[:, :, :], zd[:, :, :, :].rearrange("p k b l -> p k (b l)"),
                                    bc(cols[:, OB, :], 2, P), ALU.add).then_inc(S("zT_done"), 1)
                if a:
                    unit("q", 0, qn)
                if at_:
                    wait(dve, "out_mm", ta)
                    wait(dve, "x_copied", ta)
                    v.tensor_tensor(x1[:, 1 - p, :], ps[:, 2, 0:C], x1[:, 1 - p, :], ALU.add)\
                        .then_inc(S("x1_done"), 1)
                if c:
                    et(1)
                if d:
                    wait(dve, "zn_done", td)
                    v.tensor_copy(SC[:, bass.ds(td, 1), :].rearrange("p o n -> p (o n)"), pb[:, C:C + NS])
                    v.tensor_copy(HPR[:, bass.ds(td, 1), :].rearrange("p o n -> p (o n)"),
                                  pb[:, C + NS:C + NS + CH]).then_inc(S("scores_done"), 1)
                if c:
                    et(3)

            pipeline(dve, step)
            final_dve(dve, link)

        @block.gpsimd
        def _(pool):
            g = nc.gpsimd
            pool.wait_ge(S("zeros"), 1)
            pool.wait_ge(S("ones"), 1)
            pool.wait_ge(S("nullk_n2"), 1)
            g.tensor_scalar(nrg[0:NR, 0, 0:2], nrm[0:NR, 0, 0:2], 1e-24, None, ALU.max).then_inc(S("nullk_g"), 1)
            pool.wait_ge(S("nullk_g"), 1)
            g.tensor_tensor(rn[0:NR, 0, 0:2], nrg[0:NR, 0, 0:2], mhalf[0:NR, 0:2], ALU.pow)\
                .then_inc(S("nullk_r"), 1)
            pool.wait_ge(S("nullk_unit"), 1)
            g.memset(ve[:, :], 0.0).then_inc(S("setup_pool"), 1)
            pool.wait_ge(S("setup_pool"), 1)

            def step(i, p):
                if live(i, 0):
                    wait(pool, "y_mv", i)
                    g.tensor_tensor(ve[:, :], mv[:, 1:2], eps[:, :], ALU.add).then_inc(S("y_var"), 1)
                    wait(pool, "y_var", i)
                    g.tensor_tensor(rs[:, :], ve[:, :], mhalf[:, 0:1], ALU.pow).then_inc(S("y_rstd"), 1)
                    for n, name in ((1, "k"), (0, "q")):
                        wait(pool, name + "_guard", i)
                        g.tensor_tensor(rn[:, n, :], nrg[:, n, :], mhalf[:, :], ALU.pow)\
                            .then_inc(S(name + "_rsqrt"), 1)

            pipeline(pool, step)
            final_pool(pool)


_OUT = ((128, 64, 256), "float32")


def kernel(**inputs):
    import numpy as np
    import concourse.bacc as bacc
    from concourse import mybir as mb
    from concourse.bass_utils import run_bass_kernel_spmd as run

    a = {k: np.asarray(v) for k, v in inputs.items()}
    ar = {"x": a["x"], "condT": a["cond_512"].T}
    for n in ("L0_cond_affine_w", "L0_cond2_k_aff_w", "L0_cond2_o_aff_w", "L0_cond_weight", "L0_cond2_k_w",
              "L0_cond2_o_w"):
        ar[n + "T"] = a[n].T
    for n in ("L0_cond_bias", "L0_attn_norm_g", "L0_attn_norm_b", "L0_cond2_k_b", "L0_cond2_o_b",
              "L0_cond_affine_b", "L0_cond2_k_aff_b", "L0_cond2_o_aff_b"):
        ar[n + "_c"] = a[n].reshape(2, 128).T
    ar["qk_scale"] = np.stack([np.tile(a["L0_attn_q_scale"], 2), np.tile(a["L0_attn_k_scale"], 2)], axis=1)
    ar["sigT"] = a["L0_ffn_signatures_raw"].T
    null = a["L0_attn_null_kv"].reshape(8, 2, 2, 2, 64).transpose(3, 0, 2, 1, 4)
    ar["null_k"], ar["null_v"] = null[0].reshape(16, 2, 64), null[1].reshape(16, 2, 64)
    ar["L0_attn_Wq"] = a["L0_attn_Wq"]
    ar["Wk"], ar["Wv"] = a["L0_attn_Wkv"][:, :1024], a["L0_attn_Wkv"][:, 1024:]
    ar["L0_attn_Wout"] = a["L0_attn_Wout"]
    ar["L0_ffn_compress_w1"] = a["L0_ffn_compress_w1"]
    ar["ident"] = np.eye(128, dtype=np.float32)
    start = 2.0 ** (-2.0 ** (-(np.log2(16) - 3)))
    slopes = np.array([start * start ** i for i in range(16)], dtype=np.float32)
    row = np.arange(64)
    pos = np.concatenate([np.arange(64) + 2, np.arange(2)])
    dist = -np.abs(pos[None, :] - (row[:, None] + 2)).astype(np.float32)
    table = slopes[None, :, None] * dist[:, None, :]
    seen = pos[None, :] <= row[:, None] + 2
    table = np.where(seen[:, None, :], table, np.float32(-3.0e38)).astype(np.float32)
    table = table.reshape(64, 8, 2, 66)
    ar["alibi"] = np.concatenate([np.concatenate([z[:, :, :, :64].reshape(64, 8, 128), z[:, :, :, 64:].reshape(64, 8, 4)],
                                                 axis=2) for z in (table, table[:, :, ::-1])])
    import ml_dtypes
    own = np.arange(128)[:, None] // 16 == np.arange(128)[None, :] // 16
    ar["offmask"] = np.repeat(np.where(own, 0.0, -1e30).astype(ml_dtypes.bfloat16)[:, None, :], 4, axis=1)
    row_of = np.concatenate([a["L0_ffn_compress_w2"].T.reshape(-1), a["L0_ffn_compress_b1"],
                             a["L0_ffn_compress_b2"], a["L0_ffn_knot_values"],
                             np.arange(8, dtype=np.float32) - 8, a["L0_ffn_temperature"],
                             a["L0_ffn_output_scale"]])
    ar["coef"] = np.repeat(row_of[None, :], 128, axis=0)
    ar["gb"] = np.repeat(np.stack([a["L0_ffn_norm_gamma"], a["L0_ffn_norm_beta"]])[None], 128, axis=0)
    ar["gath"] = np.concatenate([a["L0_ffn_spline_w1"].reshape(64, 32), a["L0_ffn_spline_b1"],
                                 a["L0_ffn_spline_w2"].reshape(64, 16), a["L0_ffn_spline_b2"],
                                 a["L0_ffn_directions"]], axis=1)

    nc = bacc.Bacc("TRN2", target_bir_lowering=False, num_devices=1)
    arrays, aps = {}, {}
    for name, v in ar.items():
        v = np.ascontiguousarray(v)
        arrays[f"in_{name}"] = v
        aps[name] = nc.dram_tensor(f"in_{name}", v.shape, mb.dt.from_np(v.dtype), kind="ExternalInput").ap()
    out = nc.dram_tensor("out_0", _OUT[0], mb.dt.from_np(np.dtype(_OUT[1])), kind="ExternalOutput").ap()
    adaln_attention_ffn(nc, aps, out)
    r = run(nc, [arrays], core_ids=[0])
    return r.results[0]["out_0"]
```

```python
import concourse.bass as bass
from concourse import mybir
from contextlib import ExitStack


def adaln_attention_ffn(nc: bass.Bass, A: dict, out: bass.AP):
    f32 = mybir.dt.float32
    ALU, ACT, AX = mybir.AluOpType, mybir.ActivationFunctionType, mybir.AxisListType.X

    NB, L, C = A["x"].shape
    P = 128
    BT = P // L
    T = NB * L // P
    CK = C // P
    H, DH = 16, 64
    HP = H // 2
    NN = 2
    J = L + NN
    PJ = 2 * J
    V1 = DH + 1
    INNER = H * DH
    DM = C // H
    TG = P // H
    G = P // TG
    QG = 4
    DP = 32
    NT, NC = 64, 8
    TPC = NT // NC
    KN = 8
    GRID = 16
    CH = 64
    NS = NC + NT
    GATH = 2 * GRID + GRID + GRID + 1 + C
    CLAMP = 256.0
    LN_EPS = 1e-5

    ctx = ExitStack()
    with ctx:
        def sb(name, shape, dt=f32):
            return ctx.enter_context(nc.sbuf_tensor(name, shape, dt))

        sems = {}

        def S(name):
            if name not in sems:
                sems[name] = ctx.enter_context(nc.semaphore(name))
            return sems[name]

        def wait(eng, name, t, by=1):
            eng.wait_ge(S(name), (t + 1) * by)

        def wait_part(eng, name, t, k, of):
            eng.wait_ge(S(name), t * of + k)

        def wait_before(eng, name, t, back=1, by=1):
            if isinstance(t, int) and t < back:
                return
            eng.wait_ge(S(name), (t + 1 - back) * by)

        def wait_dma(eng, name, t, p):
            eng.wait_ge(S(name + "_even" * (not p) + "_odd" * p), (t - p) * 8 + 16)

        def wait_dma_before(eng, name, t, p):
            if isinstance(t, int) and t < 2:
                return
            eng.wait_ge(S(name + "_even" * (not p) + "_odd" * p), (t - p) * 8)

        def D(name, p):
            return S(name + "_even" * (not p) + "_odd" * p)

        ident = sb("ident", [P, P])
        token = sb("token", [P, TG])
        off = sb("off", [P, 2])
        alibi = sb("alibi", [P, HP, PJ])
        wc = sb("wc", [P, CK, C])
        wk2 = sb("wk2", [P, CK, C])
        wo2 = sb("wo2", [P, CK, C])
        wq = sb("wq", [P, 2, CK, INNER])
        wk = sb("wk", [P, 2, CK, INNER])
        wv = sb("wv", [P, 2, CK, INNER])
        wout = sb("wout", [P, HP, C])
        wsc = sb("wsc", [P, CK, NS + CH])
        sty = sb("sty", [P, 3, CK, NB])
        dem = sb("dem", [P, 3, CK, NB])
        cols = sb("cols", [P, 8, CK])
        CB, NG, NBI, KB, OB, AB0, AB1, AB2 = range(8)
        qks = sb("qks", [P, 2])
        nullw = sb("nullw", [H * NN, C])

        xin = sb("xin", [P, 2, C])
        xm = sb("xm", [P, CK, BT, L])
        yT = sb("yT", [P, CK, BT, L])
        xn = sb("xn", [P, C])
        xnT = sb("xnT", [P, CK, P])
        xnTs = sb("xnTs", [P, 2, CK, P])
        sq = sb("sq", [P, INNER])
        kn = sb("kn", [P, INNER])
        qn = sb("qn", [P, INNER])
        qT = sb("qT", [P, HP, P])
        kbd = sb("kbd", [P, BT, HP, PJ])
        vbd = sb("vbd", [P, 2, BT, HP, 2, V1])
        pr = sb("pr", [P, HP, PJ])
        pT = sb("pT", [P, HP, P])
        on = pr[:, :, :].rearrange("p a b -> p (a b)")[:, 0:INNER]
        yTp = sb("yTp", [P, 2, CK, BT, L])
        yTs = sb("yTs", [P, 2, CK, BT, L])
        pnr = sb("pnr", [P, H, NN])
        mxn = sb("mxn", [P, H])
        mxm = sb("mxm", [P, H])
        oT = pT
        pn = sb("pn", [P, H, NN])
        pnT = sb("pnT", [H * NN, P])
        st6 = sb("st6", [P, 6])
        mv = sb("mv", [P, 2])
        ve = sb("ve", [P, 1])
        rs = sb("rs", [P, 1])
        nrm = sb("nrm", [P, 2, H])
        nrg = sb("nrg", [P, 2, H])
        rn = sb("rn", [P, 2, H])
        mhalf = sb("mhalf", [P, H])
        eps = sb("eps", [P, 1])
        pad = sb("pad", [P, 1])
        mx = sb("mx", [P, H])
        den = sb("den", [P, H])
        den2 = sb("den2", [P, H])
        rden = sb("rden", [P, H])
        x1 = sb("x1", [P, 2, C])
        xm2 = sb("xm2", [P, CK, BT, L])
        kxd_ = sb("kxd_", [P, CK, BT, L])
        kxT = sb("kxT", [P, CK, P])
        kxn = sb("kxn", [P, C])
        v2 = sb("v2", [P, 2, G, DP])
        kT = sb("kT", [P, QG, P])
        kTm = sb("kTm", [P, QG, P])
        E = sb("E", [P, QG, QG, P])
        ET = E
        mx2 = sb("mx2", [P, QG, QG])
        av = sb("av", [P, QG, P])
        rd2 = sb("rd2", [P, G])
        o2 = sb("o2", [P, G, DM])
        on2 = sb("on2", [P, 2, C])
        om = sb("om", [P, CK, BT, L])
        zd = sb("zd", [P, CK, BT, L])
        zT = sb("zT", [P, CK, P])
        zn = sb("zn", [P, 2, C])
        hT = sb("hT", [CH + 1, 2, P])

        pa = ctx.enter_context(nc.psum_tensor("pa", [P, 3, 512], f32))
        ps = ctx.enter_context(nc.psum_tensor("ps", [P, 3, 512], f32))
        pc = ctx.enter_context(nc.psum_tensor("pc", [P, 512], f32))
        pb = ctx.enter_context(nc.psum_tensor("pb", [P, 512], f32))

        x1d = nc.dram_tensor("x1d", [T, P, C], f32)
        kxdr = nc.dram_tensor("kxdr", [T, P, C], f32)
        odr = nc.dram_tensor("odr", [T, P, C], f32)
        x_t = A["x"].rearrange("(t b) l c -> t (b l) c", b=BT)
        out_t = out.rearrange("(t b) l c -> t (b l) c", b=BT)

        def mixed(dram, t):
            return dram[bass.ds(t, 1), :, :].rearrange(
                "o (g k) (h d) -> (o k h) g d", k=TG, h=H)

        def plain(dram, t):
            return dram[bass.ds(t, 1), :, :].rearrange("o p c -> (o p) c")

        def bc(ap, axis, n):
            u = ap.unsqueeze(axis)
            shape = list(u.shape)
            shape[axis] = n
            return u.broadcast_to(shape)

        def part(ap):
            return ap.bitcast(mybir.dt.float32r)

        def two(bank, lo):
            return bank[:, lo:lo + C].rearrange("p (k q) -> p k q", k=CK)

        rawT = E[:, :, :, :].rearrange("p a b c -> p (a b c)")
        awT = rawT[:, 0:3 * C].rearrange("p (m c) -> p m c", m=3)
        condT = rawT[:, 3 * C:3 * C + NB]
        raw_w = {"wk": vbd[:, 0, :, :, :, :], "wv": vbd[:, 1, :, :, :, :], "wq": kbd[:, :, :, :]}
        raw_w = {n: z.rearrange("p b r e v -> p (b r e v)" if n != "wq" else "p b r j -> p (b r j)")
                 for n, z in raw_w.items()}
        raw_w = {n: z[:, 0:CK * INNER].rearrange("p (k n) -> p k n", k=CK) for n, z in raw_w.items()}
        chunks = lambda z: z.rearrange("p (k c) -> p k c", k=CK)
        prf = pr[:, :, :].rearrange("p a b -> p (a b)")
        w2 = [chunks(prf[:, 0:CK * C]), chunks(prf[:, CK * C:2 * CK * C]), x1[:, :, :]]
        s2 = rawT[:, 1024:1024 + 3 * CK * NB].rearrange("p (m k n) -> p m k n", m=3, k=CK)
        sig = kn[:, 0:CK * NT].rearrange("p (k n) -> p k n", k=CK)
        sg1 = kn[:, 256:256 + CK * NT].rearrange("p (k n) -> p k n", k=CK)
        sg2 = kn[:, 512:512 + CK * NT].rearrange("p (k n) -> p k n", k=CK)
        acc = kn[:, 768:768 + CK * NC].rearrange("p (k n) -> p k n", k=CK)
        acp = kn[:, 800:800 + CK * NC].rearrange("p (k n) -> p k n", k=CK)
        acn = kn[:, 832:832 + CK * NC].rearrange("p (k n) -> p k n", k=CK)
        NR = HP * NN
        nk = qn[0:NR, 0:P].rearrange("r (a d) -> r a d", a=2)
        nv = qn[0:NR, P:2 * P].rearrange("r (a d) -> r a d", a=2)
        nks = qn[0:NR, 2 * P:3 * P].rearrange("r (a d) -> r a d", a=2)
        nkh = qn[0:NR, 3 * P:4 * P].rearrange("r (a d) -> r a d", a=2)
        nvbd = sq[:, 0:HP * H * NN].rearrange("p (r n) -> p r n", r=HP)
        nkT = sb("nkT", [P, NR])
        dsq = on[:, 0:3 * CK * NB].rearrange("p (m k n) -> p m k n", m=3, k=CK)
        drt = pT[:, :, :].rearrange("p a b -> p (a b)")[:, 0:3 * CK * NB].rearrange(
            "p (m k n) -> p m k n", m=3, k=CK)
        dnw = kn[:, 0:3 * CK * NB].rearrange(
            "p (m k n) -> p m k n", m=3, k=CK)
        linear = ["L0_cond_weight", "L0_cond2_k_w", "L0_cond2_o_w"]
        affine = ["L0_cond_affine_w", "L0_cond2_k_aff_w", "L0_cond2_o_aff_w"]
        LOADS = {"cond_in": 8, "small_in": 8, "wk_in": 1, "wv_in": 1, "wq_in": 1, "late_in": 7}

        def loaded(eng, *names):
            for name in names:
                eng.wait_ge(S(name), 16 * LOADS[name])

        def load_all(sp):
            n = dict.fromkeys(LOADS, 0)

            def ld(group, dst, src):
                sp.dma_start(dst, src).then_inc(S(group), 16)
                n[group] += 1

            in_chunks = lambda name: A[name].rearrange("(k p) n -> p k n", p=P)
            ld("cond_in", condT, A["condT"])
            for m, name in enumerate(affine):
                ld("cond_in", awT[:, m, :], A[name + "T"])
            ld("cond_in", cols[:, :, :], A["cols"])
            for dst, name in zip((wc, wk2, wo2), linear):
                ld("cond_in", dst[:, :, :], in_chunks(name + "T"))
            ld("small_in", ident[:, :], A["ident"])
            ld("small_in", nk, A["null_k"])
            ld("small_in", nv, A["null_v"])
            ld("small_in", qks[:, :], A["qk_scale"])
            ld("small_in", coef[:, :], A["coef"])
            ld("small_in", token[:, :], A["token"])
            ld("small_in", sig, in_chunks("sigT"))
            ld("small_in", wsc[:, :, NS:NS + CH], in_chunks("L0_ffn_compress_w1"))
            ld("wk_in", raw_w["wk"], in_chunks("Wk"))
            ld("wv_in", raw_w["wv"], in_chunks("Wv"))
            ld("wq_in", raw_w["wq"], in_chunks("L0_attn_Wq"))
            ld("late_in", wout[:, :, :], A["L0_attn_Wout"].rearrange("(r p) n -> p r n", p=P))
            ld("late_in", alibi[:, :, :], A["alibi"])
            ld("late_in", off[:, :], A["off"])
            ld("late_in", w2b[:, :], A["w2b"])
            ld("late_in", b1[:, :], A["b1"])
            ld("late_in", gath[:, :], A["gath"])
            ld("late_in", gb[:, :, :], A["gb"])
            assert n == LOADS, n

        coef = sb("coef", [P, 3 * KN + 2])
        gb = sb("gb", [P, 2, C])
        gath = sb("gath", [NT, GATH])
        w2b = sb("w2b", [CH + 1, 2])
        b1 = sb("b1", [CH, 1])
        CO = {}
        at = 0
        for name, n in (("knots", KN), ("behind", NC), ("steps", KN), ("temp", 1), ("scale", 1)):
            CO[name] = coef[:, at:at + n]
            at += n
        ninv = sb("ninv", [P, 2])
        kk = sb("kk", [P, 2, KN - 1])
        sc = sb("sc", [P, 2, NT])
        esc = sb("esc", [P, 2, NC])
        lsc = sb("lsc", [P, NC])
        fl = sb("fl", [P, 2, NC])
        ge = sb("ge", [P, 2 * NC, KN - 2])
        seg = sb("seg", [P, 2, NC])
        eq = sb("eq", [P, 2 * NC, KN - 1])
        lr = sb("lr", [P, 2, 2 * NC, KN - 1])
        lo_rise = sb("lo_rise", [P, 2, 2 * NC])
        frac = sb("frac", [P, 2, NC])
        gate = sb("gate", [P, 2, NC])
        best = sb("best", [P, 2, 2])
        pick = sb("pick", [P, 2, NC])
        chosen = sb("chosen", [P, 2, 2, NC])
        own = sb("own", [P, NC, TPC])
        oh = sb("oh", [P, P])
        ohT = sb("ohT", [NT, P])
        comp = sb("comp", [P, 2, 2])
        gs = sb("gs", [P, GATH])
        hid = sb("hid", [P, 2, GRID])
        junk = sb("junk", [P, GRID])
        mag = sb("mag", [P, 2])
        yy = sb("yy", [P, C])
        ys6 = sb("ys6", [P, 6])
        ymv = sb("ymv", [P, 2])
        yve = sb("yve", [P, 2])
        yn = sb("yn", [P, C])
        xb = sb("xb", [P, 2, C])
        res = sb("res", [P, 2, C])

        def pipeline(eng, step):
            first, last = 10, T - 2
            for i in range(first):
                step(i, i % 2)
            with eng.Fori(0, (last - first) // 2) as n:
                step(n * 2 + first, 0)
                step(n * 2 + first + 1, 1)
            for i in range(last, T + 8):
                step(i, i % 2)

        def live(i, behind):
            return not isinstance(i, int) or 0 <= i - behind < T

        block = ctx.enter_context(nc.Block())

        @block.sync
        def _(sp):
            load_all(sp)

            def x_load(t, p):
                wait_before(sp, "x_copied", t, 2)
                sp.dma_start(xin[:, p, :], plain(x_t, t)).then_inc(D("x_in", p), 16)

            def step(i, p):
                if live(i, 4):
                    t = i - 4
                    wait(sp, "o2_done", t)
                    sp.dma_start(mixed(odr, t), o2[:, :, :]).then_inc(S("o2_out"), 16)
                if live(i, -1):
                    x_load(i + 1, 1 - p)
                if live(i, 4):
                    t = i - 4
                    wait(sp, "o2_out", t, 16)
                    sp.dma_start(on2[:, p, :], plain(odr, t)).then_inc(D("on2_in", p), 16)
                if live(i, 8):
                    wait(sp, "res_done", i - 8)
                    sp.dma_start(plain(out_t, i - 8), res[:, p, :]).then_inc(D("out", p), 16)
                if live(i, 6):
                    wait_before(sp, "res_done", i - 6, 2)
                    wait_dma(sp, "x1_out", i - 6, p)
                    sp.dma_start(xb[:, p, :], plain(x1d, i - 6)).then_inc(D("x1_back", p), 16)
                if live(i, 2):
                    t = i - 2
                    wait(sp, "kxn_done", t)
                    sp.dma_start(plain(kxdr, t), kxn[:, :]).then_inc(S("kx_out"), 16)
                    wait(sp, "kx_out", t, 16)
                    sp.dma_start(v2[:, p, :, 0:DM], mixed(kxdr, t)).then_inc(D("v2_in", p), 16)
                if live(i, 1):
                    t = i - 1
                    wait(sp, "x1_done", t)
                    sp.dma_start(plain(x1d, t), x1[:, 1 - p, :]).then_inc(D("x1_out", 1 - p), 16)

            x_load(0, 0)
            pipeline(sp, step)

            for p in range(2):
                sp.wait_ge(D("out", p), T * 8)

        @block.tensor
        def _(pe):
            mm = nc.tensor.matmul
            loaded(pe, "cond_in")
            for m in range(3):
                for k in range(CK):
                    last = mm(pa[:, m, k * NB:(k + 1) * NB], awT[:, m, k * P:(k + 1) * P], condT,
                              start=True, stop=True)
            last.then_inc(S("style_mm"), 1)
            pe.wait_ge(S("nullk_unit"), 1)
            loaded(pe, "small_in")
            nc.tensor.transpose(pb[:, 0:NR], qn[0:NR, 3 * P:4 * P], ident[0:NR, 0:NR])
            nc.tensor.transpose(pb[:, NR:2 * NR], qn[0:NR, P:2 * P], ident[0:NR, 0:NR])\
                .then_inc(S("null_T"), 1)
            pe.wait_ge(S("squares"), 4)
            for m in range(3):
                for o in range(CK):
                    for k in range(CK):
                        last = mm(pa[:, m, C + o * NB:C + (o + 1) * NB],
                                  w2[m][:, k, o * P:(o + 1) * P], s2[:, m, k, :],
                                  start=(k == 0), stop=(k == CK - 1))
            last.then_inc(S("demod_mm"), 1)
            pe.wait_ge(S("nvbd_done"), 2 * HP + 1)
            loaded(pe, "late_in")
            for r in range(HP):
                last = mm(pb[0:H * NN, C:2 * C], nvbd[:, r, :], wout[:, r, :],
                          start=(r == 0), stop=(r == HP - 1))
            last.then_inc(S("nullw_mm"), 1)
            pe.wait_ge(S("setup_act"), 1)
            pe.wait_ge(S("setup_dve"), 1)
            pe.wait_ge(S("setup_pool"), 1)

            def linear_T(dst, w, src):
                for o in range(CK):
                    for k in range(CK):
                        last = mm(dst[:, o, :], w[:, k, o * P:(o + 1) * P],
                                  src[:, k, :, :].rearrange("p b l -> p (b l)"),
                                  start=(k == 0), stop=(k == CK - 1))
                return last

            def to_T(dst, src):
                for k in range(CK):
                    last = nc.tensor.transpose(dst[:, k, :], src[:, k * P:(k + 1) * P], ident[:, :])
                return last

            def from_T(dst, src):
                for k in range(CK):
                    last = nc.tensor.transpose(dst[:, k, :], src[:, k, :], ident[:, :])
                return last

            def project(bank, lhs, rhs):
                n = 0
                for k in range(CK):
                    for a_, b_ in ((0, 0), (0, 1), (1, 0)):
                        last = mm(bank, part(lhs(a_, k)), part(rhs(b_, k)), start=(n == 0), stop=(n == 3 * CK - 1))
                        n += 1
                return last

            def four(bank, src, r0):
                for r in range(4):
                    last = nc.tensor.transpose(bank[:, r * P:(r + 1) * P],
                                               src[:, (r0 + r) * P:(r0 + r + 1) * P], ident[:, :])
                return last

            yTf = yT[:, :, :, :].rearrange("p k b l -> p k (b l)")
            yTpf = yTp[:, :, :, :, :].rearrange("p a k b l -> p a k (b l)")
            yTsf = yTs[:, :, :, :, :].rearrange("p a k b l -> p a k (b l)")
            wv4 = wv[:, :, :, :].rearrange("p a k (r e d) -> p a k r e d", r=HP, e=2)

            def step(i, p):
                ta, tb, tc, to, td, te, tf, tg = (i - n for n in range(1, 9))
                a, at_, b, c, o, d, e, f = (live(i, n) for n in range(8))

                def gram(g4):
                    if g4:
                        wait_part(pe, "e_done", tc, g4, QG)
                    for q in range(QG):
                        rows = slice(g4 * DP, (g4 + 1) * DP)
                        last = mm(pc[:, q * P:(q + 1) * P], kT[rows, q, :], kTm[rows, q, :],
                                  start=True, stop=True, skip_group_check=True)
                    last.then_inc(S("gram"), 1)

                def e_T(g4):
                    if g4:
                        wait_part(pe, "et_done", tc, g4, QG)
                    else:
                        wait_part(pe, "e_done", tc, QG, QG)
                    wait_part(pe, "exp_done", tc, g4 + 1, QG)
                    for q in range(QG):
                        last = nc.tensor.transpose(pc[:, q * P:(q + 1) * P], E[:, g4, q, :], ident[:, :])
                    last.then_inc(S("eT"), 1)

                def q_half(h):
                    wait_part(pe, "vbd_done", i, h + 1, 2)
                    project(pa[:, 2 - 2 * h, :], lambda a_, k: xnTs[:, a_, k, :],
                            lambda a_, k: wq[:, a_, k, h * 512:(h + 1) * 512]).then_inc(S("q_mm"), 1)

                def out_half(r0):
                    for r in range(r0, r0 + 4):
                        mm(ps[:, 2, 0:C], oT[:, r, :], wout[:, r, :], start=(r == 0), stop=False)

                if a:
                    wait_dma(pe, "x_in", i, p)
                    if not (isinstance(i, int) and i == 0):
                        wait_part(pe, "qT_done", i - 1, 1, 2)
                    to_T(two(pa[:, 0, :], 0), xin[:, p, :]).then_inc(S("xT"), 1)
                if o:
                    wait_part(pe, "et_done", to, QG, QG)
                    for q in range(QG):
                        for g4 in range(QG):
                            last = mm(pc[g4 * DP:(g4 + 1) * DP, q * P:(q + 1) * P],
                                      v2[:, p, q * QG + g4, :], ET[:, g4, q, :], start=True, stop=True,
                                      skip_group_check=True)
                    last.then_inc(S("av_mm"), 1)
                if a:
                    wait(pe, "xm_done", i)
                    wait_before(pe, "qT_done", i, 1, 2)
                    linear_T(two(pa[:, 1, :], 0), wc, xm).then_inc(S("yT_mm"), 1)
                if b:
                    if e:
                        wait(pe, "hidden", te)
                        wait(pe, "scores_done", te)
                    wait(pe, "x1_done", tb)
                    to_T(two(pb, 0), x1[:, p, :]).then_inc(S("x1T"), 1)
                if o:
                    wait(pe, "av_done", to)
                    for q in range(QG):
                        last = nc.tensor.transpose(pc[:, q * P:(q + 1) * P], av[:, q, :], ident[:, :])
                    last.then_inc(S("av_nat"), 1)
                if at_:
                    wait(pe, "kbd_done", ta, 2)
                    wait(pe, "qT_done", ta, 2)
                    wait_before(pe, "x1_done", ta)
                    for s in range(BT):
                        for r in range(HP):
                            last = mm(ps[s * L:(s + 1) * L, r // 3, (r % 3) * PJ:(r % 3 + 1) * PJ],
                                      qT[:, r, s * L:(s + 1) * L], kbd[:, s, r, :],
                                      start=True, stop=True, skip_group_check=True)
                    last.then_inc(S("sim_mm"), 1)
                if a:
                    wait(pe, "yT_done", i)
                    from_T(two(pa[:, 1, :], 0), yTf).then_inc(S("y_nat"), 1)
                if c:
                    wait_dma(pe, "v2_in", tc, 1 - p)
                    wait_before(pe, "o2_done", tc)
                    for q in range(QG):
                        last = nc.tensor.transpose(
                            pc[:, q * P:(q + 1) * P],
                            v2[:, 1 - p, q * QG:(q + 1) * QG, :].rearrange("p g d -> p (g d)"), ident[:, :])
                    last.then_inc(S("mix_kT"), 1)
                if a:
                    wait(pe, "yT_low", i)
                    project(pa[:, 2, :], lambda a_, k: yTpf[:, a_, k, :], lambda a_, k: wk[:, a_, k, 0:512])\
                        .then_inc(S("k_mm"), 1)
                    project(pa[:, 0, :], lambda a_, k: yTpf[:, a_, k, :], lambda a_, k: wk[:, a_, k, 512:])\
                        .then_inc(S("k_mm"), 1)
                if c:
                    wait(pe, "kT_done", tc)
                    gram(0)
                if b:
                    wait(pe, "xm2_done", tb)
                    linear_T(two(pb, C), wk2, xm2).then_inc(S("kxT_mm"), 1)
                if a:
                    wait_part(pe, "k_raw", i, 1, 2)
                    project(pa[:, 2, :], lambda a_, k: yTpf[:, a_, k, :], lambda a_, k: wv4[:, a_, k, :, 0, :])\
                        .then_inc(S("v_mm"), 1)
                    wait_part(pe, "k_raw", i, 2, 2)
                    wait(pe, "yTs_low", i)
                    project(pa[:, 0, :], lambda a_, k: yTsf[:, a_, k, :], lambda a_, k: wv4[:, a_, k, :, 1, :])\
                        .then_inc(S("v_mm"), 1)
                if at_:
                    wait(pe, "probs", ta)
                    for r in range(HP):
                        last = nc.tensor.transpose(ps[:, r // 4, (r % 4) * P:(r % 4 + 1) * P],
                                                   pr[:, r, 0:P], ident[:, :])
                    last.then_inc(S("pT_mm"), 1)
                if c:
                    gram(1)
                if a:
                    wait(pe, "xn_done", i)
                    to_T(two(pa[:, 1, :], 0), xn).then_inc(S("xnT_mm"), 1)
                if b:
                    wait(pe, "kxT_done", tb)
                    from_T(two(pb, 0), kxT).then_inc(S("kxn_mm"), 1)
                if at_:
                    wait(pe, "pT_done", ta)
                    for s in range(BT):
                        for r in range(HP):
                            last = mm(ps[s * L:(s + 1) * L, r // 3, (r % 3) * 2 * V1:(r % 3 + 1) * 2 * V1],
                                      pT[:, r, s * L:(s + 1) * L],
                                      vbd[:, 1 - p, s, r, :, :].rearrange("p e v -> p (e v)"),
                                      start=True, stop=True, skip_group_check=True)
                    last.then_inc(S("pv_mm"), 1)
                if c:
                    gram(2)
                if a:
                    wait(pe, "xnT_parts", i)
                    q_half(0)
                if f:
                    wait(pe, "oh_done", tf)
                    if b:
                        wait(pe, "kxn_done", tb)
                    elif e:
                        wait(pe, "hidden", te)
                        wait(pe, "scores_done", te)
                    if p == 1:
                        wait(pe, "gelu_done", te)
                        for u in range(2):
                            mm(pb[:, C + 2 * u:C + 2 * u + 2], hT[:, u, :], w2b[:, :], start=True, stop=True)
                    nc.tensor.transpose(pb[:, 0:P], oh[:, :], ident[:, :]).then_inc(S("ohT_mm"), 1)
                if a:
                    q_half(1)
                if f:
                    wait(pe, "ohT_done", tf)
                    mm(pb[:, 0:GATH], ohT[:, :], gath[:, :], start=True, stop=True)\
                        .then_inc(S("gathered"), 1)
                if a:
                    wait(pe, "kn_done", i)
                    four(pa[:, 1, :], kn, 0).then_inc(S("kT_mm"), 1)
                if at_:
                    wait(pe, "on_done", ta)
                    four(ps[:, 0, :], on, 0)
                    four(ps[:, 1, :], on, 4)
                    wait(pe, "pn_done", ta)
                    nc.tensor.transpose(ps[0:H * NN, 2, C:C + P], pn[:, :, :].rearrange("p h n -> p (h n)"),
                                        ident[:, :]).then_inc(S("oT_mm"), 1)
                if d:
                    wait_dma(pe, "on2_in", td, 1 - p)
                    if f:
                        wait(pe, "gs_done", tf)
                    elif b:
                        wait(pe, "kxn_done", tb)
                    to_T(two(pb, 0), on2[:, 1 - p, :]).then_inc(S("omT"), 1)
                if c:
                    gram(3)
                if d:
                    wait(pe, "om_done", td)
                    linear_T(two(pb, C), wo2, om).then_inc(S("zT_mm"), 1)
                if a:
                    wait_part(pe, "q_raw", i, 1, 2)
                    four(pa[:, 2, :], kn, 4).then_inc(S("kT_mm"), 1)
                if at_:
                    wait(pe, "oT_done", ta)
                    out_half(0)
                if c:
                    e_T(0)
                if at_:
                    out_half(4)
                    mm(ps[:, 2, 0:C], pnT[:, :], nullw[:, :], start=False, stop=True)\
                        .then_inc(S("out_mm"), 1)
                if c:
                    e_T(1)
                if a:
                    wait(pe, "qn_done", i)
                    four(pa[:, 0, :], qn, 0).then_inc(S("qT_mm"), 1)
                if d:
                    wait(pe, "zT_done", td)
                    from_T(two(pb, 0), zT).then_inc(S("zn_mm"), 1)
                if c:
                    e_T(2)
                if d:
                    for k in range(CK):
                        mm(pb[:, C:C + NS], zT[:, k, :], wsc[:, k, 0:NS],
                           start=(k == 0), stop=(k == CK - 1), skip_group_check=True)
                    for k in range(CK):
                        last = mm(pb[0:CH, C + P:C + 2 * P], wsc[:, k, NS:NS + CH], zT[:, k, :],
                                  start=(k == 0), stop=(k == CK - 1), skip_group_check=True)
                    last.then_inc(S("score_mm"), 1)
                if c:
                    e_T(3)
                if a:
                    wait_part(pe, "kbd_done", i, 1, 2)
                    four(pa[:, 1, :], qn, 4).then_inc(S("qT_mm"), 1)

            pipeline(pe, step)

        @block.scalar
        def _(act):
            fn = nc.scalar.activation
            loaded(act, "cond_in")
            act.wait_ge(S("style_mm"), 1)
            for m, col in enumerate((AB0, AB1, AB2)):
                for k in range(CK):
                    last = fn(sty[:, m, k, :], pa[:, m, k * NB:(k + 1) * NB], ACT.Identity,
                              bias=cols[:, col, k:k + 1], scale=(float(P) ** -0.5 if m == 0 else 1.0))
            last.then_inc(S("styles"), 1)
            act.wait_ge(S("styles"), 1)
            fn(s2, sty[:, :, :, :], ACT.Square).then_inc(S("squares"), 1)
            for m, w in enumerate((wc, wk2, wo2)):
                fn(w2[m], w[:, :, :], ACT.Square).then_inc(S("squares"), 1)
            act.wait_ge(S("demod_in"), 1)
            fn(drt, dsq, ACT.Sqrt).then_inc(S("demod_sqrt"), 1)
            for w, n in ((wk, "wk"), (wv, "wv"), (wq, "wq")):
                loaded(act, n + "_in")
                fn(part(w[:, 0, :, :]), raw_w[n], ACT.Copy).then_inc(S("high_parts"), 1)
            loaded(act, "late_in")
            act.wait_ge(S("nullw_mm"), 1)
            fn(nullw[:, :], pb[0:H * NN, C:2 * C], ACT.Copy).then_inc(S("setup_act"), 1)

            def step(i, p):
                ta, tb, tc, to, td, te, tf = (i - n for n in range(1, 8))
                a, at_, b, c, o, d, e, f = (live(i, n) for n in range(8))

                def raw(name, h):
                    wait_part(act, name + "_mm", i, h + 1, 2)
                    cols_ = slice(h * 512, (h + 1) * 512)
                    fn(sq[:, cols_], pa[:, 2 - 2 * h, :], ACT.Square)
                    fn((kn if name == "k" else qn)[:, cols_], pa[:, 2 - 2 * h, :], ACT.Copy)\
                        .then_inc(S(name + "_raw"), 1)

                def exps(g4):
                    wait_part(act, "e_done", tc, g4 + 1, QG)
                    fn(E[:, g4, :, :], E[:, g4, :, :], ACT.Exp, scale=DM ** -0.5).then_inc(S("exp_done"), 1)

                def keys(h):
                    wait_part(act, "kT_mm", i, h + 1, 2)
                    bank = pa[:, 1 + h, :].rearrange("p (r s l) -> p r s l", s=BT, l=L)
                    for e in range(2):
                        rows = slice(e * DH, (e + 1) * DH)
                        for s in range(BT):
                            slot = e ^ s
                            last = fn(kbd[rows, s, 4 * h:4 * h + 4, slot * L:(slot + 1) * L],
                                      bank[rows, :, s, :], ACT.Identity, bias=0.0, scale=qks[rows, 1:2])
                    last.then_inc(S("kbd_done"), 1)

                def queries(h):
                    wait_part(act, "qT_mm", i, h + 1, 2)
                    fn(qT[:, 4 * h:4 * h + 4, :].rearrange("p r t -> p (r t)"), pa[:, h, :], ACT.Identity,
                       bias=0.0, scale=qks[:, 0:1]).then_inc(S("qT_done"), 1)

                def et(g4):
                    wait_part(act, "eT", tc, g4 + 1, QG)
                    fn(ET[:, g4, :, :].rearrange("p b c -> p (b c)"), pc[:, :], ACT.Copy)\
                        .then_inc(S("et_done"), 1)

                if o:
                    wait(act, "av_mm", to)
                    fn(av[:, :, :].rearrange("p a b -> p (a b)"), pc[:, :], ACT.Copy).then_inc(S("av_done"), 1)
                if c:
                    wait(act, "mix_kT", tc)
                    fn(kTm[:, :, :].rearrange("p a b -> p (a b)"), pc[:, :], ACT.Identity,
                       bias=off[:, 1:2], scale=off[:, 0:1])
                    fn(kT[:, :, :].rearrange("p a b -> p (a b)"), pc[:, :], ACT.Copy)\
                        .then_inc(S("kT_done"), 1)
                if a:
                    wait_before(act, "x1T", i, 2)
                    wait_dma_before(act, "x1_out", i, p)
                    wait(act, "xT", i)
                    fn(x1[:, p, :], xin[:, p, :], ACT.Copy).then_inc(S("x_copied"), 1)
                if a:
                    wait_before(act, "q_norm", i)
                    raw("k", 0)
                    raw("k", 1)
                if at_:
                    wait(act, "pr_sub", ta)
                    fn(pr[:, :, :], pr[:, :, :], ACT.Exp).then_inc(S("probs"), 1)
                if a:
                    for h in range(2):
                        wait_part(act, "v_mm", i, h + 1, 2)
                        for s in range(BT):
                            rows = slice((s ^ h) * L, (s ^ h) * L + L)
                            last = fn(vbd[rows, p, s, :, h, 0:DH],
                                      pa[rows, 2 - 2 * h, :].rearrange("p (r d) -> p r d", d=DH), ACT.Copy)
                        last.then_inc(S("vbd_done"), 1)
                if at_:
                    wait(act, "pT_mm", ta)
                    fn(pT[:, :, :].rearrange("p (b r) t -> p b (r t)", b=2), ps[:, 0:2, :], ACT.Copy)\
                        .then_inc(S("pT_done"), 1)
                if c:
                    exps(0)
                if a:
                    wait(act, "xnT_mm", i)
                    for k in range(CK):
                        last = fn(xnT[:, k, :], pa[:, 1, k * P:(k + 1) * P], ACT.Identity,
                                  bias=cols[:, NBI, k:k + 1], scale=cols[:, NG, k:k + 1])
                    last.then_inc(S("xnT_done"), 1)
                    wait(act, "xnT_done", i)
                    fn(part(xnTs[:, 0, :, :]), xnT[:, :, :], ACT.Copy).then_inc(S("xnT_high"), 1)
                if b:
                    wait(act, "kxn_mm", tb)
                    wait_before(act, "kx_out", tb, 1, 16)
                    fn(kxn[:, :], pb[:, 0:C], ACT.Copy).then_inc(S("kxn_done"), 1)
                if c:
                    exps(1)
                if a:
                    wait(act, "k_norm", i)
                    raw("q", 0)
                if f:
                    wait(act, "ohT_mm", tf)
                    if p == 1:
                        wait_before(act, "y_sum", tf)
                        fn(comp[:, :, :], pb[:, C:C + 4].rearrange("p (u o) -> p u o", u=2), ACT.Tanh)
                    fn(ohT[:, :], pb[0:NT, 0:P], ACT.Copy).then_inc(S("ohT_done"), 1)
                if a:
                    raw("q", 1)
                if f:
                    wait(act, "gathered", tf)
                    wait_before(act, "y_sum", tf)
                    fn(gs[:, :], pb[:, 0:GATH], ACT.Copy).then_inc(S("gs_done"), 1)
                if c:
                    exps(2)
                if e:
                    wait(act, "local_score", te)
                    fn(esc[:, 1, :], lsc[:, :], ACT.Exp, scale=ninv[:, 1:2]).then_inc(S("local_exp"), 1)
                if at_:
                    wait(act, "oT_mm", ta)
                    fn(oT[:, :, :].rearrange("p (b r) t -> p b (r t)", b=2), ps[:, 0:2, :], ACT.Copy)
                    fn(pnT[:, :], ps[0:H * NN, 2, C:C + P], ACT.Copy).then_inc(S("oT_done"), 1)
                if a:
                    keys(0)
                if c:
                    exps(3)
                if a:
                    keys(1)
                if c:
                    et(0)
                    et(1)
                if a:
                    queries(0)
                if d:
                    wait(act, "zn_mm", td)
                    wait(act, "score_mm", td)
                    wait_before(act, "y_sum", td, 2)
                    fn(zn[:, 1 - p, :], pb[:, 0:C], ACT.Copy).then_inc(S("zn_done"), 1)
                    if e:
                        wait(act, "local_score", te)
                    fn(esc[:, 0, :], pb[:, C:C + NC], ACT.Exp, scale=ninv[:, 1:2])\
                        .then_inc(S("cluster_exp"), 1)
                    fn(hT[0:CH, 1 - p, :], pb[0:CH, C + P:C + 2 * P], ACT.Identity, bias=b1[:, :])\
                        .then_inc(S("hidden"), 1)
                if a:
                    queries(1)
                if d and p == 0:
                    wait(act, "hidden", td)
                    fn(hT[0:CH, :, :], hT[0:CH, :, :], ACT.Gelu).then_inc(S("gelu_done"), 2)

            pipeline(act, step)

        @block.vector
        def _(dve):
            v = nc.vector
            chain = [0]

            def link(ins):
                chain[0] += 1
                ins.then_inc(S("vector_chain"), 1)
                dve.wait_ge(S("vector_chain"), chain[0])

            v.memset(nvbd, 0.0)
            v.memset(oh[:, :], 0.0)
            v.memset(esc[:, :, :], 0.0)
            v.memset(hT[CH:CH + 1, :, :], 1.0)
            v.memset(mhalf[:, :], -0.5)
            v.memset(eps[:, :], LN_EPS)
            v.memset(v2[:, :, :, :], 0.0).then_inc(S("zeros"), 1)
            dve.wait_ge(S("zeros"), 1)
            v.memset(v2[:, :, :, DM:DM + 1], 1.0).then_inc(S("ones"), 1)
            loaded(dve, "small_in")
            for p in range(2):
                v.tensor_copy(v2[:, p, :, DM + 1:DM + 1 + TG], bc(token[:, :], 1, G))
            v.tensor_copy(kk[:, 0, :], CO["knots"][:, 0:KN - 1])
            v.tensor_tensor(kk[:, 1, :], CO["knots"][:, 1:KN], CO["knots"][:, 0:KN - 1], ALU.subtract)
            link(v.tensor_scalar(ninv[:, 0:1], CO["temp"], 1e-6, -1.0, ALU.add, ALU.mult))
            v.reciprocal(ninv[:, 1:2], ninv[:, 0:1])
            v.tensor_scalar(sg1, sig, 0.3, None, ALU.is_gt)
            link(v.tensor_scalar(sg2, sig, -0.3, None, ALU.is_lt))
            link(v.tensor_tensor(sg1, sg1, sg2, ALU.subtract))
            link(v.tensor_tensor(sg2, sg1, sig, ALU.subtract))
            link(v.tensor_tensor(wsc[:, :, NC:NS], sig, sg2, ALU.add))
            members = wsc[:, :, NC:NS].rearrange("p k (c t) -> p k c t", t=TPC)
            link(v.tensor_tensor(acc, members[:, :, :, 0], members[:, :, :, 1], ALU.add))
            for t in range(2, TPC):
                link(v.tensor_tensor(acc, acc, members[:, :, :, t], ALU.add))
            v.tensor_scalar(acp, acc, 0.0, None, ALU.is_gt)
            link(v.tensor_scalar(acn, acc, 0.0, None, ALU.is_lt))
            v.tensor_tensor(wsc[:, :, 0:NC], acp, acn, ALU.subtract)
            link(v.tensor_tensor(nks, nk, nk, ALU.mult))
            v.tensor_reduce(nrm[0:NR, 0, 0:2], nks, AX, ALU.add).then_inc(S("nullk_n2"), 1)
            dve.wait_ge(S("nullk_r"), 1)
            v.tensor_tensor(nkh, nk, bc(rn[0:NR, 0, 0:2], 2, DH), ALU.mult).then_inc(S("nullk_unit"), 1)
            dve.wait_ge(S("null_T"), 1)
            for e in range(2):
                rows = slice(e * DH, (e + 1) * DH)
                for r in range(HP):
                    at = (2 * r + e) * NN
                    v.tensor_copy(nvbd[rows, r, at:at + NN], pb[rows, NR + r * NN:NR + (r + 1) * NN])\
                        .then_inc(S("nvbd_done"), 1)
            v.tensor_scalar(nkT[:, :], pb[:, 0:NR], qks[:, 1:2], None, ALU.mult).then_inc(S("nvbd_done"), 1)
            dve.wait_ge(S("demod_mm"), 1)
            v.tensor_scalar(dsq, pa[:, 0:3, C:2 * C].rearrange("p m (k n) -> p m k n", k=CK),
                            1e-8, None, ALU.add).then_inc(S("demod_in"), 1)
            dve.wait_ge(S("demod_sqrt"), 1)
            link(v.reciprocal(dem[:, :, :, :], drt))
            link(v.tensor_tensor(dnw, dem[:, :, :, :], dem[:, :, :, :], ALU.mult))
            link(v.tensor_tensor(dnw, dnw, dsq, ALU.mult))
            link(v.tensor_scalar(dnw, dnw, -0.5, 1.5, ALU.mult, ALU.add))
            v.tensor_tensor(dem[:, :, :, :], dem[:, :, :, :], dnw, ALU.mult)
            for n, (w, name) in enumerate(((wk, "wk"), (wv, "wv"), (wq, "wq"))):
                dve.wait_ge(S("high_parts"), n + 1)
                ins = v.tensor_tensor(part(w[:, 1, :, :]), raw_w[name], w[:, 0, :, :], ALU.subtract)
                ins.then_inc(S("low_parts"), 1)
            dve.wait_ge(S("low_parts"), 3)
            for s in range(BT):
                ins = v.memset(kbd[:, s, :, :], 0.0)
            link(ins)
            for e in range(2):
                rows = slice(e * DH, (e + 1) * DH)
                for s in range(BT):
                    v.tensor_copy(kbd[rows, s, :, P + (e ^ s) * NN:P + (e ^ s) * NN + NN],
                                  nkT[rows, :].rearrange("p (r n) -> p r n", n=NN))
            dve.wait_ge(S("vbd_zeros"), 1)
            for s in range(BT):
                for e in range(2):
                    rows = slice((s ^ e) * L, (s ^ e) * L + L)
                    for p in range(2):
                        v.memset(vbd[rows, p, s, :, e, DH:V1], 1.0)
            loaded(dve, "late_in")
            v.tensor_scalar(qks[:, 0:1], qks[:, 0:1], 8.0, None, ALU.mult).then_inc(S("setup_dve"), 1)
            dve.wait_ge(S("setup_dve"), 1)

            def modulate(dst, src, table, t):
                return v.tensor_tensor(
                    dst[:, :, :, :], src.rearrange("p k (b l) -> p k b l", b=BT),
                    bc(table[:, :, bass.ds(t * BT, BT)], 3, L), ALU.mult)

            LINKS = 10 + 5 + 1
            by_pair = lambda z: z[:, :].rearrange("p (r e) -> p r e", e=2)

            def step(i, p):
                ta, tb, tc, to, td, te, tf, tg = (i - n for n in range(1, 9))
                a, at_, b, c, o, d, e, f = (live(i, n) for n in range(8))
                links = [0]

                def route(ins):
                    links[0] += 1
                    ins.then_inc(S("routing_chain"), 1)
                    wait_part(dve, "routing_chain", te, links[0], LINKS)

                both = lambda z: z[:, :, :].rearrange("p a c -> p (a c)")

                def segments():
                    if e:
                        wait(dve, "cluster_exp", te)
                    if f:
                        wait(dve, "local_exp", tf)
                    route(v.tensor_scalar(fl[:, :, :], esc[:, :, :], 1.0, None, ALU.add))
                    route(v.reciprocal(fl[:, :, :], fl[:, :, :]))
                    route(v.tensor_scalar(fl[:, :, :], fl[:, :, :], float(KN - 1), None, ALU.mult))
                    route(v.tensor_tensor(ge[:, :, :], bc(both(fl), 2, KN - 2),
                                          bc(CO["steps"][:, 1:KN - 1], 1, 2 * NC), ALU.is_ge))
                    route(v.tensor_reduce(both(seg), ge[:, :, :], AX, ALU.add))
                    v.tensor_tensor(frac[:, :, :], fl[:, :, :], seg[:, :, :], ALU.subtract)
                    route(v.tensor_tensor(eq[:, :, :], bc(both(seg), 2, KN - 1),
                                          bc(CO["steps"][:, 0:KN - 1], 1, 2 * NC), ALU.is_equal))

                def gates():
                    v.tensor_tensor(lr[:, 0, :, :], eq[:, :, :], bc(kk[:, 0, :], 1, 2 * NC), ALU.mult)
                    route(v.tensor_tensor(lr[:, 1, :, :], eq[:, :, :], bc(kk[:, 1, :], 1, 2 * NC), ALU.mult))
                    route(v.tensor_reduce(lo_rise[:, :, :], lr[:, :, :, :], AX, ALU.add))
                    route(v.tensor_tensor(both(frac), both(frac), lo_rise[:, 1, :], ALU.mult))
                    route(v.tensor_tensor(both(gate), lo_rise[:, 0, :], both(frac), ALU.add))

                def choose():
                    route(v.tensor_reduce(best[:, 0, :], gate[:, :, :], AX, ALU.max))
                    route(v.tensor_tensor(pick[:, :, :], gate[:, :, :], bc(best[:, 0, :], 2, NC), ALU.is_equal))
                    route(v.tensor_tensor(pick[:, :, :], pick[:, :, :], bc(CO["behind"], 1, 2), ALU.mult))
                    route(v.tensor_reduce(best[:, 1, :], pick[:, :, :], AX, ALU.min))
                    route(v.tensor_tensor(chosen[:, p, :, :], bc(CO["behind"], 1, 2),
                                          bc(best[:, 1, :], 2, NC), ALU.is_equal))
                    if f:
                        wait_before(dve, "ohT_mm", tf)
                        v.tensor_tensor(oh[:, 0:NT].rearrange("p (c k) -> p c k", k=TPC),
                                        bc(chosen[:, 1 - p, 0, :], 2, TPC),
                                        bc(chosen[:, p, 1, :], 1, NC), ALU.mult).then_inc(S("oh_done"), 1)
                    if e:
                        wait(dve, "scores_done", te)
                        route(v.tensor_tensor(own[:, :, :], sc[:, p, :].rearrange("p (c k) -> p c k", k=TPC),
                                              bc(chosen[:, p, 0, :], 2, TPC), ALU.mult))
                        assert links[0] == LINKS
                        v.tensor_reduce(lsc[:, :], own[:, :, :].rearrange("p c k -> p k c"), AX, ALU.add)\
                            .then_inc(S("local_score"), 1)

                def spline():
                    wait(dve, "gs_done", tf)
                    v.scalar_tensor_tensor(out=hid[:, 0, :], in0=gs[:, 0:GRID], scalar=comp[:, 1 - p, 0:1],
                                           in1=gs[:, 2 * GRID:3 * GRID], op0=ALU.mult, op1=ALU.add)\
                        .then_inc(S("hid_0"), 1)
                    wait(dve, "hid_0", tf)
                    v.scalar_tensor_tensor(out=hid[:, 1, :], in0=gs[:, GRID:2 * GRID],
                                           scalar=comp[:, 1 - p, 1:2], in1=hid[:, 0, :],
                                           op0=ALU.mult, op1=ALU.add).then_inc(S("hid_1"), 1)
                    wait(dve, "hid_1", tf)
                    v.scalar_tensor_tensor(out=junk[:, :], in0=hid[:, 1, :], scalar=0.0,
                                           in1=gs[:, 3 * GRID:4 * GRID], op0=ALU.max, op1=ALU.mult,
                                           accum_out=mag[:, 0:1]).then_inc(S("mag_sum"), 1)
                    wait(dve, "mag_sum", tf)
                    v.tensor_scalar(mag[:, 1:2], mag[:, 0:1], gs[:, 4 * GRID:4 * GRID + 1], CO["scale"],
                                    ALU.add, ALU.mult).then_inc(S("mag_done"), 1)
                    wait(dve, "mag_done", tf)
                    v.scalar_tensor_tensor(out=yy[:, :], in0=gs[:, 4 * GRID + 1:GATH], scalar=mag[:, 1:2],
                                           in1=zn[:, 1 - p, :], op0=ALU.mult, op1=ALU.add)\
                        .then_inc(S("y_sum"), 1)

                def moments():
                    wait(dve, "y_sum", tf)
                    v.bn_stats(ys6[:, :], yy[:, :]).then_inc(S("y_stats"), 1)
                    wait(dve, "y_stats", tf)
                    v.memset(pad[:, :], 0.0)
                    v.bn_aggr(ymv[:, :], ys6[:, :]).then_inc(S("y_moments"), 1)

                def normalise():
                    wait(dve, "y_rsqrt", tg)
                    wait_before(dve, "res_done", tg)
                    v.tensor_scalar(yn[:, :], yy[:, :], ymv[:, 0:1], yve[:, 1:2],
                                    ALU.subtract, ALU.mult).then_inc(S("yn_done"), 1)

                def soften(g4):
                    wait_part(dve, "gram", tc, g4 + 1, QG)
                    src = pc[:, :].rearrange("p (q n) -> p q n", n=P)
                    v.tensor_reduce(mx2[:, g4, :], src, AX, ALU.max).then_inc(S("mix_max"), 1)
                    wait_part(dve, "mix_max", tc, g4 + 1, QG)
                    v.tensor_tensor(E[:, g4, :, :], src, bc(mx2[:, g4, :], 2, P), ALU.subtract)\
                        .then_inc(S("e_done"), 1)

                def et(g4):
                    wait_part(dve, "eT", tc, g4 + 1, QG)
                    v.tensor_copy(ET[:, g4, :, :].rearrange("p b c -> p (b c)"), pc[:, :])\
                        .then_inc(S("et_done"), 1)

                def norms(name, n):
                    wait_part(dve, name + "_raw", i, 2, 2)
                    v.tensor_reduce(nrm[:, n, :], sq[:, :].rearrange("p (h d) -> p h d", d=DH), AX, ALU.add)\
                        .then_inc(S(name + "_norm"), 1)
                    wait(dve, name + "_norm", i)
                    v.tensor_scalar(nrg[:, n, :], nrm[:, n, :], 1e-24, None, ALU.max)\
                        .then_inc(S(name + "_guard"), 1)

                def unit(name, n, buf):
                    wait(dve, name + "_rsqrt", i)
                    z = buf[:, :].rearrange("p (h d) -> p h d", d=DH)
                    v.tensor_tensor(z, z, bc(rn[:, n, :], 2, DH), ALU.mult).then_inc(S(name + "n_done"), 1)

                if a:
                    wait(dve, "xT", i)
                    modulate(xm, two(pa[:, 0, :], 0), sty[:, 0, :, :], i).then_inc(S("xm_done"), 1)
                if e or f:
                    segments()
                if a:
                    wait(dve, "yT_mm", i)
                    modulate(yT, two(pa[:, 1, :], 0), dem[:, 0, :, :], i).then_inc(S("y_dem"), 1)
                    wait(dve, "y_dem", i)
                    for k in range(CK):
                        last = v.tensor_scalar(yT[:, k, :, :], yT[:, k, :, :], cols[:, CB, k:k + 1], CLAMP,
                                               ALU.add, ALU.min)
                    last.then_inc(S("y_min"), 1)
                    wait(dve, "y_min", i)
                    v.tensor_scalar(part(yTp[:, 0, :, :, :]), yT[:, :, :, :], -CLAMP, None, ALU.max)
                    v.tensor_scalar(part(yTs[:, 0, :, ::-1, :]), yT[:, :, :, :], -CLAMP, None, ALU.max)\
                        .then_inc(S("yTs_done"), 1)
                    wait(dve, "yTs_done", i)
                    v.tensor_scalar(yT[:, :, :, :], yT[:, :, :, :], -CLAMP, None, ALU.max)\
                        .then_inc(S("yT_done"), 1)
                    wait(dve, "yT_done", i)
                    v.tensor_tensor(part(yTp[:, 1, :, :, :]), yT[:, :, :, :], yTp[:, 0, :, :, :],
                                    ALU.subtract).then_inc(S("yT_low"), 1)
                if o:
                    wait(dve, "av_nat", to)
                    wait_before(dve, "o2_out", to, 1, 16)
                    src = pc[:, :].rearrange("p (g d) -> p g d", d=DP)
                    v.reciprocal(rd2[:, :], src[:, :, DM:DM + 1].rearrange("p g o -> p (g o)"))\
                        .then_inc(S("mix_rden"), 1)
                    wait(dve, "mix_rden", to)
                    v.tensor_tensor(o2[:, :, :], src[:, :, 0:DM], bc(rd2[:, :], 2, DM), ALU.mult)\
                        .then_inc(S("o2_done"), 1)
                if live(i, 8):
                    normalise()
                if b:
                    wait(dve, "x1T", tb)
                    modulate(xm2, two(pb, 0), sty[:, 1, :, :], tb).then_inc(S("xm2_done"), 1)
                if at_:
                    wait(dve, "sim_mm", ta)
                    v.tensor_tensor(pr[:, 0:6, :].rearrange("p (b r) j -> p b (r j)", b=2),
                                    ps[:, 0:2, 0:3 * PJ],
                                    alibi[:, 0:6, :].rearrange("p (b r) j -> p b (r j)", b=2), ALU.add)
                    v.tensor_tensor(pr[:, 6:8, :].rearrange("p r j -> p (r j)"), ps[:, 2, 0:2 * PJ],
                                    alibi[:, 6:8, :].rearrange("p r j -> p (r j)"), ALU.add)\
                        .then_inc(S("pr_add"), 1)
                if at_:
                    keys = pr[:, :, 0:P].rearrange("p r (e j) -> p r e j", e=2)
                    nulls = pr[:, :, P:PJ].rearrange("p r (e n) -> p r e n", e=2)
                    wait(dve, "pr_add", ta)
                    v.tensor_reduce(by_pair(mxm), keys, AX, ALU.max)
                    v.tensor_reduce(by_pair(mxn), nulls, AX, ALU.max).then_inc(S("pr_maxes"), 1)
                    wait(dve, "pr_maxes", ta)
                    v.tensor_tensor(mx[:, :], mxm[:, :], mxn[:, :], ALU.max).then_inc(S("pr_max"), 1)
                    wait(dve, "pr_max", ta)
                    v.tensor_tensor(keys, keys, bc(by_pair(mx), 3, L), ALU.subtract)
                    v.tensor_tensor(nulls, nulls, bc(by_pair(mx), 3, NN), ALU.subtract)\
                        .then_inc(S("pr_sub"), 1)
                if a:
                    wait(dve, "y_nat", i)
                    v.bn_stats(st6[:, :], pa[:, 1, 0:C]).then_inc(S("y_st6"), 1)
                    wait(dve, "y_st6", i)
                    v.memset(pad[:, :], 0.0)
                    v.bn_aggr(mv[:, :], st6[:, :]).then_inc(S("y_mv"), 1)
                if e or f:
                    gates()
                if c:
                    soften(0)
                if b:
                    wait(dve, "kxT_mm", tb)
                    modulate(kxd_, two(pb, C), dem[:, 1, :, :], tb).then_inc(S("kx_dem"), 1)
                if a:
                    wait(dve, "y_rstd", i)
                    v.tensor_scalar(xn[:, :], pa[:, 1, 0:C], mv[:, 0:1], rs[:, 0:1],
                                    ALU.subtract, ALU.mult).then_inc(S("xn_done"), 1)
                if b:
                    wait(dve, "kx_dem", tb)
                    v.tensor_tensor(kxT[:, :, :], kxd_[:, :, :, :].rearrange("p k b l -> p k (b l)"),
                                    bc(cols[:, KB, :], 2, P), ALU.add).then_inc(S("kxT_done"), 1)
                if a:
                    norms("k", 1)
                if c:
                    soften(1)
                if at_:
                    wait(dve, "probs", ta)
                    for s in range(BT):
                        rows = slice(s * L, (s + 1) * L)
                        src = pr[rows, :, P:PJ].rearrange("p r (e n) -> p r e n", e=2)
                        last = v.tensor_copy(pnr[rows, :, :].rearrange("p (r e) n -> p r e n", e=2),
                                             src[:, :, ::-1, :] if s else src)
                    last.then_inc(S("null_order"), 1)
                    wait(dve, "null_order", ta)
                    v.tensor_reduce(den[:, :], pnr[:, :, :], AX, ALU.add).then_inc(S("null_sum"), 1)
                if a:
                    wait(dve, "xnT_high", i)
                    v.tensor_tensor(part(xnTs[:, 1, :, :]), xnT[:, :, :], xnTs[:, 0, :, :], ALU.subtract)\
                        .then_inc(S("xnT_parts"), 1)
                if e or f:
                    choose()
                if at_:
                    wait(dve, "pv_mm", ta)
                    wait(dve, "null_sum", ta)
                    head = ps[:, 0:2, 0:6 * V1].rearrange("p b (h v) -> p b h v", v=V1)
                    tail = ps[:, 2, 0:4 * V1].rearrange("p (h v) -> p h v", v=V1)
                    v.tensor_tensor(den2[:, 0:12].rearrange("p (b h) -> p b h", b=2), head[:, :, :, DH],
                                    den[:, 0:12].rearrange("p (b h) -> p b h", b=2), ALU.add)
                    v.tensor_tensor(den2[:, 12:16], tail[:, :, DH], den[:, 12:16], ALU.add)\
                        .then_inc(S("den_done"), 1)
                    wait(dve, "den_done", ta)
                    v.reciprocal(rden[:, :], den2[:, :]).then_inc(S("rden_done"), 1)
                    wait(dve, "rden_done", ta)
                    v.tensor_tensor(on[:, 0:12 * DH].rearrange("p (b h d) -> p b h d", b=2, d=DH),
                                    head[:, :, :, 0:DH],
                                    bc(rden[:, 0:12].rearrange("p (b h) -> p b h", b=2), 3, DH), ALU.mult)
                    v.tensor_tensor(on[:, 12 * DH:].rearrange("p (h d) -> p h d", d=DH), tail[:, :, 0:DH],
                                    bc(rden[:, 12:16], 2, DH), ALU.mult).then_inc(S("on_done"), 1)
                    v.tensor_tensor(pn[:, :, :], pnr[:, :, :], bc(rden[:, :], 2, NN), ALU.mult)\
                        .then_inc(S("pn_done"), 1)
                if c:
                    soften(2)
                if d:
                    wait(dve, "omT", td)
                    modulate(om, two(pb, 0), sty[:, 2, :, :], td).then_inc(S("om_done"), 1)
                if a:
                    norms("q", 0)
                if c:
                    soften(3)
                if d:
                    wait(dve, "zT_mm", td)
                    modulate(zd, two(pb, C), dem[:, 2, :, :], td).then_inc(S("z_dem"), 1)
                    wait(dve, "z_dem", td)
                    v.tensor_tensor(zT[:, :, :], zd[:, :, :, :].rearrange("p k b l -> p k (b l)"),
                                    bc(cols[:, OB, :], 2, P), ALU.add).then_inc(S("zT_done"), 1)
                if f:
                    spline()
                if a:
                    unit("q", 0, qn)
                if f:
                    moments()
                if at_:
                    wait(dve, "out_mm", ta)
                    wait(dve, "x_copied", ta)
                    v.tensor_tensor(x1[:, 1 - p, :], ps[:, 2, 0:C], x1[:, 1 - p, :], ALU.add)\
                        .then_inc(S("x1_done"), 1)
                if c:
                    et(2)
                    et(3)
                if d:
                    wait(dve, "hidden", td)
                    v.tensor_copy(sc[:, 1 - p, :], pb[:, C + NC:C + NS]).then_inc(S("scores_done"), 1)

            pipeline(dve, step)

        @block.gpsimd
        def _(pool):
            g = nc.gpsimd
            pool.wait_ge(S("zeros"), 1)
            pool.wait_ge(S("ones"), 1)
            pool.wait_ge(S("nullk_n2"), 1)
            g.tensor_scalar(nrg[0:NR, 0, 0:2], nrm[0:NR, 0, 0:2], 1e-24, None, ALU.max).then_inc(S("nullk_g"), 1)
            pool.wait_ge(S("nullk_g"), 1)
            g.tensor_tensor(rn[0:NR, 0, 0:2], nrg[0:NR, 0, 0:2], mhalf[0:NR, 0:2], ALU.pow)\
                .then_inc(S("nullk_r"), 1)
            pool.wait_ge(S("nullk_unit"), 1)
            pool.wait_ge(S("low_parts"), 2)
            for p in range(2):
                last = g.memset(vbd[:, p, :, :, :, :], 0.0)
            last.then_inc(S("vbd_zeros"), 1)
            loaded(pool, "late_in")
            g.memset(ve[:, :], 0.0).then_inc(S("setup_pool"), 1)
            pool.wait_ge(S("setup_pool"), 1)

            def step(i, p):
                tf, tg = i - 7, i - 8

                def powers(name, n):
                    wait(pool, name + "_guard", i)
                    g.tensor_tensor(rn[:, n, :], nrg[:, n, :], mhalf[:, :], ALU.pow)\
                        .then_inc(S(name + "_rsqrt"), 1)

                if live(i, 8):
                    wait(pool, "yn_done", tg)
                    g.tensor_tensor(yn[:, :], yn[:, :], gb[:, 0, :], ALU.mult).then_inc(S("yn_gamma"), 1)
                    wait(pool, "yn_gamma", tg)
                    wait(pool, "x1_beta", tg)
                    wait_dma_before(pool, "out", tg, p)
                    g.tensor_tensor(res[:, p, :], yn[:, :], xb[:, p, :], ALU.add)\
                        .then_inc(S("res_done"), 1)
                if live(i, 0):
                    wait(pool, "yT_done", i)
                    wait_before(pool, "v_mm", i, 1, 2)
                    g.tensor_tensor(part(yTs[:, 1, :, :, :]), yT[:, :, ::-1, :], yTs[:, 0, :, :, :],
                                    ALU.subtract).then_inc(S("yTs_low"), 1)
                    wait(pool, "y_mv", i)
                    g.tensor_tensor(ve[:, :], mv[:, 1:2], eps[:, :], ALU.add).then_inc(S("y_var"), 1)
                    wait(pool, "y_var", i)
                    g.tensor_tensor(rs[:, :], ve[:, :], mhalf[:, 0:1], ALU.pow).then_inc(S("y_rstd"), 1)
                    powers("k", 1)
                    wait(pool, "k_rsqrt", i)
                    z = kn[:, :].rearrange("p (h d) -> p h d", d=DH)
                    g.tensor_tensor(z, z, bc(rn[:, 1, :], 2, DH), ALU.mult).then_inc(S("kn_done"), 1)
                if live(i, 7):
                    wait_dma(pool, "x1_back", tf, 1 - p)
                    g.tensor_tensor(xb[:, 1 - p, :], xb[:, 1 - p, :], gb[:, 1, :], ALU.add)\
                        .then_inc(S("x1_beta"), 1)
                if live(i, 0):
                    powers("q", 0)
                if live(i, 7):
                    wait(pool, "y_moments", tf)
                    g.tensor_tensor(yve[:, 0:1], ymv[:, 1:2], eps[:, :], ALU.add).then_inc(S("yve_0"), 1)
                    wait(pool, "yve_0", tf)
                    g.tensor_tensor(yve[:, 1:2], yve[:, 0:1], mhalf[:, 0:1], ALU.pow)\
                        .then_inc(S("y_rsqrt"), 1)

            pipeline(pool, step)


_OUT = ((128, 64, 256), "float32")


def kernel(**inputs):
    import numpy as np
    import concourse.bacc as bacc
    from concourse import mybir as mb
    from concourse.bass_utils import run_bass_kernel_spmd as run

    a = {k: np.asarray(v) for k, v in inputs.items()}
    ar = {"x": a["x"], "condT": a["cond_512"].T}
    for n in ("L0_cond_affine_w", "L0_cond2_k_aff_w", "L0_cond2_o_aff_w", "L0_cond_weight", "L0_cond2_k_w",
              "L0_cond2_o_w"):
        ar[n + "T"] = a[n].T
    ar["cols"] = np.stack([a[n].reshape(2, 128).T for n in (
        "L0_cond_bias", "L0_attn_norm_g", "L0_attn_norm_b", "L0_cond2_k_b", "L0_cond2_o_b",
        "L0_cond_affine_b", "L0_cond2_k_aff_b", "L0_cond2_o_aff_b")], axis=1)
    ar["qk_scale"] = np.stack([np.tile(a["L0_attn_q_scale"], 2), np.tile(a["L0_attn_k_scale"], 2)], axis=1)
    ar["sigT"] = a["L0_ffn_signatures_raw"].T
    null = a["L0_attn_null_kv"].reshape(8, 2, 2, 2, 64).transpose(3, 0, 2, 1, 4)
    ar["null_k"], ar["null_v"] = null[0].reshape(16, 2, 64), null[1].reshape(16, 2, 64)
    ar["L0_attn_Wq"] = a["L0_attn_Wq"]
    ar["Wk"], ar["Wv"] = a["L0_attn_Wkv"][:, :1024], a["L0_attn_Wkv"][:, 1024:]
    ar["L0_attn_Wout"] = a["L0_attn_Wout"]
    ar["L0_ffn_compress_w1"] = a["L0_ffn_compress_w1"]
    ar["ident"] = np.eye(128, dtype=np.float32)
    start = 2.0 ** (-2.0 ** (-(np.log2(16) - 3)))
    slopes = np.array([start * start ** i for i in range(16)], dtype=np.float32)
    row = np.arange(64)
    pos = np.concatenate([np.arange(64) + 2, np.arange(2)])
    dist = -np.abs(pos[None, :] - (row[:, None] + 2)).astype(np.float32)
    table = slopes[None, :, None] * dist[:, None, :]
    seen = pos[None, :] <= row[:, None] + 2
    table = np.where(seen[:, None, :], table, np.float32(-3.0e38)).astype(np.float32)
    table = table.reshape(64, 8, 2, 66)
    ar["alibi"] = np.concatenate([np.concatenate([z[:, :, :, :64].reshape(64, 8, 128), z[:, :, :, 64:].reshape(64, 8, 4)],
                                                 axis=2) for z in (table, table[:, :, ::-1])])
    ar["token"] = np.repeat(np.eye(8, dtype=np.float32), 16, axis=0)
    row = np.arange(128) % 32
    is_token = (row >= 17) & (row < 25)
    ar["off"] = np.stack([np.where(row < 16, 1.0, np.where(is_token, 1e30, 0.0)),
                          np.where(is_token, -1e30, 0.0)], axis=1).astype(np.float32)
    row_of = np.concatenate([a["L0_ffn_knot_values"], np.arange(8, dtype=np.float32) - 8,
                             np.arange(8, dtype=np.float32), a["L0_ffn_temperature"],
                             a["L0_ffn_output_scale"]])
    ar["w2b"] = np.concatenate([a["L0_ffn_compress_w2"], a["L0_ffn_compress_b2"][None, :]])
    ar["b1"] = a["L0_ffn_compress_b1"].reshape(64, 1)
    ar["coef"] = np.repeat(row_of[None, :], 128, axis=0)
    ar["gb"] = np.repeat(np.stack([a["L0_ffn_norm_gamma"], a["L0_ffn_norm_beta"]])[None], 128, axis=0)
    ar["gath"] = np.concatenate([a["L0_ffn_spline_w1"].reshape(64, 32), a["L0_ffn_spline_b1"],
                                 a["L0_ffn_spline_w2"].reshape(64, 16), a["L0_ffn_spline_b2"],
                                 a["L0_ffn_directions"]], axis=1)

    nc = bacc.Bacc("TRN2", target_bir_lowering=False, num_devices=1)
    arrays, aps = {}, {}
    for name, v in ar.items():
        v = np.ascontiguousarray(v)
        arrays[f"in_{name}"] = v
        aps[name] = nc.dram_tensor(f"in_{name}", v.shape, mb.dt.from_np(v.dtype), kind="ExternalInput").ap()
    out = nc.dram_tensor("out_0", _OUT[0], mb.dt.from_np(np.dtype(_OUT[1])), kind="ExternalOutput").ap()
    adaln_attention_ffn(nc, aps, out)
    r = run(nc, [arrays], core_ids=[0])
    return r.results[0]["out_0"]
```
